# Optimizing a Trainium2 kernel written in Bass

```python
import numpy as np
import jax
import jax.numpy as jnp

def _softmax(x, axis=-1):
    return jax.nn.softmax(x, axis=axis)

def _gelu(x):
    return jax.nn.gelu(x, approximate=True)

def _silu(x):
    return jax.nn.silu(x)

def _sigmoid(x):
    return jax.nn.sigmoid(x)

def _layernorm(x, axis=-1, eps=1e-05):
    m = jnp.mean(x, axis=axis, keepdims=True)
    v = jnp.var(x, axis=axis, keepdims=True)
    return (x - m) / jnp.sqrt(v + eps)

def _scatter_add(tgt, idx, src, axis=0):
    return tgt.at[idx].add(src)

def _segment_sum(src, seg, n):
    return jax.ops.segment_sum(src, seg, n)
kernel_name = 'mk_conv_preact_d2_conv_nchw1024_r4_456f6f'

def setup_inputs(seed: int=0):
    np.random.seed(seed)
    _w = jnp.asarray

    def _rec_inputs():
        import jax
        import jax.numpy as jnp
        _gk = jax.random.key(seed)
        x = -7.109e-05 + 0.9999 * jax.random.normal(jax.random.fold_in(_gk, 1), (16, 256, 32, 32), jnp.float32)
        return x
    x = _rec_inputs()

    def _L0_conv_setup():
        import jax, jax.numpy as jnp
        import numpy as np
        key = jax.random.key(seed)
        ks = jax.random.split(key, 7)
        B, C, H, W = (16, 256, 32, 32)
        E, R = (8, 16)
        return {'x': jax.random.normal(ks[0], (B, C, H, W), dtype=jnp.float32), 'W1': jax.random.normal(ks[1], (E, R, C), dtype=jnp.float32) * 0.03, 'b1': jax.random.normal(ks[2], (E, R), dtype=jnp.float32) * 0.01, 'W2': jax.random.normal(ks[3], (E, C, R), dtype=jnp.float32) * 0.03, 'b2': jax.random.normal(ks[4], (E, C), dtype=jnp.float32) * 0.01, 'Wg': jax.random.normal(ks[5], (E, C), dtype=jnp.float32) * 0.03, 'bg': jax.random.normal(ks[6], (E,), dtype=jnp.float32) * 0.01}
    _L0_conv_all = _L0_conv_setup()
    _L0_conv_in = {k: v for k, v in _L0_conv_all.items() if k in ('W1', 'b1', 'W2', 'b2', 'Wg', 'bg')}
    del _L0_conv_all

    def _L1_conv_setup():
        import jax, jax.numpy as jnp
        import numpy as np
        from jax import lax
        C1 = 256
        C2 = 256
        D_STATE = 8
        HEADS = 2
        D_INNER = 256
        D_HEAD = D_INNER // HEADS

        def _mobius_perm(mobius, H, W):
            ys, xs = jnp.meshgrid(jnp.linspace(-1.0, 1.0, H), jnp.linspace(-1.0, 1.0, W), indexing='ij')
            z = (xs + 1j * ys).reshape(-1).astype(jnp.complex64)
            perms = []
            for h in range(mobius.shape[0]):
                a, b, c, d = (mobius[h, 0], mobius[h, 1], mobius[h, 2], mobius[h, 3])
                s = jnp.sqrt(jnp.clip(jnp.abs(a * d - b * c), 0.001))
                a, b, c, d = (a / s, b / s, c / s, d / s)
                w = (a * z + b) / (c * z + d + 1e-06)
                score = jnp.real(w) + 1.3 * jnp.imag(w)
                perms.append(jnp.argsort(score))
            return jnp.stack(perms, 0)

        def _gather_last(v, idx):
            return jnp.take_along_axis(v, jnp.broadcast_to(idx, v.shape[:-1] + (idx.shape[-1],)), axis=-1)

        def _selective_scan(x, dt, A, Bt, Ct, D):
            Bsz, Hh, Dh, N = x.shape
            S = A.shape[-1]
            dA = jnp.exp(dt[:, :, None, :] * A[None, :, :, None])
            dB = dt[:, :, None, :] * Bt

            def step(h, inp):
                dA_t, dB_t, x_t, C_t = inp
                h = dA_t[:, :, None, :] * h + dB_t[:, :, None, :] * x_t[..., None]
                y_t = jnp.einsum('bhds,bhs->bhd', h, C_t)
                return (h, y_t)
            h0 = jnp.zeros((Bsz, Hh, Dh, S), x.dtype)
            inputs = (jnp.moveaxis(dA, -1, 0), jnp.moveaxis(dB, -1, 0), jnp.moveaxis(x, -1, 0), jnp.moveaxis(Ct, -1, 0))
            _, ys = lax.scan(step, h0, inputs)
            return jnp.moveaxis(ys, 0, -1) + D[None, :, None, None] * x
        key = jax.random.key(seed)
        ks = jax.random.split(key, 8)
        S = D_STATE
        x = jax.random.normal(ks[0], (8, C1, 32, 32), jnp.float32)
        in_proj_w = jax.random.normal(ks[1], (3 * D_INNER, C1), jnp.float32) / np.sqrt(C1)
        in_proj_b = jnp.zeros((3 * D_INNER,), jnp.float32)
        dw_w = jax.random.normal(ks[2], (D_INNER, 1, 3), jnp.float32) / np.sqrt(3.0)
        dw_b = jnp.zeros((D_INNER,), jnp.float32)
        dbc_w = jax.random.normal(ks[3], (HEADS * (1 + 2 * S), D_INNER), jnp.float32) / np.sqrt(D_INNER)
        dbc_b = jnp.zeros((HEADS * (1 + 2 * S),), jnp.float32)
        A_log = jnp.log(jnp.tile(jnp.arange(1, S + 1, dtype=jnp.float32), (HEADS, 1)))
        Dparam = jnp.ones((HEADS,), jnp.float32)
        mobius = jnp.tile(jnp.array([[1.0, 0.0, 0.0, 1.0]], jnp.float32), (HEADS, 1)) + 0.05 * jax.random.normal(ks[4], (HEADS, 4), jnp.float32)
        out_proj_w = jax.random.normal(ks[5], (C2, D_INNER), jnp.float32) / np.sqrt(D_INNER)
        out_proj_b = jnp.zeros((C2,), jnp.float32)
        return dict(x=x, in_proj_w=in_proj_w, in_proj_b=in_proj_b, dw_w=dw_w, dw_b=dw_b, dbc_w=dbc_w, dbc_b=dbc_b, A_log=A_log, Dparam=Dparam, mobius=mobius, out_proj_w=out_proj_w, out_proj_b=out_proj_b)
    _L1_conv_all = _L1_conv_setup()
    _L1_conv_in = {k: v for k, v in _L1_conv_all.items() if k in ('in_proj_w', 'in_proj_b', 'dw_w', 'dw_b', 'dbc_w', 'dbc_b', 'A_log', 'Dparam', 'mobius', 'out_proj_w', 'out_proj_b')}
    del _L1_conv_all
    return {'x': x, 'L0_conv_W1': _L0_conv_in['W1'], 'L0_conv_b1': _L0_conv_in['b1'], 'L0_conv_W2': _L0_conv_in['W2'], 'L0_conv_b2': _L0_conv_in['b2'], 'L0_conv_Wg': _L0_conv_in['Wg'], 'L0_conv_bg': _L0_conv_in['bg'], 'L1_conv_in_proj_w': _L1_conv_in['in_proj_w'], 'L1_conv_in_proj_b': _L1_conv_in['in_proj_b'], 'L1_conv_dw_w': _L1_conv_in['dw_w'], 'L1_conv_dw_b': _L1_conv_in['dw_b'], 'L1_conv_dbc_w': _L1_conv_in['dbc_w'], 'L1_conv_dbc_b': _L1_conv_in['dbc_b'], 'L1_conv_A_log': _L1_conv_in['A_log'], 'L1_conv_Dparam': _L1_conv_in['Dparam'], 'L1_conv_mobius': _L1_conv_in['mobius'], 'L1_conv_out_proj_w': _L1_conv_in['out_proj_w'], 'L1_conv_out_proj_b': _L1_conv_in['out_proj_b']}

def reference(x, L0_conv_W1, L0_conv_b1, L0_conv_W2, L0_conv_b2, L0_conv_Wg, L0_conv_bg, L1_conv_in_proj_w, L1_conv_in_proj_b, L1_conv_dw_w, L1_conv_dw_b, L1_conv_dbc_w, L1_conv_dbc_b, L1_conv_A_log, L1_conv_Dparam, L1_conv_mobius, L1_conv_out_proj_w, L1_conv_out_proj_b):
    import jax
    import jax.numpy as jnp

    def _L0_conv_ref(x, W1, b1, W2, b2, Wg, bg):
        import jax, jax.numpy as jnp
        import numpy as np
        y = jnp.mean(x, axis=(2, 3))
        gate = jax.nn.softmax(y @ Wg.T + bg, axis=1)
        h = jax.nn.relu(jnp.einsum('bc,erc->ber', y, W1) + b1)
        s = jnp.einsum('ber,ecr->bec', h, W2) + b2
        scale = jax.nn.sigmoid(jnp.einsum('bec,be->bc', s, gate))
        return x * scale[:, :, None, None]

    def _L1_conv_ref(x, in_proj_w, in_proj_b, dw_w, dw_b, dbc_w, dbc_b, A_log, Dparam, mobius, out_proj_w, out_proj_b):
        import jax, jax.numpy as jnp
        import numpy as np
        from jax import lax
        C1 = 256
        C2 = 256
        D_STATE = 8
        HEADS = 2
        D_INNER = 256
        D_HEAD = D_INNER // HEADS

        def _mobius_perm(mobius, H, W):
            ys, xs = jnp.meshgrid(jnp.linspace(-1.0, 1.0, H), jnp.linspace(-1.0, 1.0, W), indexing='ij')
            z = (xs + 1j * ys).reshape(-1).astype(jnp.complex64)
            perms = []
            for h in range(mobius.shape[0]):
                a, b, c, d = (mobius[h, 0], mobius[h, 1], mobius[h, 2], mobius[h, 3])
                s = jnp.sqrt(jnp.clip(jnp.abs(a * d - b * c), 0.001))
                a, b, c, d = (a / s, b / s, c / s, d / s)
                w = (a * z + b) / (c * z + d + 1e-06)
                score = jnp.real(w) + 1.3 * jnp.imag(w)
                perms.append(jnp.argsort(score))
            return jnp.stack(perms, 0)

        def _gather_last(v, idx):
            return jnp.take_along_axis(v, jnp.broadcast_to(idx, v.shape[:-1] + (idx.shape[-1],)), axis=-1)

        def _selective_scan(x, dt, A, Bt, Ct, D):
            Bsz, Hh, Dh, N = x.shape
            S = A.shape[-1]
            dA = jnp.exp(dt[:, :, None, :] * A[None, :, :, None])
            dB = dt[:, :, None, :] * Bt

            def step(h, inp):
                dA_t, dB_t, x_t, C_t = inp
                h = dA_t[:, :, None, :] * h + dB_t[:, :, None, :] * x_t[..., None]
                y_t = jnp.einsum('bhds,bhs->bhd', h, C_t)
                return (h, y_t)
            h0 = jnp.zeros((Bsz, Hh, Dh, S), x.dtype)
            inputs = (jnp.moveaxis(dA, -1, 0), jnp.moveaxis(dB, -1, 0), jnp.moveaxis(x, -1, 0), jnp.moveaxis(Ct, -1, 0))
            _, ys = lax.scan(step, h0, inputs)
            return jnp.moveaxis(ys, 0, -1) + D[None, :, None, None] * x
        Bsz, _, H, W = x.shape
        N = H * W
        heads, S = A_log.shape
        d_inner = dw_w.shape[0]
        d_head = d_inner // heads
        xz = jax.nn.silu(jnp.einsum('oc,bchw->bohw', in_proj_w, x) + in_proj_b[None, :, None, None])
        x_ssm, res, gate = jnp.split(xz, 3, axis=1)
        xf = x_ssm.reshape(Bsz, d_inner, N)
        xf = lax.conv_general_dilated(xf, dw_w, (1,), [(1, 1)], dimension_numbers=('NCH', 'OIH', 'NCH'), feature_group_count=d_inner) + dw_b[None, :, None]
        xf = jax.nn.silu(xf)
        x_h = xf.reshape(Bsz, heads, d_head, N)
        perm = _mobius_perm(mobius, H, W)
        x_h = _gather_last(x_h, perm[None, :, None, :])
        dbc = (jnp.einsum('oc,bcn->bon', dbc_w, xf) + dbc_b[None, :, None]).reshape(Bsz, heads, 1 + 2 * S, N)
        dt = jax.nn.softplus(dbc[:, :, 0])
        B_t = dbc[:, :, 1:1 + S]
        C_t = dbc[:, :, 1 + S:]
        dt = _gather_last(dt, perm[None, :, :])
        B_t = _gather_last(B_t, perm[None, :, None, :])
        C_t = _gather_last(C_t, perm[None, :, None, :])
        A = -jnp.exp(A_log)
        y_h = _selective_scan(x_h, dt, A, B_t, C_t, Dparam)
        inv = jnp.argsort(perm, axis=-1)
        y_h = _gather_last(y_h, inv[None, :, None, :])
        y = y_h.reshape(Bsz, d_inner, H, W)
        y = y * jax.nn.silu(gate) + res
        return jax.nn.silu(jnp.einsum('oc,bchw->bohw', out_proj_w, y) + out_proj_b[None, :, None, None])

    def _gn(v, G=32, eps=1e-05):
        B_, C_, H_, W_ = v.shape
        g = v.reshape(B_, G, C_ // G, H_, W_)
        m = jnp.mean(g, axis=(2, 3, 4), keepdims=True)
        s = jnp.var(g, axis=(2, 3, 4), keepdims=True)
        return ((g - m) / jnp.sqrt(s + eps)).reshape(v.shape)

    def _ln_c(v, eps=1e-06):
        m = jnp.mean(v, axis=1, keepdims=True)
        s = jnp.var(v, axis=1, keepdims=True)
        return (v - m) / jnp.sqrt(s + eps)

    def _ln_t(v, eps=1e-05):
        m = jnp.mean(v, axis=-1, keepdims=True)
        s = jnp.var(v, axis=-1, keepdims=True)
        return (v - m) / jnp.sqrt(s + eps)

    def _to_tokens(v):
        B_, C_, H_, W_ = v.shape
        return v.reshape(B_, C_, H_ * W_).transpose(0, 2, 1)

    def _from_tokens(t, like):
        B_, C_, H_, W_ = like.shape
        return t.transpose(0, 2, 1).reshape(B_, C_, H_, W_)
    x = x + _L0_conv_ref(_gn(x), L0_conv_W1, L0_conv_b1, L0_conv_W2, L0_conv_b2, L0_conv_Wg, L0_conv_bg)
    x = x + _L1_conv_ref(_gn(x), L1_conv_in_proj_w, L1_conv_in_proj_b, L1_conv_dw_w, L1_conv_dw_b, L1_conv_dbc_w, L1_conv_dbc_b, L1_conv_A_log, L1_conv_Dparam, L1_conv_mobius, L1_conv_out_proj_w, L1_conv_out_proj_b)
    return x

_drawn_inputs = setup_inputs


def setup_inputs(seed=0):
    import zlib

    import numpy as np

    out = dict(_drawn_inputs(seed))
    spreads = {'L1_conv_in_proj_b': (0.0, 0.311),
     'L1_conv_dw_b': (0.0, 0.8),
     'L1_conv_dbc_b': (0.0, 0.8),
     'L1_conv_Dparam': (1.0, 0.6),
     'L1_conv_out_proj_b': (0.0, 0.1)}
    factors = {'L0_conv_W1': 64.0,
     'L0_conv_b1': 64.0,
     'L0_conv_W2': 64.0,
     'L0_conv_b2': 64.0,
     'L0_conv_Wg': 64.0,
     'L0_conv_bg': 64.0,
     'L1_conv_A_log': 8.0,
     'L1_conv_mobius': 8.0}
    for name, (base, spread) in spreads.items():
        noise = np.random.default_rng([zlib.crc32(name.encode()), seed]).standard_normal(out[name].shape)
        drawn = base * np.exp(spread * noise) if base else spread * noise
        out[name] = jnp.asarray(drawn.astype(out[name].dtype))
    for name, factor in factors.items():
        out[name] = (out[name] * factor).astype(out[name].dtype)
    return out
```

```python
import numpy as np
from contextlib import ExitStack

import concourse.bass as bass
from concourse import mybir

F32 = mybir.dt.float32
U32 = mybir.dt.uint32
ALU = mybir.AluOpType
ACT = mybir.ActivationFunctionType
AX = mybir.AxisListType

P = 128
B, C, IMG = 16, 256, 32
N = IMG * IMG
CT = C // P
H, S = 2, 8
E, R = 8, 16
NB = 2
PH = B // NB
NT = N // P
L = 16
CPT = P // L
NC = N // L
K1 = 1 + 2 * S
ROW = NB * (P + K1)
Q = NB * NT
HALF = 512
EPS = 1e-5

SEG, CUM, TOT = 0, Q * L, Q * L + Q
EEW = TOT + Q * CPT

CONST_WIDTHS = dict(ident=P, after=P, upto=P, ones=P, group=P, before=P, notbefore=P,
                    fromstart=L, chunk=CPT, causal=P, diag=L, gridcol=2 * NT)
CONST_AT = {}
_at = 0
for _name, _width in CONST_WIDTHS.items():
    CONST_AT[_name] = _at
    _at += _width
CONST_W = _at

PRM_P, PRM_A, PRM_B, PRM_BIAS, PRM_W = 0, 2, 4, 6, 12


def constants():
    r, c = np.arange(P)[:, None], np.arange(P)[None, :]
    same = (r // L) == (c // L)
    lin = np.linspace(-1.0, 1.0, IMG).astype(np.float32)
    gy, gx = (v.reshape(-1) for v in np.meshgrid(lin, lin, indexing="ij"))
    part = dict(
        ident=r == c, after=same & (r > c), upto=same & (r <= c), ones=np.ones((P, P)),
        group=((r // 8) == (c // 8)) / 8.0, before=c < r, notbefore=c >= r,
        fromstart=(r % L) <= c[:, :L], chunk=(r // L) == c[:, :CPT], causal=same & (c >= r),
        diag=(r % L) == c[:, :L],
        gridcol=np.concatenate([gx.reshape(NT, P).T, gy.reshape(NT, P).T], 1))
    table = np.concatenate([part[k].astype(np.float32) for k in CONST_WIDTHS], 1)
    return np.ascontiguousarray(table), np.ascontiguousarray(np.stack([gx, gy])[None].astype(np.float32))


def build(nc, x_d, w1g_d, b1g_d, w2_d, b2_d, inw_d, inb_d, dww_d, dwb_d, dbcw_d, dbcb_d, alog_d,
          dpar_d, mob_d, outw_d, outb_d, const_d, grid_d, out_d):
    with ExitStack() as ctx:
        def sb(name, width, dt=F32):
            return ctx.enter_context(nc.sbuf_tensor(name, [P, width], dt))

        def sem(name):
            return ctx.enter_context(nc.semaphore(name))

        def v(tensor, off, *dims, parts=P, p0=0):
            width = tensor.shape[1]
            assert off + sum(st_ * (n_ - 1) for st_, n_ in dims) < width if isinstance(off, int) else True, (tensor.name, off, dims)
            return bass.AP(tensor, p0 * width + off, [[width, parts]] + [list(d) for d in dims])

        xt_d = nc.dram_tensor("xt_scratch", [H * N, ROW], F32)
        yt_d = nc.dram_tensor("yt_scratch", [H * N, NB * P], F32)
        cd_d = nc.dram_tensor("cd_scratch", [H * N, S * NB], F32)

        cst = sb("cst", CONST_W)
        inw = sb("inw", CT * 3 * C)
        outw = sb("outw", CT * C)
        dbcw = sb("dbcw", CT * H * K1)
        small = sb("small", 96)
        xb = [sb("xb0", NB * CT * N), sb("xb1", NB * CT * N)]
        wa = sb("wa", NB * CT * C)
        wc = sb("wc", NB * CT * 2 * C)
        xs = sb("xs", CT * (N + 2))
        xf = sb("xf", CT * N)
        stage = sb("stage", NT * H * ROW)
        xp = sb("xp", H * NT * ROW)
        crow = sb("crow", H * NT * L * S * NB)
        big = sb("big", S * EEW + S * Q * L)
        mblk = sb("mblk", Q * P)
        bblk = sb("bblk", Q * CPT * S)
        cblk = sb("cblk", Q * CPT * S)
        m16 = sb("m16", Q * L)
        rseg = sb("rseg", H * Q * L)
        rtot = sb("rtot", H * Q * CPT)
        dts = sb("dts", 8 * H * Q)
        bc8 = sb("bc8", 3 * Q * S)
        hs = sb("hs", NB * (NC + 1) * S)
        ch = sb("ch", 2 * 2 * P)
        gt = sb("gt", NB * CT * N)
        rs = sb("rs", NB * CT * N)
        prm = sb("prm", B * PRM_W)
        pcur = sb("pcur", 2 * NB * PRM_W)
        idx = sb("idx", H * NT, U32)
        W_OFF = S * EEW

        INB, DWW, DWB, OUTB, DBCB, ANEG, DPAR, MOB = 0, 6, 12, 14, 16, 50, 66, 68

        pj = [ctx.enter_context(nc.psum_tensor(f"pj{i}", [P, HALF], F32)) for i in range(4)]
        tp = [ctx.enter_context(nc.psum_tensor(f"tp{i}", [P, HALF], F32)) for i in range(2)]
        sg = ctx.enter_context(nc.psum_tensor("sg", [P, HALF], F32))
        st = ctx.enter_context(nc.psum_tensor("st", [P, HALF], F32))

        def const(name, *dims, off=0, parts=P):
            width = CONST_WIDTHS[name]
            return v(cst, CONST_AT[name] + off, *(dims or ((1, width),)), parts=parts)

        weights_in = sem("weights_in")
        x_in = [sem("x_in0"), sem("x_in1")]
        out_stored = [sem("out_stored0"), sem("out_stored1")]
        rows_scattered = sem("rows_scattered")
        rows_in = sem("rows_in")
        c_stored = sem("c_stored")
        crow_in = sem("crow_in")
        y_stored = sem("y_stored")
        y_gathered = sem("y_gathered")
        stats_done = sem("stats_done")
        setup_v = sem("setup_v")
        setup_a = sem("setup_a")
        setup_p = sem("setup_p")
        setup_g = sem("setup_g")
        params_ready = sem("params_ready")
        pcur_ready = sem("pcur_ready")
        wa_ready = sem("wa_ready")
        wc_ready = sem("wc_ready")
        pj_full = sem("pj_full")
        pj_drained = sem("pj_drained")
        tp_full = sem("tp_full")
        tp_drained = sem("tp_drained")
        conv_step = sem("conv_step")
        xf_ready = sem("xf_ready")
        sp_v = sem("sp_v")
        sp_a = sem("sp_a")
        r_ready = sem("r_ready")
        sg_full = sem("sg_full")
        ee_ready = sem("ee_ready")
        w_ready = sem("w_ready")
        bc_step = sem("bc_step")
        blk_ready = sem("blk_ready")
        m_step = sem("m_step")
        mblk_ready = sem("mblk_ready")
        st_full = sem("st_full")
        hs_ready = sem("hs_ready")
        ch_used = sem("ch_used")
        g_ready = sem("g_ready")
        z_half = sem("z_half")
        z_ready = sem("z_ready")
        x1_ready = sem("x1_ready")
        out_ready = sem("out_ready")
        pool_passed = sem("pool_passed")

        def base(stage_name, i, a, b, c):
            if stage_name == "A":
                return 0 if isinstance(i, int) and i == 0 else i * (a + b + c) - c
            if stage_name == "B":
                return i * (a + b + c) + a
            last = isinstance(i, int) and i == PH - 1
            return i * (a + b + c) + (a + b if last else 2 * a + b)

        PJA, PJB, PJC = NB * 4, H * NB * 2, NB * 12
        TPA, TPB, TPC = NB * NT, H * NB * NT // 2, NB * H * 2

        def pjb(s, i):
            return base(s, i, PJA, PJB, PJC)

        def pjf(s, i):
            return base(s, i, PJA, 0, PJC)

        def tpb(s, i):
            return base(s, i, TPA, TPB, TPC)

        def wait(eng, semaphore, value):
            if isinstance(value, int) and value <= 0:
                return
            eng.wait_ge(semaphore, value)

        def phases(eng, stage_a, stage_b, stage_c):
            stage_a(0, 0, 0)
            stage_b(0, 0, 0)
            stage_a(1, 1, 0)
            stage_c(0, 0, 0)
            with eng.Fori(0, (PH - 2) // 2) as t:
                i = t * 2 + 1
                stage_b(i, 1, t)
                stage_a(i + 1, 0, t + 1)
                stage_c(i, 1, t)
                stage_b(i + 1, 0, t + 1)
                stage_a(i + 2, 1, t + 1)
                stage_c(i + 1, 0, t + 1)
            stage_b(PH - 1, 1, PH // 2 - 1)
            stage_c(PH - 1, 1, PH // 2 - 1)

        def x_view(par, b, ct, off=0, n=N):
            return v(xb[par], (b * CT + ct) * N + off, (1, n))

        x_dram = x_d.rearrange("b (t p) n -> p b t n", p=P)
        out_dram = out_d.rearrange("b (t p) n -> p b t n", p=P)
        WEIGHTS = 16 * 16

        def pair(i):
            return slice(i * NB, i * NB + NB) if isinstance(i, int) else bass.ds(i * NB, NB)

        block = ctx.enter_context(nc.Block())

        @block.sync
        def _(sp):
            def bcast(src, n):
                return bass.AP(src.tensor, 0, [[0, P], [1, n]])

            def load_x(i, par):
                sp.dma_start(v(xb[par], 0, (CT * N, NB), (N, CT), (1, N)), x_dram[:, pair(i)]).then_inc(x_in[par], 16)

            load_x(0, 0)
            sp.dma_start(cst[:, :], const_d).then_inc(weights_in, 16)
            sp.dma_start(v(gt, 0, (N, 2), (1, N)), bass.AP(grid_d.tensor, 0, [[0, P], [N, 2], [1, N]])).then_inc(weights_in, 16)
            sp.dma_start(v(small, MOB, (1, 8)), bcast(mob_d, 8)).then_inc(weights_in, 16)
            sp.dma_start(v(small, ANEG, (1, 16)), bcast(alog_d, 16)).then_inc(weights_in, 16)
            sp.dma_start(v(small, DPAR, (1, 2)), bcast(dpar_d, 2)).then_inc(weights_in, 16)
            sp.dma_start(v(small, DBCB, (1, H * K1)), bcast(dbcb_d, H * K1)).then_inc(weights_in, 16)
            load_x(1, 1)
            sp.dma_start(v(small, INB, (1, 6)), inb_d).then_inc(weights_in, 16)
            sp.dma_start(v(small, DWW, (1, 6)), dww_d).then_inc(weights_in, 16)
            sp.dma_start(v(small, DWB, (1, 2)), dwb_d).then_inc(weights_in, 16)
            sp.dma_start(v(small, OUTB, (1, 2)), outb_d).then_inc(weights_in, 16)
            sp.dma_start(v(inw, 0, (3 * C, CT), (1, 3 * C)), inw_d).then_inc(weights_in, 16)
            sp.dma_start(v(outw, 0, (C, CT), (1, C)), outw_d).then_inc(weights_in, 16)
            sp.dma_start(v(dbcw, 0, (H * K1, CT), (1, H * K1)), dbcw_d).then_inc(weights_in, 16)
            sp.dma_start(v(xp, 0, (136, CT), (1, 136)), w1g_d).then_inc(weights_in, 16)
            sp.dma_start(v(xp, 272, (1, 136), parts=1), b1g_d).then_inc(weights_in, 16)
            sp.dma_start(v(xp, 408, (1, C)), w2_d).then_inc(weights_in, 16)
            sp.dma_start(v(xp, 664, (1, C), parts=E), b2_d).then_inc(weights_in, 16)
            for i in range(2, PH):
                sp.wait_ge(stats_done, i - 1)
                load_x(i, i % 2)
            for i in range(2):
                sp.wait_ge(stats_done, PH - 1 + i)
                load_x(i, i)

            def load_rows(i):
                sp.wait_ge(rows_scattered, 256 * (i + 1))
                if not (isinstance(i, int) and i == 0):
                    sp.wait_ge(pj_drained, pjb("B", i - 1) + PJB)
                else:
                    sp.wait_ge(params_ready, 1)
                sp.dma_start(v(xp, 0, (ROW, H * NT), (1, ROW)),
                             bass.AP(xt_d, 0, [[ROW, P], [P * ROW, H * NT], [1, ROW]])).then_inc(rows_in, 16)
                sp.wait_ge(rows_in, 16 * (i + 1))
                sp.dma_start(bass.AP(cd_d, 0, [[S * NB, P], [P * S * NB, H * NT], [1, S * NB]]),
                             v(xp, NB * (P + 1 + S), (ROW, H * NT), (1, S * NB))).then_inc(c_stored, 16)
                sp.wait_ge(c_stored, 16 * (i + 1))
                for c in range(CPT):
                    run = L * S * NB
                    sp.dma_start(v(crow, 0, (run, H * NT), (1, run), parts=L, p0=c * L),
                                 bass.AP(cd_d, c * run, [[0, L], [CPT * run, H * NT], [1, run]])).then_inc(crow_in, 16)

            def stage_a(i, par, half):
                load_rows(i)

            def stage_b(i, par, half):
                for h in range(H):
                    sp.wait_ge(pj_drained, pjb("B", i) + (h + 1) * NB * 2)
                    sp.dma_start(bass.AP(yt_d, h * N * NB * P, [[NB * P, P], [P * NB * P, NT], [1, NB * P]]),
                                 v(stage, h * NT * NB * P, (NB * P, NT), (1, NB * P))).then_inc(y_stored, 16)

            def stage_c(i, par, half):
                for b in range(NB):
                    sp.wait_ge(out_ready, (i * NB + b + 1) * CT)
                    at = i * NB + b
                    dst = out_dram[:, at:at + 1] if isinstance(at, int) else out_dram[:, bass.ds(at, 1)]
                    sp.dma_start(dst, v(xb[par], b * CT * N, (CT * N, 1), (N, CT), (1, N))).then_inc(out_stored[par], 16)
                if isinstance(i, int) and i >= PH - 2:
                    return
                sp.wait_ge(out_stored[par], 32 * (half + 1))
                load_x(i + 2, par) if isinstance(i, int) else load_x(i + 2, par)

            stage_a(0, 0, 0)
            stage_b(0, 0, 0)
            stage_a(1, 1, 0)
            stage_c(0, 0, 0)
            with sp.Fori(0, (PH - 4) // 2) as t:
                i = t * 2 + 1
                stage_b(i, 1, t)
                stage_a(i + 1, 0, t + 1)
                stage_c(i, 1, t)
                stage_b(i + 1, 0, t + 1)
                stage_a(i + 2, 1, t + 1)
                stage_c(i + 1, 0, t + 1)
            for i in range(PH - 3, PH):
                stage_b(i, i % 2, i // 2)
                if i < PH - 1:
                    stage_a(i + 1, (i + 1) % 2, (i + 1) // 2)
                stage_c(i, i % 2, i // 2)
            for par in range(2):
                sp.wait_ge(out_stored[par], 16 * B // 2)

        @block.gpsimd
        def _(pool):
            pool.wait_ge(params_ready, 1)

            def hold(semaphore, value):
                if isinstance(value, int) and value <= 0:
                    return
                pool.wait_ge(semaphore, value)
                pool.sem_inc(pool_passed, 1)


            def scatter(i):
                for nt in range(NT):
                    for h in range(H):
                        if h == 0:
                            hold(tp_drained, tpb("A", i) + NT + nt + 1)
                        k = h * NT + nt
                        pool.indirect_dma_start(
                            out=xt_d.ap(), out_offset=bass.IndirectOffsetOnAxis(ap=idx[:, k:k + 1], axis=0),
                            in_=v(stage, (nt * H + h) * ROW, (1, ROW)), in_offset=None).then_inc(rows_scattered, 16)

            def stage_a(i, par, half):
                hold(pcur_ready, i + 1)
                for b in range(NB):
                    if not (isinstance(i, int) and i == 0):
                        hold(pj_full, pjf("A", i - 1) + (b + 1) * 4)
                    for ct in range(CT):
                        last = nc.gpsimd.tensor_scalar(v(wa, (b * CT + ct) * C, (1, C)), v(inw, ct * 3 * C, (1, C)),
                                                       v(pcur, (par * NB + b) * PRM_W + PRM_P + ct, (1, 1)), 0.0,
                                                       ALU.mult, ALU.add)
                    last.then_inc(wa_ready, 1)
                if not (isinstance(i, int) and i == 0):
                    gather(i - 1)
                    hold(rows_in, 16 * i)
                scatter(i)

            def gather(i):
                hold(y_stored, 32 * (i + 1))
                hold(mblk_ready, H * (i + 1))
                hold(hs_ready, H * NB * S * (i + 1))
                for h in range(H):
                    for nt in range(NT):
                        k = h * NT + nt
                        pool.indirect_dma_start(
                            out=v(big, k * NB * P, (1, NB * P)), out_offset=None, in_=yt_d.ap(),
                            in_offset=bass.IndirectOffsetOnAxis(ap=idx[:, k:k + 1], axis=0)).then_inc(y_gathered, 16)

            def stage_b(i, par, half):
                hold(crow_in, 16 * CPT * (i + 1))
                for h in range(H):
                    hold(ee_ready, i * H + h + 1)
                    hold(m_step, (i * H + h) * 3)
                    for s in range(S):
                        for b in range(NB):
                            last = nc.gpsimd.tensor_tensor(
                                v(big, W_OFF + (s * Q + b * NT) * L, (L, NT), (1, L)),
                                v(big, s * EEW + SEG + b * NT * L, (L, NT), (1, L)),
                                v(crow, h * NT * L * S * NB + s * NB + b, (L * S * NB, NT), (S * NB, L)), ALU.mult)
                    last.then_inc(w_ready, 1)
                for b in range(NB):
                    if not (isinstance(i, int) and i == 0):
                        hold(pj_full, pjf("C", i - 1) + (b + 1) * 8)
                    for ct in range(CT):
                        last = nc.gpsimd.tensor_scalar(v(wc, (b * CT + ct) * 2 * C, (1, 2 * C)), v(inw, ct * 3 * C + C, (1, 2 * C)),
                                                       v(pcur, (par * NB + b) * PRM_W + PRM_P + ct, (1, 1)), 0.0,
                                                       ALU.mult, ALU.add)
                    last.then_inc(wc_ready, 1)

            def stage_c(i, par, half):
                if isinstance(i, int) and i == PH - 1:
                    gather(i)
                for b in range(NB):
                    hold(pj_full, pjf("C", i) + (b + 1) * 8)
                    for ct in range(CT):
                        o = (par * NB + b) * PRM_W
                        last = nc.gpsimd.tensor_scalar(x_view(par, b, ct), x_view(par, b, ct), v(pcur, o + PRM_A + ct, (1, 1)),
                                                       v(pcur, o + PRM_B + ct, (1, 1)), ALU.mult, ALU.add)
                    last.then_inc(x1_ready, 1)

            phases(pool, stage_a, stage_b, stage_c)

        @block.scalar
        def _(act):
            n_a = [0]

            def did(ins):
                n_a[0] += 1
                ins.then_inc(setup_a, 1)

            act.wait_ge(weights_in, WEIGHTS + 16)
            did(nc.scalar.activation(v(small, ANEG, (1, 16)), v(small, ANEG, (1, 16)), ACT.Exp))
            act.wait_ge(setup_v, V_MOB)
            did(nc.scalar.activation(v(small, MOB + 10, (1, 2)), v(small, MOB + 8, (1, 2)), ACT.Sqrt))
            act.wait_ge(setup_v, V_VAR1)
            did(nc.scalar.activation(v(dts, 0, (1, 32)), v(dts, 0, (1, 32)), ACT.Sqrt))
            act.wait_ge(setup_v, V_MAX)
            did(nc.scalar.activation(v(bc8, 0, (1, E), parts=B), v(bc8, 0, (1, E), parts=B), ACT.Exp,
                                     bias=v(bc8, 140, (1, 1), parts=B), accum_out=v(bc8, 141, (1, 1), parts=B)))
            act.wait_ge(setup_p, P_EXPERT)
            did(nc.scalar.activation(v(dts, 96, (1, 32)), v(tp[1], 0, (1, 32)), ACT.Exp, scale=-1.0))
            act.wait_ge(setup_v, V_VAR2)
            did(nc.scalar.activation(v(dts, 0, (1, 32)), v(dts, 0, (1, 32)), ACT.Sqrt))
            act.wait_ge(params_ready, 1)

            def stage_a(i, par, half):
                u = pjf("A", i)
                k = 0
                act.wait_ge(pcur_ready, i + 1)
                for b in range(NB):
                    for ot in range(CT):
                        if b == 1 or not (isinstance(i, int) and i == 0):
                            act.wait_ge(conv_step, (i * NB + b - 1) * CT * 3 + (ot + 1) * 3)
                        for nt in range(2):
                            act.wait_ge(pj_full, u + k + 1)
                            nc.scalar.activation(v(xs, ot * (N + 2) + 1 + nt * HALF, (1, HALF)), pj[k % 4][:, :], ACT.Silu,
                                                 bias=v(pcur, (par * NB + b) * PRM_W + PRM_BIAS + ot, (1, 1))).then_inc(pj_drained, 1)
                            k += 1
                    for ot in range(CT):
                        act.wait_ge(conv_step, (i * NB + b) * CT * 3 + (ot + 1) * 3)
                        nc.scalar.activation(v(xf, ot * N, (1, N)), v(xf, ot * N, (1, N)), ACT.Silu,
                                             bias=v(small, DWB + ot, (1, 1))).then_inc(xf_ready, 1)

            def stage_b(i, par, half):
                act.wait_ge(sp_v, i * 9 + 1)
                nc.scalar.activation(v(dts, 32, (1, 32)), v(dts, 0, (1, 32)), ACT.Exp, scale=-1.0).then_inc(sp_a, 1)
                act.wait_ge(sp_v, i * 9 + 2)
                nc.scalar.activation(v(dts, 96, (1, 32)), v(dts, 64, (1, 32)), ACT.Ln).then_inc(sp_a, 1)

                def decays(h):
                    act.wait_ge(sg_full, i * H + h + 1)
                    if h == 0:
                        if not (isinstance(i, int) and i == 0):
                            act.wait_ge(tp_full, tpb("C", i - 1) + TPC)
                    else:
                        act.wait_ge(w_ready, i * H + h)
                        act.wait_ge(hs_ready, (i * H + h) * NB * S)
                    for s in range(S):
                        last = nc.scalar.activation(v(big, s * EEW, (1, EEW)), v(sg, 0, (1, EEW)), ACT.Exp,
                                                    scale=v(small, ANEG + h * S + s, (1, 1)))
                    last.then_inc(ee_ready, 1)

                def results(h):
                    for b in range(NB):
                        act.wait_ge(ch_used, i * 16 + (h * NB + b) * 4 + 4)
                        for e in range(2):
                            k = (h * NB + b) * 2 + e
                            if k == 0:
                                act.wait_ge(rows_in, 16 * (i + 1))
                            nc.scalar.copy(v(stage, (h * NT + e) * NB * P + b * P, (2 * NB * P, 4), (1, P)),
                                           v(pj[k % 4], 0, (P, 4), (1, P))).then_inc(pj_drained, 1)

                decays(0)
                decays(1)
                results(0)
                results(1)

            def stage_c(i, par, half):
                u = pjf("C", i)
                drained = pjb("C", i)

                def silu(k, dst, bias):
                    act.wait_ge(pj_full, u + k + 1)
                    nc.scalar.activation(dst, pj[k % 4][:, :], ACT.Silu, bias=bias).then_inc(pj_drained, 1)

                def gate_and_residual(b):
                    o = (par * NB + b) * PRM_W + PRM_BIAS
                    if not (isinstance(i, int) and i == 0):
                        act.wait_ge(pj_full, pjf("C", i - 1) + NB * 8 + (b + 1) * 4)
                        act.wait_ge(out_ready, ((i - 1) * NB + b + 1) * CT)
                    for ct in range(CT):
                        for nt in range(2):
                            silu(b * 8 + ct * 2 + nt, v(gt, (b * CT + ct) * N + nt * HALF, (1, HALF)), v(pcur, o + 4 + ct, (1, 1)))
                        act.wait_ge(pj_drained, drained + b * 8 + ct * 2 + 2)
                        g = v(gt, (b * CT + ct) * N, (1, N))
                        nc.scalar.activation(g, g, ACT.Silu).then_inc(g_ready, 1)
                    for ct in range(CT):
                        for nt in range(2):
                            silu(b * 8 + 4 + ct * 2 + nt, v(rs, (b * CT + ct) * N + nt * HALF, (1, HALF)), v(pcur, o + 2 + ct, (1, 1)))

                def output(b):
                    act.wait_ge(z_ready, (i * NB + b + 1) * 4)
                    for ot in range(CT):
                        for nt in range(2):
                            silu(16 + b * 4 + ot * 2 + nt, v(rs, (b * CT + ot) * N + nt * HALF, (1, HALF)), v(small, OUTB + ot, (1, 1)))

                for b in range(NB):
                    gate_and_residual(b)
                for b in range(NB):
                    output(b)

            phases(act, stage_a, stage_b, stage_c)

        @block.vector
        def _(dve):
            n = [0]

            def link(ins):
                n[0] += 1
                ins.then_inc(setup_v, 1)
                dve.wait_ge(setup_v, n[0])

            def mark(number):
                assert n[0] == number, n[0]

            nc.vector.memset(v(xs, 0, (N + 2, CT), (1, 1)), 0.0)
            nc.vector.memset(v(xs, N + 1, (N + 2, CT), (1, 1)), 0.0)
            link(nc.vector.memset(v(hs, 0, ((NC + 1) * S, NB), (1, S)), 0.0))

            dve.wait_ge(weights_in, WEIGHTS + 16)
            m = MOB
            link(nc.vector.tensor_tensor(v(small, m + 8, (1, 2)), v(small, m, (4, 2)), v(small, m + 3, (4, 2)), ALU.mult))
            link(nc.vector.tensor_tensor(v(small, m + 10, (1, 2)), v(small, m + 1, (4, 2)), v(small, m + 2, (4, 2)), ALU.mult))
            link(nc.vector.tensor_tensor(v(small, m + 8, (1, 2)), v(small, m + 8, (1, 2)), v(small, m + 10, (1, 2)), ALU.subtract))
            link(nc.vector.scalar_tensor_tensor(v(small, m + 8, (1, 2)), v(small, m + 8, (1, 2)), -1.0, v(small, m + 8, (1, 2)), ALU.mult, ALU.max))
            link(nc.vector.tensor_scalar(v(small, m + 8, (1, 2)), v(small, m + 8, (1, 2)), 1e-3, None, ALU.max))
            mark(V_MOB)
            dve.wait_ge(setup_a, 2)
            link(nc.vector.reciprocal(v(small, m + 12, (1, 2)), v(small, m + 10, (1, 2))))
            for h in range(H):
                link(nc.vector.tensor_scalar(v(small, m + 4 * h, (1, 4)), v(small, m + 4 * h, (1, 4)), v(small, m + 12 + h, (1, 1)), None, ALU.mult))
            link(nc.vector.tensor_scalar(v(small, m + 3, (4, 2)), v(small, m + 3, (4, 2)), 1e-6, None, ALU.add))
            link(nc.vector.tensor_scalar(v(small, ANEG, (1, 16)), v(small, ANEG, (1, 16)), -1.0, None, ALU.mult))
            WIDE = N + NT
            xfw = [v(stage, k * WIDE, (1, WIDE)) for k in range(4)]
            for k in range(2):
                nc.vector.tensor_copy(v(crow, (1 + k) * WIDE, (1, N)), v(gt, k * N, (1, N)))
                link(nc.vector.tensor_copy(v(crow, (1 + k) * WIDE + N, (1, NT)), const("gridcol", (1, NT), off=k * NT)))
            gx, gy = (v(crow, (1 + k) * WIDE, (1, WIDE)) for k in range(2))
            nr, ni, dr, di = xfw
            t0, den, num = v(mblk, 0, (1, WIDE)), v(big, 0, (1, WIDE)), v(big, WIDE, (1, WIDE))
            t1 = v(big, 2 * WIDE, (1, WIDE))
            score = [v(big, 3 * WIDE, (1, WIDE)), v(crow, 0, (1, WIDE))]
            for h in range(H):
                a_, b_, c_, d_ = (v(small, m + 4 * h + k, (1, 1)) for k in range(4))
                nc.vector.tensor_scalar(nr, gx, a_, b_, ALU.mult, ALU.add)
                nc.vector.tensor_scalar(ni, gy, a_, None, ALU.mult)
                nc.vector.tensor_scalar(dr, gx, c_, d_, ALU.mult, ALU.add)
                link(nc.vector.tensor_scalar(di, gy, c_, None, ALU.mult))
                nc.vector.tensor_tensor(t0, dr, dr, ALU.mult)
                link(nc.vector.tensor_tensor(t1, di, di, ALU.mult))
                link(nc.vector.tensor_tensor(den, t0, t1, ALU.add))
                nc.vector.tensor_tensor(t0, nr, dr, ALU.mult)
                link(nc.vector.tensor_tensor(t1, ni, di, ALU.mult))
                link(nc.vector.tensor_tensor(num, t0, t1, ALU.add))
                nc.vector.tensor_tensor(t0, ni, dr, ALU.mult)
                link(nc.vector.tensor_tensor(t1, nr, di, ALU.mult))
                link(nc.vector.tensor_tensor(t0, t0, t1, ALU.subtract))
                link(nc.vector.scalar_tensor_tensor(num, t0, 1.3, num, ALU.mult, ALU.add))
                link(nc.vector.reciprocal(den, den))
                link(nc.vector.tensor_tensor(num, num, den, ALU.mult))
                link(nc.vector.tensor_scalar(score[h], num, 3.4e38, -3.4e38, ALU.min, ALU.max))
            counts = v(m16, 0, (1, 4 * H * NT))
            link(nc.vector.memset(counts, 0.0))
            for h in range(H):
                for nt in range(NT):
                    mine = v(score[h].tensor, score[h].offset + N + nt, (1, 1))

                    def span(lo, hi):
                        return v(score[h].tensor, score[h].offset + lo, (1, hi - lo))

                    def count(k):
                        return v(m16, (h * NT + nt) * 4 + k, (1, 1))

                    lo, hi = nt * P, nt * P + P
                    if nt:
                        nc.vector.tensor_scalar(v(mblk, 0, (1, lo)), span(0, lo), mine, None, ALU.is_le, ALU.add, accum_out=count(0))
                    if nt < NT - 1:
                        nc.vector.tensor_scalar(v(mblk, N - P, (1, N - hi)), span(hi, N), mine, None, ALU.is_lt, ALU.add, accum_out=count(1))
                    nc.vector.scalar_tensor_tensor(v(mblk, 2 * (N - P), (1, P)), span(lo, hi), mine, const("before"), ALU.is_le, ALU.mult, accum_out=count(2))
                    link(nc.vector.scalar_tensor_tensor(v(mblk, 2 * N - P, (1, P)), span(lo, hi), mine, const("notbefore"), ALU.is_lt, ALU.mult, accum_out=count(3)))
            link(nc.vector.tensor_reduce(v(bblk, 0, (1, H * NT)), v(m16, 0, (4, H * NT), (1, 4)), AX.X, ALU.add))
            nc.vector.tensor_scalar(v(idx, 0, (1, NT)), v(bblk, 0, (1, NT)), 0.0, None, ALU.add)
            link(nc.vector.tensor_scalar(v(idx, NT, (1, NT)), v(bblk, NT, (1, NT)), float(N), None, ALU.add))

            SW = 24
            for i in range(PH):
                dve.wait_ge(x_in[i % 2], 16 * (i // 2 + 1))
                for b in range(NB):
                    for ct in range(CT):
                        for half in range(2):
                            unit = ct * B + i * NB + b
                            last = nc.vector.bn_stats(v(rs, unit * 12 + half * 6, (1, 6)), x_view(i % 2, b, ct, half * HALF, HALF))
                last.then_inc(stats_done, 1)
            dve.wait_ge(stats_done, PH)
            U = CT * B
            MEAN, SQ, T = 1024, 1024 + U, 1024 + 2 * U
            col = lambda off: v(rs, off, (1, U))
            link(nc.vector.tensor_reduce(col(MEAN), v(rs, 1, (12, U), (3, 4)), AX.X, ALU.add))
            link(nc.vector.tensor_scalar(col(MEAN), col(MEAN), 0.25, None, ALU.mult))
            link(nc.vector.tensor_tensor(v(rs, 1200, (4, U), (1, 4)), v(rs, 1, (12, U), (3, 4)), v(rs, 1, (12, U), (3, 4)), ALU.mult))
            link(nc.vector.tensor_reduce(col(SQ), v(rs, 1200, (4, U), (1, 4)), AX.X, ALU.add))
            link(nc.vector.tensor_reduce(col(T), v(rs, 2, (12, U), (3, 4)), AX.X, ALU.add))
            link(nc.vector.tensor_scalar(col(T), col(T), 1.0 / N, None, ALU.mult))
            link(nc.vector.scalar_tensor_tensor(col(SQ), col(SQ), 0.25, col(T), ALU.mult, ALU.add))
            mark(V_STATS)

            def group_rstd(sqrt_number):
                link(nc.vector.tensor_copy(v(dts, 32, (1, U)), v(tp[0], 0, (1, U))))
                link(nc.vector.tensor_tensor(v(dts, 64, (1, U)), v(dts, 32, (1, U)), v(dts, 32, (1, U)), ALU.mult))
                link(nc.vector.tensor_tensor(v(dts, 0, (1, U)), v(tp[0], U, (1, U)), v(dts, 64, (1, U)), ALU.subtract))
                link(nc.vector.tensor_scalar(v(dts, 0, (1, U)), v(dts, 0, (1, U)), 0.0, EPS, ALU.max, ALU.add))

            MG, RSTD = v(dts, 32, (1, U)), v(dts, 128, (1, U))
            dve.wait_ge(setup_p, 1)
            group_rstd(3)
            mark(V_VAR1)
            dve.wait_ge(setup_a, 3)
            link(nc.vector.reciprocal(RSTD, v(dts, 0, (1, U))))
            link(nc.vector.tensor_tensor(col(T), col(MEAN), MG, ALU.subtract))
            link(nc.vector.tensor_tensor(col(T), col(T), RSTD, ALU.mult))
            mark(V_Y)
            dve.wait_ge(setup_p, 2)
            link(nc.vector.tensor_copy(v(bc8, 0, (1, 136), parts=B), v(tp[1], 0, (1, 136), parts=B)))
            link(nc.vector.reduce_max(v(bc8, 140, (1, 1), parts=B), v(bc8, 0, (1, E), parts=B), AX.X))
            link(nc.vector.tensor_scalar(v(bc8, 140, (1, 1), parts=B), v(bc8, 140, (1, 1), parts=B), -1.0, None, ALU.mult))
            mark(V_MAX)
            dve.wait_ge(setup_a, 4)
            link(nc.vector.reciprocal(v(bc8, 142, (1, 1), parts=B), v(bc8, 141, (1, 1), parts=B)))
            link(nc.vector.tensor_scalar(v(bc8, 0, (1, E), parts=B), v(bc8, 0, (1, E), parts=B), v(bc8, 142, (1, 1), parts=B), None, ALU.mult))
            link(nc.vector.scalar_tensor_tensor(v(bc8, 8, (R, E), (1, R), parts=B), v(bc8, 8, (R, E), (1, R), parts=B), 0.0,
                                                v(bc8, 0, (1, E), (0, R), parts=B), ALU.max, ALU.mult))
            mark(V_HID)
            dve.wait_ge(setup_p, 3)
            nc.vector.tensor_copy(v(bc8, 160, (1, B)), v(tp[0], 0, (1, B)))
            link(nc.vector.tensor_copy(v(bc8, 180, (1, B), parts=E), v(tp[0], P, (1, B), parts=E)))
            mark(V_HIDT)
            dve.wait_ge(setup_a, 5)
            SC, A_, B_ = v(dts, 96, (1, U)), v(dts, 160, (1, U)), v(dts, 192, (1, U))
            link(nc.vector.tensor_scalar(SC, SC, 1.0, None, ALU.add))
            link(nc.vector.reciprocal(SC, SC))
            link(nc.vector.tensor_tensor(SC, SC, RSTD, ALU.mult))
            link(nc.vector.tensor_scalar(A_, SC, 1.0, None, ALU.add))
            link(nc.vector.tensor_tensor(B_, SC, MG, ALU.mult))
            link(nc.vector.tensor_scalar(B_, B_, -1.0, None, ALU.mult))
            link(nc.vector.tensor_tensor(col(T), col(MEAN), col(MEAN), ALU.mult))
            link(nc.vector.tensor_tensor(col(SQ), col(SQ), col(T), ALU.subtract))
            link(nc.vector.tensor_tensor(col(SQ), col(SQ), A_, ALU.mult))
            link(nc.vector.tensor_tensor(col(SQ), col(SQ), A_, ALU.mult))
            link(nc.vector.tensor_tensor(col(MEAN), col(MEAN), A_, ALU.mult))
            link(nc.vector.tensor_tensor(col(MEAN), col(MEAN), B_, ALU.add))
            link(nc.vector.tensor_tensor(col(T), col(MEAN), col(MEAN), ALU.mult))
            link(nc.vector.tensor_tensor(col(SQ), col(SQ), col(T), ALU.add))
            mark(V_STATS2)
            dve.wait_ge(setup_p, 5)
            group_rstd(6)
            mark(V_VAR2)
            dve.wait_ge(setup_a, 6)
            link(nc.vector.reciprocal(RSTD, v(dts, 0, (1, U))))
            link(nc.vector.tensor_tensor(SC, B_, MG, ALU.subtract))
            link(nc.vector.tensor_tensor(col(T), SC, RSTD, ALU.mult))
            mark(V_Q)
            per_image = lambda off: v(prm, off, (1, CT), (PRM_W, B))
            nc.vector.tensor_tensor(per_image(PRM_P), v(dts, 128, (B, CT), (1, B)), v(dts, 160, (B, CT), (1, B)), ALU.mult)
            nc.vector.tensor_copy(per_image(PRM_A), v(dts, 160, (B, CT), (1, B)))
            nc.vector.tensor_copy(per_image(PRM_B), v(dts, 192, (B, CT), (1, B)))
            dve.wait_ge(setup_p, 6)
            link(nc.vector.tensor_tensor(v(prm, PRM_BIAS, (1, 6), (PRM_W, B)), v(tp[1], 0, (B, 6), (1, B)),
                                         v(small, INB, (1, 6), (0, B)), ALU.add))
            nc.vector.memset(v(m16, 0, (1, 1)), 0.0).then_inc(params_ready, 1)

            def take_params(i, par):
                if not (isinstance(i, int) and i < 2):
                    dve.wait_ge(x1_ready, (i - 1) * NB)
                    dve.wait_ge(pj_drained, pjb("C", i - 2) + PJC)
                src = (v(prm, i * NB * PRM_W, (1, NB * PRM_W)) if isinstance(i, int)
                       else prm[:, bass.ds(i * (NB * PRM_W), NB * PRM_W)])
                nc.vector.tensor_copy(v(pcur, par * NB * PRM_W, (1, NB * PRM_W)), src).then_inc(pcur_ready, 1)

            def stage_a(i, par, half):
                take_params(i, par)
                uj, ut = pjb("A", i), tpb("A", i)
                for b in range(NB):
                    for ot in range(CT):
                        step = (i * NB + b) * CT * 3 + ot * 3
                        dve.wait_ge(pj_drained, uj + b * 4 + ot * 2 + 2)
                        if b == 1:
                            dve.wait_ge(tp_full, ut + NT)
                        elif not (isinstance(i, int) and i == 0):
                            dve.wait_ge(tp_full, tpb("A", i - 1) + TPA)
                        dst = v(xf, ot * N, (1, N))
                        tap = lambda k: v(xs, ot * (N + 2) + k, (1, N))
                        wt = lambda k: v(small, DWW + ot * 3 + k, (1, 1))
                        nc.vector.tensor_scalar(dst, tap(0), wt(0), None, ALU.mult).then_inc(conv_step, 1)
                        for k in (1, 2):
                            dve.wait_ge(conv_step, step + k)
                            nc.vector.scalar_tensor_tensor(dst, tap(k), wt(k), dst, ALU.mult, ALU.add).then_inc(conv_step, 1)
                    for nt in range(NT):
                        k = b * NT + nt
                        dve.wait_ge(tp_full, ut + k + 1)
                        if k == 0 and not (isinstance(i, int) and i == 0):
                            dve.wait_ge(y_stored, 32 * i)
                        o = nt * H * ROW
                        nc.vector.tensor_copy(v(stage, o + b * P, (ROW, H), (1, P)), v(tp[k % 2], 0, (P, H), (1, P)))
                        nc.vector.tensor_tensor(v(stage, o + NB * P + b, (ROW, H), (NB, K1)), v(tp[k % 2], 2 * P, (K1, H), (1, K1)),
                                                v(small, DBCB, (K1, H), (1, K1)), ALU.add).then_inc(tp_drained, 1)

            HQ = H * Q
            AXO, UO, WO, LO, MO, DO = 0, 32, 64, 96, 128, 192

            def part(h, off):
                return h * NT * ROW + NB * P + off

            def stage_b(i, par, half):
                d = lambda off: v(dts, off, (1, HQ))
                s0 = i * 9
                dve.wait_ge(rows_in, 16 * (i + 1))
                if not (isinstance(i, int) and i == 0):
                    dve.wait_ge(sg_full, i * H)
                for h in range(H):
                    raw = v(xp, part(h, 0), (1, NB), (ROW, NT))
                    last = nc.vector.scalar_tensor_tensor(v(dts, AXO + h * Q, (NT, NB), (1, NT)), raw, -1.0, raw, ALU.mult, ALU.max)
                last.then_inc(sp_v, 1)
                dve.wait_ge(sp_a, i * 2 + 1)
                nc.vector.tensor_scalar(d(WO), d(UO), 1.0, None, ALU.add).then_inc(sp_v, 1)
                dve.wait_ge(sp_v, s0 + 2)
                nc.vector.tensor_scalar(d(MO), d(WO), 1.0, None, ALU.is_equal).then_inc(sp_v, 1)
                dve.wait_ge(sp_v, s0 + 3)
                dve.wait_ge(sp_a, i * 2 + 2)
                nc.vector.tensor_tensor(d(LO), d(LO), d(MO), ALU.add).then_inc(sp_v, 1)
                nc.vector.scalar_tensor_tensor(d(WO), d(WO), -1.0, d(MO), ALU.add, ALU.add).then_inc(sp_v, 1)
                dve.wait_ge(sp_v, s0 + 5)
                nc.vector.reciprocal(d(WO), d(WO)).then_inc(sp_v, 1)
                dve.wait_ge(sp_v, s0 + 6)
                nc.vector.tensor_tensor(d(LO), d(LO), d(WO), ALU.mult).then_inc(sp_v, 1)
                dve.wait_ge(sp_v, s0 + 7)
                nc.vector.tensor_tensor(d(LO), d(LO), d(UO), ALU.mult).then_inc(sp_v, 1)
                dve.wait_ge(sp_v, s0 + 8)
                for h in range(H):
                    last = nc.vector.scalar_tensor_tensor(
                        v(dts, DO + h * Q, (NT, NB), (1, NT)), v(xp, part(h, 0), (1, NB), (ROW, NT)), 0.0,
                        v(dts, LO + h * Q, (NT, NB), (1, NT)), ALU.max, ALU.add)
                last.then_inc(sp_v, 1)
                dve.wait_ge(sp_v, s0 + 9)
                nc.vector.tensor_tensor(v(rseg, 0, (L, HQ), (1, L)), v(dts, DO, (1, HQ), (0, L)),
                                        const("fromstart", (0, HQ), (1, L)), ALU.mult).then_inc(r_ready, 1)
                nc.vector.tensor_tensor(v(rtot, 0, (CPT, HQ), (1, CPT)), v(dts, DO, (1, HQ), (0, CPT)),
                                        const("chunk", (0, HQ), (1, CPT)), ALU.mult).then_inc(r_ready, 1)

                def scans(h, b):
                    hb = i * H * NB + h * NB + b
                    dve.wait_ge(st_full, hb + 1)
                    if h or not (isinstance(i, int) and i == 0):
                        prev = tpb("B", i) + (b + 1) * 4 if h else tpb("B", i - 1) + 8 + (b + 1) * 4
                        dve.wait_ge(tp_full, prev)
                    for s in range(S):
                        nc.vector.tensor_tensor_scan(
                            v(hs, (b * (NC + 1) + 1) * S + s, (S, NC)), v(big, s * EEW + TOT + b * NC, (1, NC)),
                            v(st, s, (S, NC)), 0.0, ALU.mult, ALU.add).then_inc(hs_ready, 1)

                for h in range(H):
                    ih = i * H + h
                    DB, DBE, CS = 0, Q * S, 2 * Q * S
                    for b in range(NB):
                        last = nc.vector.tensor_tensor(
                            v(bc8, DB + b * NT * S, (S, NT), (1, S)), v(xp, part(h, NB + b), (ROW, NT), (NB, S)),
                            v(dts, DO + h * Q + b * NT, (1, NT), (0, S)), ALU.mult)
                    last.then_inc(bc_step, 1)
                    dve.wait_ge(ee_ready, ih + 1)
                    dve.wait_ge(bc_step, ih * 3 + 1)
                    nc.vector.tensor_tensor(v(bc8, DBE, (S, Q), (1, S)), v(bc8, DB, (S, Q), (1, S)),
                                            v(big, SEG + L - 1, (L, Q), (EEW, S)), ALU.mult).then_inc(bc_step, 1)
                    for b in range(NB):
                        last = nc.vector.tensor_tensor(
                            v(bc8, CS + b * NT * S, (S, NT), (1, S)), v(xp, part(h, NB * (1 + S) + b), (ROW, NT), (NB, S)),
                            v(big, CUM + b * NT, (1, NT), (EEW, S)), ALU.mult)
                    last.then_inc(bc_step, 1)
                    if ih is not None and not (isinstance(ih, int) and ih == 0):
                        dve.wait_ge(st_full, ih * NB)
                    dve.wait_ge(bc_step, ih * 3 + 2)
                    nc.vector.tensor_tensor(v(bblk, 0, (CPT * S, Q), (S, CPT), (1, S)), v(bc8, DBE, (S, Q), (0, CPT), (1, S)),
                                            const("chunk", (0, Q), (1, CPT), (0, S)), ALU.mult).then_inc(blk_ready, 1)
                    dve.wait_ge(bc_step, ih * 3 + 3)
                    if h:
                        dve.wait_ge(tp_full, tpb("B", i) + 8)
                    elif not (isinstance(i, int) and i == 0):
                        dve.wait_ge(tp_full, tpb("B", i - 1) + TPB)
                    nc.vector.tensor_tensor(v(cblk, 0, (CPT * S, Q), (S, CPT), (1, S)), v(bc8, CS, (S, Q), (0, CPT), (1, S)),
                                            const("chunk", (0, Q), (1, CPT), (0, S)), ALU.mult).then_inc(blk_ready, 1)
                    scans(h, 0)
                    dve.wait_ge(w_ready, ih + 1)
                    W = v(big, W_OFF, (Q * L, S), (L, Q), (1, L))
                    nc.vector.tensor_tensor(W, W, v(bc8, DB, (1, S), (S, Q), (0, L)), ALU.mult).then_inc(m_step, 1)
                    scans(h, 1)
                    dve.wait_ge(m_step, ih * 3 + 1)
                    nc.vector.tensor_reduce(m16[:, :], v(big, W_OFF, (1, Q * L), (Q * L, S)), AX.X, ALU.add).then_inc(m_step, 1)
                    dve.wait_ge(m_step, ih * 3 + 2)
                    nc.vector.scalar_tensor_tensor(v(m16, 0, (L, Q), (1, L)), const("diag", (0, Q), (1, L)),
                                                   v(small, DPAR + h, (1, 1)), v(m16, 0, (L, Q), (1, L)),
                                                   ALU.mult, ALU.add).then_inc(m_step, 1)
                    dve.wait_ge(m_step, ih * 3 + 3)
                    wait(dve, ch_used, ih * 8)
                    nc.vector.tensor_tensor(v(mblk, 0, (P, Q), (L, CPT), (1, L)), v(m16, 0, (L, Q), (0, CPT), (1, L)),
                                            const("causal", (0, Q), (L, CPT), (1, L)), ALU.mult).then_inc(mblk_ready, 1)
                    for k in range(8):
                        u = h * 8 + k
                        dve.wait_ge(tp_full, tpb("B", i) + u + 1)
                        if u >= 2 or not (isinstance(i, int) and i == 0):
                            dve.wait_ge(ch_used, i * 16 + u - 1)
                        nc.vector.tensor_copy(v(ch, (u % 2) * 2 * P, (1, 2 * P)), v(tp[u % 2], 0, (1, 2 * P))).then_inc(tp_drained, 1)

            def stage_c(i, par, half):
                uj, ut = pjb("C", i), tpb("C", i)

                def gated(b):
                    for h in range(H):
                        dve.wait_ge(g_ready, i * NB * CT + b * CT + h + 1)
                        for nq in range(2):
                            k = (b * H + h) * 2 + nq
                            dve.wait_ge(tp_full, ut + k + 1)
                            o = (b * CT + h) * N + nq * HALF
                            nc.vector.tensor_tensor(v(gt, o, (1, HALF)), v(tp[k % 2], 0, (1, HALF)), v(gt, o, (1, HALF)),
                                                    ALU.mult).then_inc(tp_drained, 1)
                            dve.wait_ge(tp_drained, ut + k + 1)
                            dve.wait_ge(pj_drained, uj + b * 8 + 4 + h * 2 + nq + 1)
                            nc.vector.tensor_tensor(v(gt, o, (1, HALF)), v(gt, o, (1, HALF)), v(rs, o, (1, HALF)),
                                                    ALU.add).then_inc(z_ready, 1)

                def output(b):
                    dve.wait_ge(x1_ready, i * NB + b + 1)
                    for ot in range(CT):
                        dve.wait_ge(pj_drained, uj + 16 + b * 4 + ot * 2 + 2)
                        nc.vector.tensor_tensor(x_view(par, b, ot), x_view(par, b, ot), v(rs, (b * CT + ot) * N, (1, N)),
                                                ALU.add).then_inc(out_ready, 1)

                gated(0)
                gated(1)
                output(0)
                output(1)

            phases(dve, stage_a, stage_b, stage_c)

        @block.tensor
        def _(pe):
            U = CT * B
            MEAN, T = 1024, 1024 + 2 * U
            pe.wait_ge(weights_in, WEIGHTS + 16)
            pe.wait_ge(setup_v, V_STATS)
            nc.tensor.matmul(v(tp[0], 0, (1, 2 * U)), const("group"), v(rs, MEAN, (1, 2 * U)), start=True, stop=True).then_inc(setup_p, 1)
            pe.wait_ge(setup_v, V_Y)
            for ct in range(CT):
                nc.tensor.matmul(v(tp[1], 0, (1, 136), parts=B), v(rs, T + ct * B, (1, B)), v(xp, ct * 136, (1, 136)), start=(ct == 0), stop=False)
            nc.tensor.matmul(v(tp[1], 0, (1, 136), parts=B), const("ones", (1, B), parts=1), v(xp, 272, (1, 136), parts=1),
                             start=False, stop=True).then_inc(setup_p, 1)
            pe.wait_ge(setup_v, V_HID)
            ident16 = const("ident", (1, B), parts=B)
            nc.tensor.transpose(v(tp[0], 0, (1, B)), v(bc8, 8, (1, P), parts=B), ident16)
            nc.tensor.transpose(v(tp[0], P, (1, B), parts=E), v(bc8, 0, (1, E), parts=B), ident16).then_inc(setup_p, 1)
            pe.wait_ge(setup_v, V_HIDT)
            for ct in range(CT):
                o = v(tp[1], ct * B, (1, B))
                nc.tensor.matmul(o, v(xp, 408 + ct * P, (1, P)), v(bc8, 160, (1, B)), start=True, stop=False)
                last = nc.tensor.matmul(o, v(xp, 664 + ct * P, (1, P), parts=E), v(bc8, 180, (1, B), parts=E), start=False, stop=True)
            last.then_inc(setup_p, 1)
            pe.wait_ge(setup_v, V_STATS2)
            nc.tensor.matmul(v(tp[0], 0, (1, 2 * U)), const("group"), v(rs, MEAN, (1, 2 * U)), start=True, stop=True).then_inc(setup_p, 1)
            pe.wait_ge(setup_v, V_Q)
            for ot in range(6):
                for ct in range(CT):
                    last = nc.tensor.matmul(v(tp[1], ot * B, (1, B)), v(inw, ct * 3 * C + ot * P, (1, P)),
                                            v(rs, T + ct * B, (1, B)), start=(ct == 0), stop=(ct == CT - 1))
            last.then_inc(setup_p, 1)
            pe.wait_ge(params_ready, 1)

            def pj_slot(u, k):
                wait(pe, pj_drained, u + k - 3)
                return pj[k % 4]

            def tp_slot(u, k):
                wait(pe, tp_drained, u + k - 1)
                return tp[k % 2]

            def stage_a(i, par, half):
                uj, ut = pjb("A", i), tpb("A", i)
                pe.wait_ge(x_in[par], 16 * (PH // 2 + half + 1))
                k = 0
                for b in range(NB):
                    pe.wait_ge(wa_ready, i * NB + b + 1)
                    for ot in range(CT):
                        for nt in range(2):
                            o = pj_slot(uj, k)
                            for ct in range(CT):
                                last = nc.tensor.matmul(o[:, :], v(wa, (b * CT + ct) * C + ot * P, (1, P)),
                                                        x_view(par, b, ct, nt * HALF, HALF), start=(ct == 0), stop=(ct == CT - 1))
                            last.then_inc(pj_full, 1)
                            k += 1
                for b in range(NB):
                    pe.wait_ge(xf_ready, (i * NB + b + 1) * CT)
                    for nt in range(NT):
                        o = tp_slot(ut, b * NT + nt)
                        tile = lambda ct: v(xf, ct * N + nt * P, (1, P))
                        for ct in range(CT):
                            nc.tensor.transpose(v(o, ct * P, (1, P)), tile(ct), const("ident"))
                        for ct in range(CT):
                            last = nc.tensor.matmul(v(o, 2 * P, (1, H * K1)), tile(ct), v(dbcw, ct * H * K1, (1, H * K1)),
                                                    start=(ct == 0), stop=(ct == CT - 1))
                        last.then_inc(tp_full, 1)

            def stage_b(i, par, half):
                uj, ut = pjb("B", i), tpb("B", i)

                def segments(h):
                    wait(pe, ee_ready, i * H + h)
                    nc.tensor.matmul(v(sg, SEG, (1, Q * L)), const("after"), v(rseg, h * Q * L, (1, Q * L)), start=True, stop=True)
                    nc.tensor.matmul(v(sg, CUM, (1, Q)), const("upto"), v(dts, 192 + h * Q, (1, Q)), start=True, stop=True)
                    nc.tensor.matmul(v(sg, TOT, (1, Q * CPT)), const("ones"), v(rtot, h * Q * CPT, (1, Q * CPT)),
                                     start=True, stop=True).then_inc(sg_full, 1)

                def rows(h, b, g):
                    return v(xp, (h * NT + g) * ROW + b * P, (1, P))

                def chunk_sums(h, b):
                    hb = (i * H + h) * NB + b
                    wait(pe, hs_ready, hb * S)
                    pe.wait_ge(blk_ready, (i * H + h) * 2 + 1)
                    for g in range(NT):
                        last = nc.tensor.matmul(v(st, g * CPT * S, (1, CPT * S)), rows(h, b, g),
                                                v(bblk, (b * NT + g) * CPT * S, (1, CPT * S)), start=True, stop=True)
                    last.then_inc(st_full, 1)

                def turn(h, b, gp):
                    k = (h * NB + b) * 4 + gp
                    o = tp_slot(ut, k)
                    if gp == 0:
                        pe.wait_ge(blk_ready, (i * H + h) * 2 + 2)
                        pe.wait_ge(hs_ready, ((i * H + h) * NB + b + 1) * S)
                    nc.tensor.transpose(v(o, 0, (1, P)), v(cblk, (b * NT + 2 * gp) * CPT * S, (1, P)), const("ident"))
                    nc.tensor.transpose(v(o, P, (1, P)), v(hs, (b * (NC + 1) + 2 * gp * CPT) * S, (1, P)), const("ident")).then_inc(tp_full, 1)

                def results(h, b, gp):
                    u = (h * NB + b) * 4 + gp
                    k = (h * NB + b) * 2
                    if gp == 0:
                        pj_slot(uj, k + 1)
                    pe.wait_ge(mblk_ready, i * H + h + 1)
                    pe.wait_ge(tp_drained, ut + u + 1)
                    for e in range(2):
                        g = 2 * gp + e
                        d = v(pj[(k + e) % 4], gp * P, (1, P))
                        nc.tensor.matmul(d, v(mblk, (b * NT + g) * P, (1, P)), rows(h, b, g), start=True, stop=False)
                        half_rows = dict(parts=64, p0=64 * e)
                        last = nc.tensor.matmul(d, v(ch, (u % 2) * 2 * P, (1, P), **half_rows),
                                                v(ch, (u % 2) * 2 * P + P, (1, P), **half_rows), start=False, stop=True)
                    last.then_inc(ch_used, 1)

                pe.wait_ge(r_ready, i * 2 + 2)
                segments(0)
                chunk_sums(0, 0)
                segments(1)
                chunk_sums(0, 1)
                for h in range(H):
                    if h:
                        chunk_sums(h, 0)
                        chunk_sums(h, 1)
                    order = [(b, gp) for b in range(NB) for gp in range(4)]
                    turn(h, *order[0])
                    for n, (b, gp) in enumerate(order):
                        if n + 1 < len(order):
                            turn(h, *order[n + 1])
                        results(h, b, gp)

            def stage_c(i, par, half):
                uj, ut = pjb("C", i), tpb("C", i)

                def gate_and_residual(b):
                    pe.wait_ge(wc_ready, i * NB + b + 1)
                    for k in range(8):
                        ot = (k // 2 + 2) % 4
                        o = pj_slot(uj, b * 8 + k)
                        for ct in range(CT):
                            last = nc.tensor.matmul(o[:, :], v(wc, (b * CT + ct) * 2 * C + ot * P, (1, P)),
                                                    x_view(par, b, ct, (k % 2) * HALF, HALF), start=(ct == 0), stop=(ct == CT - 1))
                        last.then_inc(pj_full, 1)

                def turn_back(b):
                    for h in range(H):
                        for nq in range(2):
                            k = (b * H + h) * 2 + nq
                            o = tp_slot(ut, k)
                            for e in range(4):
                                last = nc.tensor.transpose(v(o, e * P, (1, P)), v(big, (h * NT + nq * 4 + e) * NB * P + b * P, (1, P)), const("ident"))
                            last.then_inc(tp_full, 1)

                def output(b):
                    pe.wait_ge(z_ready, (i * NB + b + 1) * 4)
                    for k in range(4):
                        o = pj_slot(uj, 16 + b * 4 + k)
                        for h in range(CT):
                            last = nc.tensor.matmul(o[:, :], v(outw, h * C + (k // 2) * P, (1, P)),
                                                    v(gt, (b * CT + h) * N + (k % 2) * HALF, (1, HALF)), start=(h == 0), stop=(h == CT - 1))
                        last.then_inc(pj_full, 1)

                for b in range(NB):
                    gate_and_residual(b)
                pe.wait_ge(y_gathered, 256 * (i + 1))
                for b in range(NB):
                    turn_back(b)
                for b in range(NB):
                    output(b)

            phases(pe, stage_a, stage_b, stage_c)


V_MOB = 6
V_STATS = 61
V_VAR1 = 65
V_Y = 68
V_MAX = 71
V_HID = 74
V_HIDT = 75
V_STATS2 = 89
V_VAR2 = 93
V_Q = 96
P_EXPERT = 4


def kernel(**inputs):
    import concourse.bacc as _bacc
    from concourse.bass_utils import run_bass_kernel_spmd as _run

    w = {k: np.ascontiguousarray(np.asarray(a)) for k, a in inputs.items()}
    L1, L0 = "L1_conv_", "L0_conv_"

    def by_tile(a):
        return np.ascontiguousarray(a.reshape(-1, P, a.shape[-1]).transpose(1, 0, 2))

    def column(a):
        return np.ascontiguousarray(a.reshape(-1, P).T)

    table, grid = constants()
    w1 = w[L0 + "W1"].reshape(E * R, C).T
    arrays = dict(
        x=w["x"].reshape(B, C, N),
        w1g=by_tile(np.concatenate([w[L0 + "Wg"].T, w1], 1)),
        b1g=np.concatenate([w[L0 + "bg"], w[L0 + "b1"].reshape(-1)])[None],
        w2=np.ascontiguousarray(w[L0 + "W2"].transpose(0, 2, 1).reshape(E * R, C)),
        b2=w[L0 + "b2"],
        inw=by_tile(w[L1 + "in_proj_w"].T),
        inb=column(w[L1 + "in_proj_b"]),
        dww=np.ascontiguousarray(w[L1 + "dw_w"].reshape(CT, P, 3).transpose(1, 0, 2).reshape(P, 6)),
        dwb=column(w[L1 + "dw_b"]),
        dbcw=by_tile(w[L1 + "dbc_w"].T),
        dbcb=w[L1 + "dbc_b"][None],
        alog=w[L1 + "A_log"].reshape(1, H * S),
        dpar=w[L1 + "Dparam"][None],
        mob=w[L1 + "mobius"].reshape(1, 4 * H),
        outw=by_tile(w[L1 + "out_proj_w"].T),
        outb=column(w[L1 + "out_proj_b"]),
        const=table, grid=grid)
    nc = _bacc.Bacc("TRN2", target_bir_lowering=False, num_devices=1)
    feeds, args = {}, []
    for name, a in arrays.items():
        a = np.ascontiguousarray(a)
        feeds[f"in_{name}"] = a
        args.append(nc.dram_tensor(f"in_{name}", a.shape, mybir.dt.from_np(a.dtype), kind="ExternalInput").ap())
    out = nc.dram_tensor("out_0", (B, C, N), F32, kind="ExternalOutput").ap()
    build(nc, *args, out)
    r = _run(nc, [feeds], core_ids=[0])
    return r.results[0]["out_0"].reshape(B, C, IMG, IMG)
```

```python
import numpy as np
from contextlib import ExitStack

import concourse.bass as bass
from concourse import mybir

F32 = mybir.dt.float32
U32 = mybir.dt.uint32
ALU = mybir.AluOpType
ACT = mybir.ActivationFunctionType
AX = mybir.AxisListType

P = 128
B, C, IMG = 16, 256, 32
N = IMG * IMG
CT = C // P
H, S = 2, 8
E, R = 8, 16
NB = 2
PH = B // NB
NT = N // P
L = 16
CPT = P // L
NC = N // L
K1 = 1 + 2 * S
ROW = NB * (P + K1)
Q = NB * NT
HALF = 512
EPS = 1e-5

SEG, CUM, TOT = 0, Q * L, Q * L + Q
EEW = TOT + Q * CPT

CONST_WIDTHS = dict(ident=P, after=P, upto=P, ones=P, group=P, before=P, notbefore=P,
                    fromstart=L, chunk=CPT, causal=P, diag=L, gridcol=2 * NT)
CONST_AT = {}
_at = 0
for _name, _width in CONST_WIDTHS.items():
    CONST_AT[_name] = _at
    _at += _width
CONST_W = _at

PRM_P, PRM_A, PRM_B, PRM_BIAS, PRM_W = 0, 2, 4, 6, 12


def constants():
    r, c = np.arange(P)[:, None], np.arange(P)[None, :]
    same = (r // L) == (c // L)
    lin = np.linspace(-1.0, 1.0, IMG).astype(np.float32)
    gy, gx = (v.reshape(-1) for v in np.meshgrid(lin, lin, indexing="ij"))
    part = dict(
        ident=r == c, after=same & (r > c), upto=same & (r <= c), ones=np.ones((P, P)),
        group=((r // 8) == (c // 8)) / 8.0, before=c < r, notbefore=c >= r,
        fromstart=(r % L) <= c[:, :L], chunk=(r // L) == c[:, :CPT], causal=same & (c >= r),
        diag=(r % L) == c[:, :L],
        gridcol=np.concatenate([gx.reshape(NT, P).T, gy.reshape(NT, P).T], 1))
    table = np.concatenate([part[k].astype(np.float32) for k in CONST_WIDTHS], 1)
    return np.ascontiguousarray(table)


def build(nc, x_d, w1g_d, b1g_d, w2_d, b2_d, inw_d, inb_d, dww_d, dwb_d, dbcw_d, dbcb_d, alog_d,
          dpar_d, mob_d, outw_d, outb_d, const_d, out_d):
    with ExitStack() as ctx:
        def sb(name, width, dt=F32):
            return ctx.enter_context(nc.sbuf_tensor(name, [P, width], dt))

        def sem(name):
            return ctx.enter_context(nc.semaphore(name))

        def v(tensor, off, *dims, parts=P, p0=0):
            width = tensor.shape[1]
            assert off + sum(st_ * (n_ - 1) for st_, n_ in dims) < width if isinstance(off, int) else True, (tensor.name, off, dims)
            return bass.AP(tensor, p0 * width + off, [[width, parts]] + [list(d) for d in dims])

        xt_d = nc.dram_tensor("xt_scratch", [H * N, ROW], F32)
        yt_d = nc.dram_tensor("yt_scratch", [H * N, NB * P], F32)
        cd_d = nc.dram_tensor("cd_scratch", [H * N, S * NB], F32)

        cst = sb("cst", CONST_W)
        inw = sb("inw", CT * 3 * C)
        outw = sb("outw", CT * C)
        dbcw = sb("dbcw", CT * H * K1)
        small = sb("small", 96)
        xb = [sb("xb0", NB * CT * N), sb("xb1", NB * CT * N)]
        wsc = sb("wsc", NB * CT * 2 * C)
        xs = sb("xs", CT * (N + 2))
        xf = sb("xf", CT * N)
        stage = sb("stage", NT * H * ROW)
        xp = sb("xp", H * NT * ROW)
        crow = sb("crow", H * NT * L * S * NB)
        big = sb("big", S * EEW + S * Q * L)
        mblk = sb("mblk", Q * P)
        bblk = sb("bblk", Q * CPT * S)
        cblk = sb("cblk", Q * CPT * S)
        m16 = sb("m16", Q * L)
        rseg = sb("rseg", H * Q * L)
        rtot = sb("rtot", H * Q * CPT)
        dts = sb("dts", 8 * H * Q)
        bc8 = sb("bc8", 3 * Q * S)
        hs = sb("hs", NB * (NC + 1) * S)
        ch = sb("ch", 4 * 2 * P)
        gt = sb("gt", NB * CT * N)
        rs = sb("rs", NB * CT * N)
        prm = sb("prm", B * PRM_W)
        pcur = sb("pcur", 2 * NB * PRM_W)
        idx = sb("idx", H * NT, U32)
        W_OFF = S * EEW

        INB, DWW, DWB, OUTB, DBCB, ANEG, DPAR, MOB = 0, 6, 12, 14, 16, 50, 66, 68

        pj = [ctx.enter_context(nc.psum_tensor(f"pj{i}", [P, HALF], F32)) for i in range(4)]
        tp = [ctx.enter_context(nc.psum_tensor(f"tp{i}", [P, HALF], F32)) for i in range(2)]
        sg = ctx.enter_context(nc.psum_tensor("sg", [P, HALF], F32))
        st = ctx.enter_context(nc.psum_tensor("st", [P, HALF], F32))

        def const(name, *dims, off=0, parts=P):
            width = CONST_WIDTHS[name]
            return v(cst, CONST_AT[name] + off, *(dims or ((1, width),)), parts=parts)

        weights_in = sem("weights_in")
        x_in = [[sem(f"x_in{par}{b}") for b in range(NB)] for par in range(2)]
        out_stored = [[sem(f"out_stored{par}{b}") for b in range(NB)] for par in range(2)]
        rows_scattered = sem("rows_scattered")
        rows_in = sem("rows_in")
        c_stored = sem("c_stored")
        crow_in = [sem(f"crow_in{h}") for h in range(H)]
        y_stored = [sem(f"y_stored{h}") for h in range(H)]
        y_gathered = [sem(f"y_gathered{h}") for h in range(H)]
        stats_done = sem("stats_done")
        stats_done_a = sem("stats_done_a")
        setup_v = sem("setup_v")
        setup_a = sem("setup_a")
        setup_p = sem("setup_p")
        setup_g = sem("setup_g")
        params_ready = sem("params_ready")
        pcur_ready = sem("pcur_ready")
        wa_ready = sem("wa_ready")
        wg_ready = sem("wg_ready")
        wr_ready = sem("wr_ready")
        a_full, a_drained = sem("a_full"), sem("a_drained")
        g_full, g_drained = sem("g_full"), sem("g_drained")
        e_full, e_drained = sem("e_full"), sem("e_drained")
        o_full, o_drained = sem("o_full"), sem("o_drained")
        r_drained = sem("r_drained")
        x_full, x_drained = sem("x_full"), sem("x_drained")
        t_full, t_drained = sem("t_full"), sem("t_drained")
        y_full, y_drained = sem("y_full"), sem("y_drained")
        stage_ready = sem("stage_ready")
        conv_step = [sem(f"conv_step{ct}") for ct in range(CT)]
        xf_ready = sem("xf_ready")
        sp_v = sem("sp_v")
        sp_a = sem("sp_a")
        r_ready = sem("r_ready")
        sg_full = sem("sg_full")
        ee_ready = sem("ee_ready")
        w_ready = sem("w_ready")
        bc_step = sem("bc_step")
        blk_ready = sem("blk_ready")
        m_step = sem("m_step")
        mblk_ready = sem("mblk_ready")
        st_full = sem("st_full")
        hs_ready = sem("hs_ready")
        ch_used = sem("ch_used")
        g_ready = sem("g_ready")
        z_ready = sem("z_ready")
        x1_ready = sem("x1_ready")
        out_ready = sem("out_ready")
        pool_passed = sem("pool_passed")

        A_U, R_U, G_U, E_U, O_U = NB * 4, H * NB * 2, NB * 4, NB * 4, NB * 4
        X_U, T_U, Y_U = NB * NT, H * NB * NT // 2, NB * H * 2
        CH = 4
        AHEAD = 2

        def wait(eng, semaphore, value):
            if isinstance(value, int) and value <= 0:
                return
            eng.wait_ge(semaphore, value)

        def first(i):
            return isinstance(i, int) and i == 0

        def last_phase(i):
            return isinstance(i, int) and i == PH - 1

        def phases(eng, cycle):
            cycle(0, 0, 0)
            with eng.Fori(0, (PH - 2) // 2) as t:
                cycle(t * 2 + 1, 1, t)
                cycle(t * 2 + 2, 0, t + 1)
            cycle(PH - 1, 1, PH // 2 - 1)

        def x_view(par, b, ct, off=0, n=N):
            return v(xb[par], (b * CT + ct) * N + off, (1, n))

        x_dram = x_d.rearrange("b (t p) n -> p b t n", p=P)
        out_dram = out_d.rearrange("b (t p) n -> p b t n", p=P)
        block = ctx.enter_context(nc.Block())

        @block.sync
        def _(sp):
            def bcast(src, n):
                return bass.AP(src.tensor, 0, [[0, P], [1, n]])

            def load_x(i, par, b):
                at = i * NB + b
                src = x_dram[:, at:at + 1] if isinstance(at, int) else x_dram[:, bass.ds(at, 1)]
                sp.dma_start(v(xb[par], b * CT * N, (CT * N, 1), (N, CT), (1, N)), src).then_inc(x_in[par][b], 16)

            sp.dma_start(cst[:, :], const_d).then_inc(weights_in, 16)
            sp.dma_start(v(small, MOB, (1, 8)), bcast(mob_d, 8)).then_inc(weights_in, 16)
            for b in range(NB):
                load_x(0, 0, b)
            sp.dma_start(v(small, ANEG, (1, 16)), bcast(alog_d, 16)).then_inc(weights_in, 16)
            sp.dma_start(v(small, DPAR, (1, 2)), bcast(dpar_d, 2)).then_inc(weights_in, 16)
            sp.dma_start(v(small, DBCB, (1, H * K1)), bcast(dbcb_d, H * K1)).then_inc(weights_in, 16)
            sp.dma_start(v(small, INB, (1, 6)), inb_d).then_inc(weights_in, 16)
            sp.dma_start(v(small, DWW, (1, 6)), dww_d).then_inc(weights_in, 16)
            sp.dma_start(v(small, DWB, (1, 2)), dwb_d).then_inc(weights_in, 16)
            sp.dma_start(v(small, OUTB, (1, 2)), outb_d).then_inc(weights_in, 16)
            for b in range(NB):
                load_x(1, 1, b)
            sp.dma_start(v(inw, 0, (3 * C, CT), (1, 3 * C)), inw_d).then_inc(weights_in, 16)
            sp.dma_start(v(outw, 0, (C, CT), (1, C)), outw_d).then_inc(weights_in, 16)
            sp.dma_start(v(dbcw, 0, (H * K1, CT), (1, H * K1)), dbcw_d).then_inc(weights_in, 16)
            sp.dma_start(v(xp, 0, (136, CT), (1, 136)), w1g_d).then_inc(weights_in, 16)
            sp.dma_start(v(xp, 272, (1, 136), parts=1), b1g_d).then_inc(weights_in, 16)
            sp.dma_start(v(xp, 408, (1, C)), w2_d).then_inc(weights_in, 16)
            sp.dma_start(v(xp, 664, (1, C), parts=E), b2_d).then_inc(weights_in, 16)
            for i in range(2, PH + 2):
                sp.wait_ge(stats_done, i - 1)
                sp.wait_ge(stats_done_a, i - 1)
                for b in range(NB):
                    load_x(i % PH, i % 2, b)

            def load_rows(i):
                sp.wait_ge(rows_scattered, 256 * (i + 1))
                if first(i):
                    sp.wait_ge(params_ready, 1)
                else:
                    sp.wait_ge(ch_used, T_U * i)
                sp.dma_start(v(xp, 0, (ROW, H * NT), (1, ROW)),
                             bass.AP(xt_d, 0, [[ROW, P], [P * ROW, H * NT], [1, ROW]])).then_inc(rows_in, 16)

            def store_c(i):
                sp.wait_ge(rows_in, 16 * (i + 1))
                sp.dma_start(bass.AP(cd_d, 0, [[S * NB, P], [P * S * NB, H * NT], [1, S * NB]]),
                             v(xp, NB * (P + 1 + S), (ROW, H * NT), (1, S * NB))).then_inc(c_stored, 16)

            def load_c(i):
                sp.wait_ge(c_stored, 16 * (i + 1))
                run = L * S * NB
                for h in range(H):
                    for c in range(CPT):
                        sp.dma_start(v(crow, h * NT * run, (run, NT), (1, run), parts=L, p0=c * L),
                                     bass.AP(cd_d, (h * NT * CPT + c) * run, [[0, L], [CPT * run, NT], [1, run]])).then_inc(crow_in[h], 16)

            def store_out(i, par, b):
                sp.wait_ge(out_ready, (i * NB + b + 1) * CT)
                at = i * NB + b
                dst = out_dram[:, at:at + 1] if isinstance(at, int) else out_dram[:, bass.ds(at, 1)]
                sp.dma_start(dst, v(xb[par], b * CT * N, (CT * N, 1), (N, CT), (1, N))).then_inc(out_stored[par][b], 16)

            def cycle(i, par, half, more):
                for h in range(H):
                    sp.wait_ge(r_drained, i * R_U + (h + 1) * 4)
                    sp.dma_start(bass.AP(yt_d, h * N * NB * P, [[NB * P, P], [P * NB * P, NT], [1, NB * P]]),
                                 v(rs, h * NT * NB * P, (NB * P, NT), (1, NB * P))).then_inc(y_stored[h], 16)
                if not last_phase(i):
                    load_rows(i + 1)
                    store_c(i + 1)
                store_out(i, par, 0)
                if not last_phase(i):
                    load_c(i + 1)
                store_out(i, par, 1)
                if more:
                    for b in range(NB):
                        sp.wait_ge(out_stored[par][b], 16 * (half + 1))
                        load_x(i + 2, par, b)

            load_rows(0)
            store_c(0)
            load_c(0)
            cycle(0, 0, 0, True)
            with sp.Fori(0, (PH - 4) // 2) as t:
                cycle(t * 2 + 1, 1, t, True)
                cycle(t * 2 + 2, 0, t + 1, True)
            for i in range(PH - 3, PH):
                cycle(i, i % 2, i // 2, i < PH - 2)
            for par in range(2):
                for b in range(NB):
                    sp.wait_ge(out_stored[par][b], 16 * (PH // 2))

        @block.gpsimd
        def _(pool):
            pool.wait_ge(params_ready, 1)

            def hold(semaphore, value):
                if isinstance(value, int) and value <= 0:
                    return
                pool.wait_ge(semaphore, value)
                pool.sem_inc(pool_passed, 1)

            def scaled(par, b, slot, col, ready):
                for ct in range(CT):
                    last = nc.gpsimd.tensor_scalar(v(wsc, (b * CT + ct) * 2 * C + slot * C, (1, C)), v(inw, ct * 3 * C + col, (1, C)),
                                                   v(pcur, (par * NB + b) * PRM_W + PRM_P + ct, (1, 1)), 0.0,
                                                   ALU.mult, ALU.add)
                last.then_inc(ready, 1)

            def weights_x(i, par, b):
                if not first(i):
                    hold(g_full, (i - 1) * G_U + (b + 1) * 4)
                scaled(par, b, 0, 0, wa_ready)

            def weights_gate(i, par, b):
                hold(a_full, i * A_U + (b + 1) * 4)
                scaled(par, b, 0, 2 * C, wg_ready)

            def weights_residual(i, par):
                hold(e_full, i * E_U)
                for b in range(NB):
                    scaled(par, b, 1, C, wr_ready)

            def scatter(i, tiles):
                for nt in tiles:
                    hold(stage_ready, i * NT + nt + 1)
                    if nt == 0:
                        hold(rows_in, 16 * i)
                    for h in range(H):
                        k = h * NT + nt
                        pool.indirect_dma_start(
                            out=xt_d.ap(), out_offset=bass.IndirectOffsetOnAxis(ap=idx[:, k:k + 1], axis=0),
                            in_=v(stage, (nt * H + h) * ROW, (1, ROW)), in_offset=None).then_inc(rows_scattered, 16)

            def gather(i, h):
                hold(y_stored[h], 16 * (i + 1))
                if h == 0:
                    hold(mblk_ready, H * (i + 1))
                    hold(hs_ready, H * NB * S * (i + 1))
                for nt in range(NT):
                    k = h * NT + nt
                    pool.indirect_dma_start(
                        out=v(big, k * NB * P, (1, NB * P)), out_offset=None, in_=yt_d.ap()[0:(h + 1) * N],
                        in_offset=bass.IndirectOffsetOnAxis(ap=idx[:, k:k + 1], axis=0)).then_inc(y_gathered[h], 16)

            def weigh(i, h):
                hold(ee_ready, i * H + h + 1)
                hold(crow_in[h], 16 * CPT * (i + 1))
                hold(m_step, (i * H + h) * 3)
                for s in range(S):
                    for b in range(NB):
                        last = nc.gpsimd.tensor_tensor(
                            v(big, W_OFF + (s * Q + b * NT) * L, (L, NT), (1, L)),
                            v(big, s * EEW + SEG + b * NT * L, (L, NT), (1, L)),
                            v(crow, h * NT * L * S * NB + s * NB + b, (L * S * NB, NT), (S * NB, L)), ALU.mult)
                last.then_inc(w_ready, 1)

            def first_tap(i, b):
                for ot in range(CT):
                    hold(a_drained, i * A_U + b * 4 + ot * 2 + 2)
                    hold(x_full, (i * NB + b) * NT)
                    nc.gpsimd.tensor_scalar(v(xf, ot * N, (1, N)), v(xs, ot * (N + 2), (1, N)), v(small, DWW + ot * 3, (1, 1)), 0.0,
                                            ALU.mult, ALU.add).then_inc(conv_step[ot], 1)

            def cycle(i, par, half):
                more = not last_phase(i)
                if more:
                    hold(pcur_ready, i + 2)
                    weights_x(i + 1, 1 - par, 0)
                weigh(i, 0)
                if more:
                    weights_x(i + 1, 1 - par, 1)
                weights_residual(i, par)
                if more:
                    first_tap(i + 1, 0)
                weigh(i, 1)
                if more:
                    weights_gate(i + 1, 1 - par, 0)
                    weights_gate(i + 1, 1 - par, 1)
                    first_tap(i + 1, 1)
                gather(i, 0)
                if more:
                    scatter(i + 1, range(0, 2))
                gather(i, 1)
                if more:
                    scatter(i + 1, range(2, NT))

            hold(pcur_ready, 1)
            for b in range(NB):
                weights_x(0, 0, b)
            for b in range(NB):
                first_tap(0, b)
            for b in range(NB):
                weights_gate(0, 0, b)
            scatter(0, range(NT))
            phases(pool, cycle)

        @block.scalar
        def _(act):
            def did(ins):
                ins.then_inc(setup_a, 1)

            act.wait_ge(weights_in, 16 * 16)
            did(nc.scalar.activation(v(small, ANEG, (1, 16)), v(small, ANEG, (1, 16)), ACT.Exp))
            act.wait_ge(setup_v, V_MOB)
            did(nc.scalar.activation(v(small, MOB + 10, (1, 2)), v(small, MOB + 8, (1, 2)), ACT.Sqrt))
            act.wait_ge(setup_g, 1)
            for k in range(4):
                last = nc.scalar.copy(v(crow, k * HALF, (1, HALF)), pj[k][:, :])
            did(last)
            for i in range(PH):
                act.wait_ge(x_in[i % 2][1], 16 * (i // 2 + 1))
                if i:
                    act.wait_ge(stats_done_a, i)
                src = x_view(i % 2, 1, 1)
                nc.scalar.activation(v(gt, 0, (1, N)), src, ACT.Identity, accum_out=v(rs, 400 + i, (1, 1)))
                nc.scalar.activation(v(gt, N, (1, N)), src, ACT.Square, accum_out=v(rs, 408 + i, (1, 1))).then_inc(stats_done_a, 1)
            act.wait_ge(setup_v, V_VAR1)
            did(nc.scalar.activation(v(dts, 0, (1, 32)), v(dts, 0, (1, 32)), ACT.Sqrt))
            act.wait_ge(setup_v, V_MAX)
            did(nc.scalar.activation(v(bc8, 0, (1, E), parts=B), v(bc8, 0, (1, E), parts=B), ACT.Exp,
                                     bias=v(bc8, 140, (1, 1), parts=B), accum_out=v(bc8, 141, (1, 1), parts=B)))
            act.wait_ge(setup_p, P_EXPERT)
            did(nc.scalar.activation(v(dts, 96, (1, 32)), v(tp[1], 0, (1, 32)), ACT.Exp, scale=-1.0))
            act.wait_ge(setup_v, V_VAR2)
            did(nc.scalar.activation(v(dts, 0, (1, 32)), v(dts, 0, (1, 32)), ACT.Sqrt))
            act.wait_ge(params_ready, 1)

            def bias(par, b, ot):
                return v(pcur, (par * NB + b) * PRM_W + PRM_BIAS + ot, (1, 1))

            def project(i, par, b, ot):
                act.wait_ge(pcur_ready, i + 1)
                if b or not first(i):
                    act.wait_ge(conv_step[ot], (i * NB + b) * 3)
                for nt in range(2):
                    k = b * 4 + ot * 2 + nt
                    act.wait_ge(a_full, i * A_U + k + 1)
                    nc.scalar.activation(v(xs, ot * (N + 2) + 1 + nt * HALF, (1, HALF)), pj[k % 4][:, :], ACT.Silu,
                                         bias=bias(par, b, ot)).then_inc(a_drained, 1)

            def convolved(i, b):
                for ot in range(CT):
                    act.wait_ge(conv_step[ot], (i * NB + b + 1) * 3)
                    nc.scalar.activation(v(xf, ot * N, (1, N)), v(xf, ot * N, (1, N)), ACT.Silu,
                                         bias=v(small, DWB + ot, (1, 1))).then_inc(xf_ready, 1)

            def softplus(i):
                act.wait_ge(sp_v, i * 9 + 1)
                nc.scalar.activation(v(dts, 32, (1, 32)), v(dts, 0, (1, 32)), ACT.Exp, scale=-1.0).then_inc(sp_a, 1)
                act.wait_ge(sp_v, i * 9 + 2)
                nc.scalar.activation(v(dts, 96, (1, 32)), v(dts, 64, (1, 32)), ACT.Ln).then_inc(sp_a, 1)

            def decays(i, h):
                act.wait_ge(sg_full, i * H + h + 1)
                if h == 0:
                    wait(act, y_full, i * Y_U)
                else:
                    act.wait_ge(w_ready, i * H + h)
                    act.wait_ge(hs_ready, (i * H + h) * NB * S)
                for s in range(S):
                    last = nc.scalar.activation(v(big, s * EEW, (1, EEW)), v(sg, 0, (1, EEW)), ACT.Exp,
                                                scale=v(small, ANEG + h * S + s, (1, 1)))
                last.then_inc(ee_ready, 1)

            def rows_out(i, b):
                if b == 0:
                    wait(act, rows_scattered, 256 * i)
                for nt in range(NT):
                    act.wait_ge(x_full, i * X_U + b * NT + nt + 1)
                    o = nt * H * ROW
                    nc.scalar.copy(v(stage, o + b * P, (ROW, H), (1, P)), v(tp[nt % 2], 0, (P, H), (1, P)))
                    nc.scalar.copy(v(stage, o + NB * P + b, (ROW, H), (NB, K1)),
                                   v(tp[nt % 2], 2 * P, (K1, H), (1, K1))).then_inc(x_drained, 1)

            def turned(i, h, ks):
                for k in ks:
                    u = h * 8 + k
                    act.wait_ge(t_full, i * T_U + u + 1)
                    wait(act, ch_used, i * T_U + u + 1 - CH)
                    nc.scalar.copy(v(ch, (u % CH) * 2 * P, (1, 2 * P)), v(tp[u % 2], 0, (1, 2 * P))).then_inc(t_drained, 1)

            def result(i, h, b):
                if h == 0 and b == 0:
                    wait(act, out_ready, i * NB * CT)
                act.wait_ge(ch_used, i * T_U + (h * NB + b) * 4 + 4)
                for e in range(2):
                    k = (h * NB + b) * 2 + e
                    nc.scalar.copy(v(rs, (h * NT + e) * NB * P + b * P, (2 * NB * P, 4), (1, P)),
                                   v(pj[k % 4], 0, (P, 4), (1, P))).then_inc(r_drained, 1)

            def results(i, h):
                turned(i, h, range(0, 4 + AHEAD))
                result(i, h, 0)
                turned(i, h, range(4 + AHEAD, 8))
                result(i, h, 1)

            def gate(i, par, units):
                for k in units:
                    b, ct, nt = k // 4, k // 2 % 2, k % 2
                    if k == 0:
                        wait(act, o_full, i * O_U)
                    act.wait_ge(g_full, i * G_U + k + 1)
                    nc.scalar.activation(v(gt, (b * CT + ct) * N + nt * HALF, (1, HALF)), pj[k % 4][:, :], ACT.Silu,
                                         bias=bias(par, b, 4 + ct)).then_inc(g_drained, 1)

            def gate_again(i):
                for b in range(NB):
                    for ct in range(CT):
                        act.wait_ge(g_drained, i * G_U + b * 4 + ct * 2 + 2)
                        g = v(gt, (b * CT + ct) * N, (1, N))
                        nc.scalar.activation(g, g, ACT.Silu).then_inc(g_ready, 1)

            def residual(i, par):
                for h in range(H):
                    act.wait_ge(y_stored[h], 16 * (i + 1))
                for k in range(E_U):
                    ct, b, nt = k // 4, k // 2 % 2, k % 2
                    act.wait_ge(e_full, i * E_U + k + 1)
                    nc.scalar.activation(v(rs, (b * CT + ct) * N + nt * HALF, (1, HALF)), pj[k % 4][:, :], ACT.Silu,
                                         bias=bias(par, b, 2 + ct)).then_inc(e_drained, 1)

            def x_again(i, par):
                for b in range(NB):
                    o = (par * NB + b) * PRM_W
                    for ct in range(CT):
                        last = nc.scalar.activation(x_view(par, b, ct), x_view(par, b, ct), ACT.Identity,
                                                    bias=v(pcur, o + PRM_B + ct, (1, 1)), scale=v(pcur, o + PRM_A + ct, (1, 1)))
                    last.then_inc(x1_ready, 1)

            def output(i, b):
                act.wait_ge(z_ready, i * 4 + 3 + b)
                for ot in range(CT):
                    for nt in range(2):
                        k = b * 4 + ot * 2 + nt
                        act.wait_ge(o_full, i * O_U + k + 1)
                        nc.scalar.activation(v(rs, (b * CT + ot) * N + nt * HALF, (1, HALF)), pj[k % 4][:, :], ACT.Silu,
                                             bias=v(small, OUTB + ot, (1, 1))).then_inc(o_drained, 1)

            def cycle(i, par, half):
                more = not last_phase(i)
                decays(i, 0)
                gate(i, par, range(0, 8))
                decays(i, 1)
                if more:
                    for ot in range(CT):
                        project(i + 1, 1 - par, 0, ot)
                results(i, 0)
                if more:
                    convolved(i + 1, 0)
                gate_again(i)
                if more:
                    for ot in range(CT):
                        project(i + 1, 1 - par, 1, ot)
                    rows_out(i + 1, 0)
                results(i, 1)
                if more:
                    convolved(i + 1, 1)
                    rows_out(i + 1, 1)
                residual(i, par)
                x_again(i, par)
                output(i, 0)
                if more:
                    softplus(i + 1)
                output(i, 1)

            for b in range(NB):
                for ot in range(CT):
                    project(0, 0, b, ot)
                convolved(0, b)
                rows_out(0, b)
            softplus(0)
            phases(act, cycle)

        @block.vector
        def _(dve):
            n = [0]

            def link(ins):
                n[0] += 1
                ins.then_inc(setup_v, 1)
                dve.wait_ge(setup_v, n[0])

            def mark(number):
                assert n[0] == number, n[0]

            nc.vector.memset(v(xs, 0, (N + 2, CT), (1, 1)), 0.0)
            nc.vector.memset(v(xs, N + 1, (N + 2, CT), (1, 1)), 0.0)
            link(nc.vector.memset(v(hs, 0, ((NC + 1) * S, NB), (1, S)), 0.0))

            dve.wait_ge(weights_in, 16 * 16)
            m = MOB
            link(nc.vector.tensor_tensor(v(small, m + 8, (1, 2)), v(small, m, (4, 2)), v(small, m + 3, (4, 2)), ALU.mult))
            link(nc.vector.tensor_tensor(v(small, m + 10, (1, 2)), v(small, m + 1, (4, 2)), v(small, m + 2, (4, 2)), ALU.mult))
            link(nc.vector.tensor_tensor(v(small, m + 8, (1, 2)), v(small, m + 8, (1, 2)), v(small, m + 10, (1, 2)), ALU.subtract))
            link(nc.vector.scalar_tensor_tensor(v(small, m + 8, (1, 2)), v(small, m + 8, (1, 2)), -1.0, v(small, m + 8, (1, 2)), ALU.mult, ALU.max))
            link(nc.vector.tensor_scalar(v(small, m + 8, (1, 2)), v(small, m + 8, (1, 2)), 1e-3, None, ALU.max))
            mark(V_MOB)
            dve.wait_ge(setup_a, 2)
            link(nc.vector.reciprocal(v(small, m + 12, (1, 2)), v(small, m + 10, (1, 2))))
            for h in range(H):
                link(nc.vector.tensor_scalar(v(small, m + 4 * h, (1, 4)), v(small, m + 4 * h, (1, 4)), v(small, m + 12 + h, (1, 1)), None, ALU.mult))
            link(nc.vector.tensor_scalar(v(small, m + 3, (4, 2)), v(small, m + 3, (4, 2)), 1e-6, None, ALU.add))
            link(nc.vector.tensor_scalar(v(small, ANEG, (1, 16)), v(small, ANEG, (1, 16)), -1.0, None, ALU.mult))
            def t8(k):
                return v(bc8, k * NT, (1, NT))

            gx, gy = const("gridcol", (1, NT)), const("gridcol", (1, NT), off=NT)
            nr, ni, dr, di, t0, t1, den, num = (t8(k) for k in range(8))
            for h in range(H):
                a_, b_, c_, d_ = (v(small, m + 4 * h + k, (1, 1)) for k in range(4))
                nc.vector.tensor_scalar(nr, gx, a_, b_, ALU.mult, ALU.add)
                nc.vector.tensor_scalar(ni, gy, a_, None, ALU.mult)
                nc.vector.tensor_scalar(dr, gx, c_, d_, ALU.mult, ALU.add)
                link(nc.vector.tensor_scalar(di, gy, c_, None, ALU.mult))
                nc.vector.tensor_tensor(t0, dr, dr, ALU.mult)
                link(nc.vector.tensor_tensor(t1, di, di, ALU.mult))
                link(nc.vector.tensor_tensor(den, t0, t1, ALU.add))
                nc.vector.tensor_tensor(t0, nr, dr, ALU.mult)
                link(nc.vector.tensor_tensor(t1, ni, di, ALU.mult))
                link(nc.vector.tensor_tensor(num, t0, t1, ALU.add))
                nc.vector.tensor_tensor(t0, ni, dr, ALU.mult)
                link(nc.vector.tensor_tensor(t1, nr, di, ALU.mult))
                link(nc.vector.tensor_tensor(t0, t0, t1, ALU.subtract))
                link(nc.vector.scalar_tensor_tensor(num, t0, 1.3, num, ALU.mult, ALU.add))
                link(nc.vector.reciprocal(den, den))
                link(nc.vector.tensor_tensor(num, num, den, ALU.mult))
                link(nc.vector.tensor_scalar(num, num, 3.4e38, -3.4e38, ALU.min, ALU.max))
                link(nc.vector.tensor_tensor(v(big, h * N, (P, NT), (1, P)), v(bc8, 7 * NT, (1, NT), (0, P)),
                                             const("ident", (0, NT), (1, P)), ALU.mult))
            mark(V_DIAG)
            dve.wait_ge(setup_a, 3)
            for k in range(H * NT):
                nc.vector.scalar_tensor_tensor(v(mblk, k * P, (1, P)), v(crow, k * P, (1, P)), 1.0, const("ident"),
                                               ALU.mult, ALU.mult, accum_out=v(bc8, 80 + k, (1, 1)))
            link(nc.vector.memset(v(m16, 0, (1, 4 * H * NT)), 0.0))

            def rank(h, nt):
                mine = v(bc8, 80 + h * NT + nt, (1, 1))

                def span(lo, hi):
                    return v(crow, h * N + lo, (1, hi - lo))

                def count(k):
                    return v(m16, (h * NT + nt) * 4 + k, (1, 1))

                lo, hi = nt * P, nt * P + P
                if nt:
                    nc.vector.tensor_scalar(v(mblk, 0, (1, lo)), span(0, lo), mine, None, ALU.is_le, ALU.add, accum_out=count(0))
                if nt < NT - 1:
                    nc.vector.tensor_scalar(v(mblk, N - P, (1, N - hi)), span(hi, N), mine, None, ALU.is_lt, ALU.add, accum_out=count(1))
                nc.vector.scalar_tensor_tensor(v(mblk, 2 * (N - P), (1, P)), span(lo, hi), mine, const("before"), ALU.is_le, ALU.mult, accum_out=count(2))
                link(nc.vector.scalar_tensor_tensor(v(mblk, 2 * N - P, (1, P)), span(lo, hi), mine, const("notbefore"), ALU.is_lt, ALU.mult, accum_out=count(3)))

            link(nc.vector.memset(v(rs, 0, (1, CT * B * 12)), 0.0))
            for i in range(PH):
                for b in range(NB):
                    dve.wait_ge(x_in[i % 2][b], 16 * (i // 2 + 1))
                    for ct in range(CT - b):
                        for half in range(2):
                            unit = ct * B + i * NB + b
                            last = nc.vector.bn_stats(v(rs, unit * 12 + half * 6, (1, 6)), x_view(i % 2, b, ct, half * HALF, HALF))
                last.then_inc(stats_done, 1)
                for k in (2 * i, 2 * i + 1):
                    rank(k // NT, k % NT)
            dve.wait_ge(stats_done, PH)
            link(nc.vector.tensor_reduce(v(bblk, 0, (1, H * NT)), v(m16, 0, (4, H * NT), (1, 4)), AX.X, ALU.add))
            nc.vector.tensor_scalar(v(idx, 0, (1, NT)), v(bblk, 0, (1, NT)), 0.0, None, ALU.add)
            link(nc.vector.tensor_scalar(v(idx, NT, (1, NT)), v(bblk, NT, (1, NT)), float(N), None, ALU.add))
            U = CT * B
            MEAN, SQ, T = 1024, 1024 + U, 1024 + 2 * U
            col = lambda off: v(rs, off, (1, U))
            link(nc.vector.tensor_reduce(col(MEAN), v(rs, 1, (12, U), (3, 4)), AX.X, ALU.add))
            link(nc.vector.tensor_scalar(col(MEAN), col(MEAN), 0.25, None, ALU.mult))
            link(nc.vector.tensor_tensor(v(rs, 1200, (4, U), (1, 4)), v(rs, 1, (12, U), (3, 4)), v(rs, 1, (12, U), (3, 4)), ALU.mult))
            link(nc.vector.tensor_reduce(col(SQ), v(rs, 1200, (4, U), (1, 4)), AX.X, ALU.add))
            link(nc.vector.tensor_reduce(col(T), v(rs, 2, (12, U), (3, 4)), AX.X, ALU.add))
            link(nc.vector.tensor_scalar(col(T), col(T), 1.0 / N, None, ALU.mult))
            link(nc.vector.scalar_tensor_tensor(col(SQ), col(SQ), 0.25, col(T), ALU.mult, ALU.add))
            dve.wait_ge(stats_done_a, PH)
            nc.vector.tensor_scalar(v(rs, MEAN + B + 1, (NB, PH)), v(rs, 400, (1, PH)), 1.0 / N, None, ALU.mult)
            link(nc.vector.tensor_scalar(v(rs, SQ + B + 1, (NB, PH)), v(rs, 408, (1, PH)), 1.0 / N, None, ALU.mult))
            mark(V_STATS)

            def group_rstd(sqrt_number):
                link(nc.vector.tensor_copy(v(dts, 32, (1, U)), v(tp[0], 0, (1, U))))
                link(nc.vector.tensor_tensor(v(dts, 64, (1, U)), v(dts, 32, (1, U)), v(dts, 32, (1, U)), ALU.mult))
                link(nc.vector.tensor_tensor(v(dts, 0, (1, U)), v(tp[0], U, (1, U)), v(dts, 64, (1, U)), ALU.subtract))
                link(nc.vector.tensor_scalar(v(dts, 0, (1, U)), v(dts, 0, (1, U)), 0.0, EPS, ALU.max, ALU.add))

            MG, RSTD = v(dts, 32, (1, U)), v(dts, 128, (1, U))
            dve.wait_ge(setup_p, 1)
            group_rstd(3)
            mark(V_VAR1)
            dve.wait_ge(setup_a, 4)
            link(nc.vector.reciprocal(RSTD, v(dts, 0, (1, U))))
            link(nc.vector.tensor_tensor(col(T), col(MEAN), MG, ALU.subtract))
            link(nc.vector.tensor_tensor(col(T), col(T), RSTD, ALU.mult))
            mark(V_Y)
            dve.wait_ge(setup_p, 2)
            link(nc.vector.tensor_copy(v(bc8, 0, (1, 136), parts=B), v(tp[1], 0, (1, 136), parts=B)))
            link(nc.vector.reduce_max(v(bc8, 140, (1, 1), parts=B), v(bc8, 0, (1, E), parts=B), AX.X))
            link(nc.vector.tensor_scalar(v(bc8, 140, (1, 1), parts=B), v(bc8, 140, (1, 1), parts=B), -1.0, None, ALU.mult))
            mark(V_MAX)
            dve.wait_ge(setup_a, 5)
            link(nc.vector.reciprocal(v(bc8, 142, (1, 1), parts=B), v(bc8, 141, (1, 1), parts=B)))
            link(nc.vector.tensor_scalar(v(bc8, 0, (1, E), parts=B), v(bc8, 0, (1, E), parts=B), v(bc8, 142, (1, 1), parts=B), None, ALU.mult))
            link(nc.vector.scalar_tensor_tensor(v(bc8, 8, (R, E), (1, R), parts=B), v(bc8, 8, (R, E), (1, R), parts=B), 0.0,
                                                v(bc8, 0, (1, E), (0, R), parts=B), ALU.max, ALU.mult))
            mark(V_HID)
            dve.wait_ge(setup_p, 3)
            nc.vector.tensor_copy(v(bc8, 160, (1, B)), v(tp[0], 0, (1, B)))
            link(nc.vector.tensor_copy(v(bc8, 180, (1, B), parts=E), v(tp[0], P, (1, B), parts=E)))
            mark(V_HIDT)
            dve.wait_ge(setup_a, 6)
            SC, A_, B_ = v(dts, 96, (1, U)), v(dts, 160, (1, U)), v(dts, 192, (1, U))
            link(nc.vector.tensor_scalar(SC, SC, 1.0, None, ALU.add))
            link(nc.vector.reciprocal(SC, SC))
            link(nc.vector.tensor_tensor(SC, SC, RSTD, ALU.mult))
            link(nc.vector.tensor_scalar(A_, SC, 1.0, None, ALU.add))
            link(nc.vector.tensor_tensor(B_, SC, MG, ALU.mult))
            link(nc.vector.tensor_scalar(B_, B_, -1.0, None, ALU.mult))
            link(nc.vector.tensor_tensor(col(T), col(MEAN), col(MEAN), ALU.mult))
            link(nc.vector.tensor_tensor(col(SQ), col(SQ), col(T), ALU.subtract))
            link(nc.vector.tensor_tensor(col(SQ), col(SQ), A_, ALU.mult))
            link(nc.vector.tensor_tensor(col(SQ), col(SQ), A_, ALU.mult))
            link(nc.vector.tensor_tensor(col(MEAN), col(MEAN), A_, ALU.mult))
            link(nc.vector.tensor_tensor(col(MEAN), col(MEAN), B_, ALU.add))
            link(nc.vector.tensor_tensor(col(T), col(MEAN), col(MEAN), ALU.mult))
            link(nc.vector.tensor_tensor(col(SQ), col(SQ), col(T), ALU.add))
            mark(V_STATS2)
            dve.wait_ge(setup_p, 5)
            group_rstd(6)
            mark(V_VAR2)
            dve.wait_ge(setup_a, 7)
            link(nc.vector.reciprocal(RSTD, v(dts, 0, (1, U))))
            link(nc.vector.tensor_tensor(SC, B_, MG, ALU.subtract))
            link(nc.vector.tensor_tensor(col(T), SC, RSTD, ALU.mult))
            mark(V_Q)
            per_image = lambda off: v(prm, off, (1, CT), (PRM_W, B))
            nc.vector.tensor_tensor(per_image(PRM_P), v(dts, 128, (B, CT), (1, B)), v(dts, 160, (B, CT), (1, B)), ALU.mult)
            nc.vector.tensor_copy(per_image(PRM_A), v(dts, 160, (B, CT), (1, B)))
            nc.vector.tensor_copy(per_image(PRM_B), v(dts, 192, (B, CT), (1, B)))
            dve.wait_ge(setup_p, 6)
            link(nc.vector.tensor_tensor(v(prm, PRM_BIAS, (1, 6), (PRM_W, B)), v(tp[1], 0, (B, 6), (1, B)),
                                         v(small, INB, (1, 6), (0, B)), ALU.add))
            nc.vector.memset(v(m16, 0, (1, 1)), 0.0).then_inc(params_ready, 1)

            def take_params(i, par):
                if not (isinstance(i, int) and i < 2):
                    dve.wait_ge(x1_ready, (i - 1) * NB)
                    dve.wait_ge(e_drained, (i - 1) * E_U)
                src = (v(prm, i * NB * PRM_W, (1, NB * PRM_W)) if isinstance(i, int)
                       else prm[:, bass.ds(i * (NB * PRM_W), NB * PRM_W)])
                nc.vector.tensor_copy(v(pcur, par * NB * PRM_W, (1, NB * PRM_W)), src).then_inc(pcur_ready, 1)

            def convolve(i, b):
                for ot in range(CT):
                    step = (i * NB + b) * 3
                    dst = v(xf, ot * N, (1, N))
                    for k in (1, 2):
                        dve.wait_ge(conv_step[ot], step + k)
                        nc.vector.scalar_tensor_tensor(dst, v(xs, ot * (N + 2) + k, (1, N)), v(small, DWW + ot * 3 + k, (1, 1)),
                                                       dst, ALU.mult, ALU.add).then_inc(conv_step[ot], 1)

            def add_bias(i):
                for nt in range(NT):
                    dve.wait_ge(x_drained, i * X_U + NT + nt + 1)
                    d = v(stage, nt * H * ROW + NB * P, (ROW, H), (NB, K1), (1, NB))
                    nc.vector.tensor_tensor(d, d, v(small, DBCB, (K1, H), (1, K1), (0, NB)), ALU.add).then_inc(stage_ready, 1)

            HQ = H * Q
            AXO, UO, WO, LO, MO, DO = 0, 32, 64, 96, 128, 192
            DB, DBE, CS = 0, Q * S, 2 * Q * S

            def part(h, off):
                return h * NT * ROW + NB * P + off

            def softplus(i):
                d = lambda off: v(dts, off, (1, HQ))
                s0 = i * 9
                dve.wait_ge(rows_in, 16 * (i + 1))
                wait(dve, sg_full, i * H)
                for h in range(H):
                    raw = v(xp, part(h, 0), (1, NB), (ROW, NT))
                    last = nc.vector.scalar_tensor_tensor(v(dts, AXO + h * Q, (NT, NB), (1, NT)), raw, -1.0, raw, ALU.mult, ALU.max)
                last.then_inc(sp_v, 1)
                dve.wait_ge(sp_a, i * 2 + 1)
                nc.vector.tensor_scalar(d(WO), d(UO), 1.0, None, ALU.add).then_inc(sp_v, 1)
                dve.wait_ge(sp_v, s0 + 2)
                nc.vector.tensor_scalar(d(MO), d(WO), 1.0, None, ALU.is_equal).then_inc(sp_v, 1)
                dve.wait_ge(sp_v, s0 + 3)
                dve.wait_ge(sp_a, i * 2 + 2)
                nc.vector.tensor_tensor(d(LO), d(LO), d(MO), ALU.add).then_inc(sp_v, 1)
                nc.vector.scalar_tensor_tensor(d(WO), d(WO), -1.0, d(MO), ALU.add, ALU.add).then_inc(sp_v, 1)
                dve.wait_ge(sp_v, s0 + 5)
                nc.vector.reciprocal(d(WO), d(WO)).then_inc(sp_v, 1)
                dve.wait_ge(sp_v, s0 + 6)
                nc.vector.tensor_tensor(d(LO), d(LO), d(WO), ALU.mult).then_inc(sp_v, 1)
                dve.wait_ge(sp_v, s0 + 7)
                nc.vector.tensor_tensor(d(LO), d(LO), d(UO), ALU.mult).then_inc(sp_v, 1)
                dve.wait_ge(sp_v, s0 + 8)
                for h in range(H):
                    last = nc.vector.scalar_tensor_tensor(
                        v(dts, DO + h * Q, (NT, NB), (1, NT)), v(xp, part(h, 0), (1, NB), (ROW, NT)), 0.0,
                        v(dts, LO + h * Q, (NT, NB), (1, NT)), ALU.max, ALU.add)
                last.then_inc(sp_v, 1)
                dve.wait_ge(sp_v, s0 + 9)
                nc.vector.tensor_tensor(v(rseg, 0, (L, HQ), (1, L)), v(dts, DO, (1, HQ), (0, L)),
                                        const("fromstart", (0, HQ), (1, L)), ALU.mult).then_inc(r_ready, 1)
                nc.vector.tensor_tensor(v(rtot, 0, (CPT, HQ), (1, CPT)), v(dts, DO, (1, HQ), (0, CPT)),
                                        const("chunk", (0, HQ), (1, CPT)), ALU.mult).then_inc(r_ready, 1)

            def scans(i, h, b):
                ih = i * H + h
                dve.wait_ge(st_full, ih * NB + b + 1)
                wait(dve, t_full, (ih - 1) * 8 + (b + 1) * 4)
                for s in range(S):
                    nc.vector.tensor_tensor_scan(
                        v(hs, (b * (NC + 1) + 1) * S + s, (S, NC)), v(big, s * EEW + TOT + b * NC, (1, NC)),
                        v(st, s, (S, NC)), 0.0, ALU.mult, ALU.add).then_inc(hs_ready, 1)

            def factors(i, h):
                ih = i * H + h
                for b in range(NB):
                    last = nc.vector.tensor_tensor(
                        v(bc8, DB + b * NT * S, (S, NT), (1, S)), v(xp, part(h, NB + b), (ROW, NT), (NB, S)),
                        v(dts, DO + h * Q + b * NT, (1, NT), (0, S)), ALU.mult)
                last.then_inc(bc_step, 1)
                dve.wait_ge(ee_ready, ih + 1)
                dve.wait_ge(bc_step, ih * 3 + 1)
                nc.vector.tensor_tensor(v(bc8, DBE, (S, Q), (1, S)), v(bc8, DB, (S, Q), (1, S)),
                                        v(big, SEG + L - 1, (L, Q), (EEW, S)), ALU.mult).then_inc(bc_step, 1)
                for b in range(NB):
                    last = nc.vector.tensor_tensor(
                        v(bc8, CS + b * NT * S, (S, NT), (1, S)), v(xp, part(h, NB * (1 + S) + b), (ROW, NT), (NB, S)),
                        v(big, CUM + b * NT, (1, NT), (EEW, S)), ALU.mult)
                last.then_inc(bc_step, 1)
                wait(dve, st_full, ih * NB)
                dve.wait_ge(bc_step, ih * 3 + 2)
                nc.vector.tensor_tensor(v(bblk, 0, (CPT * S, Q), (S, CPT), (1, S)), v(bc8, DBE, (S, Q), (0, CPT), (1, S)),
                                        const("chunk", (0, Q), (1, CPT), (0, S)), ALU.mult).then_inc(blk_ready, 1)
                dve.wait_ge(bc_step, ih * 3 + 3)
                wait(dve, t_full, ih * 8)
                nc.vector.tensor_tensor(v(cblk, 0, (CPT * S, Q), (S, CPT), (1, S)), v(bc8, CS, (S, Q), (0, CPT), (1, S)),
                                        const("chunk", (0, Q), (1, CPT), (0, S)), ALU.mult).then_inc(blk_ready, 1)

            def token_weights(i, h):
                ih = i * H + h
                dve.wait_ge(w_ready, ih + 1)
                W = v(big, W_OFF, (Q * L, S), (L, Q), (1, L))
                nc.vector.tensor_tensor(W, W, v(bc8, DB, (1, S), (S, Q), (0, L)), ALU.mult).then_inc(m_step, 1)
                dve.wait_ge(m_step, ih * 3 + 1)
                nc.vector.tensor_reduce(m16[:, :], v(big, W_OFF, (1, Q * L), (Q * L, S)), AX.X, ALU.add).then_inc(m_step, 1)
                dve.wait_ge(m_step, ih * 3 + 2)
                nc.vector.scalar_tensor_tensor(v(m16, 0, (L, Q), (1, L)), const("diag", (0, Q), (1, L)),
                                               v(small, DPAR + h, (1, 1)), v(m16, 0, (L, Q), (1, L)),
                                               ALU.mult, ALU.add).then_inc(m_step, 1)
                dve.wait_ge(m_step, ih * 3 + 3)
                wait(dve, ch_used, ih * 8)
                nc.vector.tensor_tensor(v(mblk, 0, (P, Q), (L, CPT), (1, L)), v(m16, 0, (L, Q), (0, CPT), (1, L)),
                                        const("causal", (0, Q), (L, CPT), (1, L)), ALU.mult).then_inc(mblk_ready, 1)

            def gated(i, h):
                for b in range(NB):
                    dve.wait_ge(g_ready, (i * NB + b) * CT + h + 1)
                    o = (b * CT + h) * N
                    for nq in range(2):
                        k = (h * NB + b) * 2 + nq
                        dve.wait_ge(y_full, i * Y_U + k + 1)
                        half_gate = v(gt, o + nq * HALF, (1, HALF))
                        nc.vector.tensor_tensor(half_gate, v(tp[k % 2], 0, (1, HALF)), half_gate, ALU.mult).then_inc(y_drained, 1)
                for b in range(NB):
                    o = (b * CT + h) * N
                    dve.wait_ge(y_drained, i * Y_U + h * 4 + b * 2 + 2)
                    dve.wait_ge(e_drained, i * E_U + h * 4 + b * 2 + 2)
                    nc.vector.tensor_tensor(v(gt, o, (1, N)), v(gt, o, (1, N)), v(rs, o, (1, N)), ALU.add).then_inc(z_ready, 1)

            def output(i, par, b):
                dve.wait_ge(x1_ready, i * NB + b + 1)
                for ot in range(CT):
                    dve.wait_ge(o_drained, i * O_U + b * 4 + ot * 2 + 2)
                    nc.vector.tensor_tensor(x_view(par, b, ot), x_view(par, b, ot), v(rs, (b * CT + ot) * N, (1, N)),
                                            ALU.add).then_inc(out_ready, 1)

            def cycle(i, par, half):
                more = not last_phase(i)
                if more:
                    take_params(i + 1, 1 - par)
                factors(i, 0)
                scans(i, 0, 0)
                scans(i, 0, 1)
                token_weights(i, 0)
                if more:
                    convolve(i + 1, 0)
                factors(i, 1)
                scans(i, 1, 0)
                scans(i, 1, 1)
                token_weights(i, 1)
                if more:
                    convolve(i + 1, 1)
                    add_bias(i + 1)
                for h in range(H):
                    gated(i, h)
                output(i, par, 0)
                if more:
                    softplus(i + 1)
                output(i, par, 1)

            take_params(0, 0)
            for b in range(NB):
                convolve(0, b)
            add_bias(0)
            softplus(0)
            phases(dve, cycle)

        @block.tensor
        def _(pe):
            U = CT * B
            MEAN, T = 1024, 1024 + 2 * U
            pe.wait_ge(weights_in, 16 * 16)
            pe.wait_ge(setup_v, V_DIAG)
            for k in range(4):
                last = nc.tensor.matmul(pj[k][:, :], const("ones"), v(big, k * HALF, (1, HALF)), start=True, stop=True)
            last.then_inc(setup_g, 1)
            pe.wait_ge(setup_v, V_STATS)
            nc.tensor.matmul(v(tp[0], 0, (1, 2 * U)), const("group"), v(rs, MEAN, (1, 2 * U)), start=True, stop=True).then_inc(setup_p, 1)
            pe.wait_ge(setup_v, V_Y)
            for ct in range(CT):
                nc.tensor.matmul(v(tp[1], 0, (1, 136), parts=B), v(rs, T + ct * B, (1, B)), v(xp, ct * 136, (1, 136)), start=(ct == 0), stop=False)
            nc.tensor.matmul(v(tp[1], 0, (1, 136), parts=B), const("ones", (1, B), parts=1), v(xp, 272, (1, 136), parts=1),
                             start=False, stop=True).then_inc(setup_p, 1)
            pe.wait_ge(setup_v, V_HID)
            ident16 = const("ident", (1, B), parts=B)
            nc.tensor.transpose(v(tp[0], 0, (1, B)), v(bc8, 8, (1, P), parts=B), ident16)
            nc.tensor.transpose(v(tp[0], P, (1, B), parts=E), v(bc8, 0, (1, E), parts=B), ident16).then_inc(setup_p, 1)
            pe.wait_ge(setup_v, V_HIDT)
            for ct in range(CT):
                o = v(tp[1], ct * B, (1, B))
                nc.tensor.matmul(o, v(xp, 408 + ct * P, (1, P)), v(bc8, 160, (1, B)), start=True, stop=False)
                last = nc.tensor.matmul(o, v(xp, 664 + ct * P, (1, P), parts=E), v(bc8, 180, (1, B), parts=E), start=False, stop=True)
            last.then_inc(setup_p, 1)
            pe.wait_ge(setup_v, V_STATS2)
            nc.tensor.matmul(v(tp[0], 0, (1, 2 * U)), const("group"), v(rs, MEAN, (1, 2 * U)), start=True, stop=True).then_inc(setup_p, 1)
            pe.wait_ge(setup_v, V_Q)
            for ot in range(6):
                for ct in range(CT):
                    last = nc.tensor.matmul(v(tp[1], ot * B, (1, B)), v(inw, ct * 3 * C + ot * P, (1, P)),
                                            v(rs, T + ct * B, (1, B)), start=(ct == 0), stop=(ct == CT - 1))
            last.then_inc(setup_p, 1)
            pe.wait_ge(params_ready, 1)

            def pj_slot(k, own, own_base, before):
                if k < 4:
                    if before:
                        wait(pe, before[0], before[1] - 3 + k)
                else:
                    pe.wait_ge(own, own_base + k - 3)
                return pj[k % 4]

            def tp_slot(k, own, own_base, before):
                if k < 2:
                    if before:
                        wait(pe, before[0], before[1] - 1 + k)
                else:
                    pe.wait_ge(own, own_base + k - 1)
                return tp[k % 2]

            def part(o, par, b, slot, ot, nt):
                for ct in range(CT):
                    last = nc.tensor.matmul(o[:, :], v(wsc, (b * CT + ct) * 2 * C + slot * C + ot * P, (1, P)),
                                            x_view(par, b, ct, nt * HALF, HALF), start=(ct == 0), stop=(ct == CT - 1))
                return last

            def project(i, par, half, b, before, units=range(4)):
                for k in units:
                    if k == 0:
                        pe.wait_ge(x_in[par][b], 16 * (PH // 2 + half + 1))
                        pe.wait_ge(wa_ready, i * NB + b + 1)
                    o = pj_slot(k, a_drained, i * A_U + b * 4, before)
                    part(o, par, b, 0, k // 2, k % 2).then_inc(a_full, 1)

            def rows(i, b, before):
                pe.wait_ge(xf_ready, (i * NB + b + 1) * CT)
                for nt in range(NT):
                    o = tp_slot(nt, x_drained, i * X_U + b * NT, before)
                    tile = lambda ct: v(xf, ct * N + nt * P, (1, P))
                    for ct in range(CT):
                        nc.tensor.transpose(v(o, ct * P, (1, P)), tile(ct), const("ident"))
                    for ct in range(CT):
                        last = nc.tensor.matmul(v(o, 2 * P, (1, H * K1)), tile(ct), v(dbcw, ct * H * K1, (1, H * K1)),
                                                start=(ct == 0), stop=(ct == CT - 1))
                    last.then_inc(x_full, 1)

            def segments(i, h):
                wait(pe, ee_ready, i * H + h)
                nc.tensor.matmul(v(sg, SEG, (1, Q * L)), const("after"), v(rseg, h * Q * L, (1, Q * L)), start=True, stop=True)
                nc.tensor.matmul(v(sg, CUM, (1, Q)), const("upto"), v(dts, 192 + h * Q, (1, Q)), start=True, stop=True)
                nc.tensor.matmul(v(sg, TOT, (1, Q * CPT)), const("ones"), v(rtot, h * Q * CPT, (1, Q * CPT)),
                                 start=True, stop=True).then_inc(sg_full, 1)

            def x_rows(h, b, g):
                return v(xp, (h * NT + g) * ROW + b * P, (1, P))

            def chunk_sums(i, h, b):
                wait(pe, hs_ready, ((i * H + h) * NB + b) * S)
                pe.wait_ge(blk_ready, (i * H + h) * 2 + 1)
                for g in range(NT):
                    last = nc.tensor.matmul(v(st, g * CPT * S, (1, CPT * S)), x_rows(h, b, g),
                                            v(bblk, (b * NT + g) * CPT * S, (1, CPT * S)), start=True, stop=True)
                last.then_inc(st_full, 1)

            def turn(i, h, k, before):
                b, gp = divmod(k, 4)
                o = tp_slot(k, t_drained, i * T_U + h * 8, before)
                if gp == 0:
                    pe.wait_ge(blk_ready, (i * H + h) * 2 + 2)
                    pe.wait_ge(hs_ready, ((i * H + h) * NB + b + 1) * S)
                nc.tensor.transpose(v(o, 0, (1, P)), v(cblk, (b * NT + 2 * gp) * CPT * S, (1, P)), const("ident"))
                nc.tensor.transpose(v(o, P, (1, P)), v(hs, (b * (NC + 1) + 2 * gp * CPT) * S, (1, P)), const("ident")).then_inc(t_full, 1)

            def result(i, h, k, before):
                b, gp = divmod(k, 4)
                u = h * 8 + k
                if gp == 0:
                    pj_slot(2 * b + 1, None, None, before)
                    pe.wait_ge(mblk_ready, i * H + h + 1)
                pe.wait_ge(t_drained, i * T_U + u + 1)
                for e in range(2):
                    g = 2 * gp + e
                    d = v(pj[2 * b + e], gp * P, (1, P))
                    nc.tensor.matmul(d, v(mblk, (b * NT + g) * P, (1, P)), x_rows(h, b, g), start=True, stop=False)
                    half_rows = dict(parts=64, p0=64 * e)
                    last = nc.tensor.matmul(d, v(ch, (u % CH) * 2 * P, (1, P), **half_rows),
                                            v(ch, (u % CH) * 2 * P + P, (1, P), **half_rows), start=False, stop=True)
                last.then_inc(ch_used, 1)

            def results(i, h, before_t, before_r, between=None):
                for k in range(AHEAD):
                    turn(i, h, k, before_t)
                for k in range(8):
                    if k + AHEAD < 8:
                        turn(i, h, k + AHEAD, before_t)
                    result(i, h, k, before_r)
                    if k == 3 and between:
                        between()

            def gate(i, par, units, before):
                for k in units:
                    b = k // 4
                    if k % 4 == 0:
                        pe.wait_ge(wg_ready, i * NB + b + 1)
                    o = pj_slot(k, g_drained, i * G_U, before)
                    part(o, par, b, 0, k // 2 % 2, k % 2).then_inc(g_full, 1)

            def residual(i, par, before):
                pe.wait_ge(wr_ready, (i + 1) * NB)
                for k in range(E_U):
                    o = pj_slot(k, e_drained, i * E_U, before)
                    part(o, par, k // 2 % 2, 1, k // 4, k % 2).then_inc(e_full, 1)

            def turn_back(i, h, before):
                pe.wait_ge(y_gathered[h], 128 * (i + 1))
                for k in range(h * 4, h * 4 + 4):
                    b, nq = k // 2 % 2, k % 2
                    o = tp_slot(k, y_drained, i * Y_U, before)
                    for e in range(4):
                        last = nc.tensor.transpose(v(o, e * P, (1, P)), v(big, (h * NT + nq * 4 + e) * NB * P + b * P, (1, P)), const("ident"))
                    last.then_inc(y_full, 1)

            def output(i, before):
                for k in range(O_U):
                    b, ot, nt = k // 4, k // 2 % 2, k % 2
                    if k % 4 == 0:
                        pe.wait_ge(z_ready, i * 4 + 3 + b)
                    o = pj_slot(k, o_drained, i * O_U, before)
                    for h in range(CT):
                        last = nc.tensor.matmul(o[:, :], v(outw, h * C + ot * P, (1, P)),
                                                v(gt, (b * CT + h) * N + nt * HALF, (1, HALF)), start=(h == 0), stop=(h == CT - 1))
                    last.then_inc(o_full, 1)

            def cycle(i, par, half):
                more = not last_phase(i)
                nxt = (i + 1, 1 - par, half + par)
                before_g = (a_drained, A_U) if first(i) else (o_drained, i * O_U)
                before_t = (x_drained, X_U) if first(i) else (y_drained, i * Y_U)
                g_all = (g_drained, (i + 1) * G_U)
                pe.wait_ge(r_ready, i * 2 + 2)
                segments(i, 0)
                gate(i, par, range(0, 5), before_g)
                chunk_sums(i, 0, 0)
                segments(i, 1)
                gate(i, par, range(5, 7), before_g)
                chunk_sums(i, 0, 1)
                gate(i, par, range(7, 8), before_g)
                if more:
                    project(*nxt, 0, g_all)
                results(i, 0, before_t, (a_drained, (i + 1) * A_U + 4) if more else g_all,
                        between=lambda: chunk_sums(i, 1, 0))
                r_half = (r_drained, i * R_U + 4)
                if more:
                    project(*nxt, 1, r_half, range(0, 1))
                chunk_sums(i, 1, 1)
                if more:
                    project(*nxt, 1, r_half, range(1, 4))
                t_half = (t_drained, i * T_U + 8)
                if more:
                    rows(i + 1, 0, t_half)
                results(i, 1, (x_drained, (i + 1) * X_U + NT) if more else t_half,
                        (a_drained, (i + 2) * A_U) if more else r_half)
                t_all = (t_drained, (i + 1) * T_U)
                if more:
                    rows(i + 1, 1, t_all)
                before_y = (x_drained, (i + 2) * X_U) if more else t_all
                turn_back(i, 0, before_y)
                residual(i, par, (r_drained, (i + 1) * R_U))
                turn_back(i, 1, None)
                output(i, (e_drained, (i + 1) * E_U))

            project(0, 0, 0, 0, None)
            rows(0, 0, None)
            project(0, 0, 0, 1, (a_drained, 4))
            rows(0, 1, (x_drained, NT))
            phases(pe, cycle)


V_MOB = 6
V_STATS = 63
V_VAR1 = 67
V_Y = 70
V_MAX = 73
V_HID = 76
V_HIDT = 77
V_STATS2 = 91
V_VAR2 = 95
V_DIAG = 35
V_Q = 98
P_EXPERT = 4


def kernel(**inputs):
    import concourse.bacc as _bacc
    from concourse.bass_utils import run_bass_kernel_spmd as _run

    w = {k: np.ascontiguousarray(np.asarray(a)) for k, a in inputs.items()}
    L1, L0 = "L1_conv_", "L0_conv_"

    def by_tile(a):
        return np.ascontiguousarray(a.reshape(-1, P, a.shape[-1]).transpose(1, 0, 2))

    def column(a):
        return np.ascontiguousarray(a.reshape(-1, P).T)

    table = constants()
    w1 = w[L0 + "W1"].reshape(E * R, C).T
    arrays = dict(
        x=w["x"].reshape(B, C, N),
        w1g=by_tile(np.concatenate([w[L0 + "Wg"].T, w1], 1)),
        b1g=np.concatenate([w[L0 + "bg"], w[L0 + "b1"].reshape(-1)])[None],
        w2=np.ascontiguousarray(w[L0 + "W2"].transpose(0, 2, 1).reshape(E * R, C)),
        b2=w[L0 + "b2"],
        inw=by_tile(w[L1 + "in_proj_w"].T),
        inb=column(w[L1 + "in_proj_b"]),
        dww=np.ascontiguousarray(w[L1 + "dw_w"].reshape(CT, P, 3).transpose(1, 0, 2).reshape(P, 6)),
        dwb=column(w[L1 + "dw_b"]),
        dbcw=by_tile(w[L1 + "dbc_w"].T),
        dbcb=w[L1 + "dbc_b"][None],
        alog=w[L1 + "A_log"].reshape(1, H * S),
        dpar=w[L1 + "Dparam"][None],
        mob=w[L1 + "mobius"].reshape(1, 4 * H),
        outw=by_tile(w[L1 + "out_proj_w"].T),
        outb=column(w[L1 + "out_proj_b"]),
        const=table)
    nc = _bacc.Bacc("TRN2", target_bir_lowering=False, num_devices=1)
    feeds, args = {}, []
    for name, a in arrays.items():
        a = np.ascontiguousarray(a)
        feeds[f"in_{name}"] = a
        args.append(nc.dram_tensor(f"in_{name}", a.shape, mybir.dt.from_np(a.dtype), kind="ExternalInput").ap())
    out = nc.dram_tensor("out_0", (B, C, N), F32, kind="ExternalOutput").ap()
    build(nc, *args, out)
    r = _run(nc, [feeds], core_ids=[0])
    return r.results[0]["out_0"].reshape(B, C, IMG, IMG)
```

```python
import numpy as np
from contextlib import ExitStack

import concourse.bass as bass
from concourse import mybir

F32 = mybir.dt.float32
U32 = mybir.dt.uint32
ALU = mybir.AluOpType
ACT = mybir.ActivationFunctionType
AX = mybir.AxisListType

P = 128
B, C, IMG = 16, 256, 32
N = IMG * IMG
CT = C // P
H, S = 2, 8
E, R = 8, 16
NB = 2
PH = B // NB
NT = N // P
L = 16
CPT = P // L
NC = N // L
K1 = 1 + 2 * S
ROW = NB * (P + K1)
Q = NB * NT
HALF = 512
EPS = 1e-5

SEG, CUM, TOT = 0, Q * L, Q * L + Q
EEW = TOT + Q * CPT

CONST_WIDTHS = dict(ident=P, after=P, upto=P, ones=P, group=P, before=P, notbefore=P,
                    fromstart=L, chunk=CPT, causal=P, diag=L, gridcol=2 * NT)
CONST_AT = {}
_at = 0
for _name, _width in CONST_WIDTHS.items():
    CONST_AT[_name] = _at
    _at += _width
CONST_W = _at

PRM_P, PRM_A, PRM_B, PRM_BIAS, PRM_W = 0, 2, 4, 6, 12


def constants():
    r, c = np.arange(P)[:, None], np.arange(P)[None, :]
    same = (r // L) == (c // L)
    lin = np.linspace(-1.0, 1.0, IMG).astype(np.float32)
    gy, gx = (v.reshape(-1) for v in np.meshgrid(lin, lin, indexing="ij"))
    part = dict(
        ident=r == c, after=same & (r > c), upto=same & (r <= c), ones=np.ones((P, P)),
        group=((r // 8) == (c // 8)) / 8.0, before=c < r, notbefore=c >= r,
        fromstart=(r % L) <= c[:, :L], chunk=(r // L) == c[:, :CPT], causal=same & (c >= r),
        diag=(r % L) == c[:, :L],
        gridcol=np.concatenate([gx.reshape(NT, P).T, gy.reshape(NT, P).T], 1))
    table = np.concatenate([part[k].astype(np.float32) for k in CONST_WIDTHS], 1)
    return np.ascontiguousarray(table)


def build(nc, x_d, w1g_d, b1g_d, w2_d, b2_d, inw_d, inb_d, dww_d, dwb_d, dbcw_d, dbcb_d, alog_d,
          dpar_d, mob_d, outw_d, outb_d, const_d, out_d):
    with ExitStack() as ctx:
        def sb(name, width, dt=F32):
            return ctx.enter_context(nc.sbuf_tensor(name, [P, width], dt))

        def sem(name):
            return ctx.enter_context(nc.semaphore(name))

        def v(tensor, off, *dims, parts=P, p0=0):
            width = tensor.shape[1]
            assert off + sum(step * (count - 1) for step, count in dims) < width
            return bass.AP(tensor, p0 * width + off, [[width, parts]] + [list(d) for d in dims])

        xt_d = nc.dram_tensor("xt_scratch", [H * N, ROW], F32)
        yt_d = nc.dram_tensor("yt_scratch", [H * N, NB * P], F32)
        cd_d = nc.dram_tensor("cd_scratch", [H * N, S * NB], F32)

        cst = sb("cst", CONST_W)
        inw = sb("inw", CT * 3 * C)
        outw = sb("outw", CT * C)
        dbcw = sb("dbcw", CT * H * K1)
        small = sb("small", 96)
        xb = [sb("xb0", NB * CT * N), sb("xb1", NB * CT * N)]
        wsc = sb("wsc", NB * CT * 2 * C)
        xs = sb("xs", CT * (N + 2))
        xf = sb("xf", CT * N)
        stage = sb("stage", NT * H * ROW)
        xp = sb("xp", H * NT * ROW)
        crow = sb("crow", H * NT * L * S * NB)
        big = sb("big", S * EEW + S * Q * L)
        mblk = sb("mblk", Q * P)
        bblk = sb("bblk", Q * CPT * S)
        cblk = sb("cblk", Q * CPT * S)
        m16 = sb("m16", Q * L)
        rseg = sb("rseg", H * Q * L)
        rtot = sb("rtot", H * Q * CPT)
        dts = sb("dts", 8 * H * Q)
        bc8 = sb("bc8", 3 * Q * S)
        hs = sb("hs", NB * (NC + 1) * S)
        ch = sb("ch", 4 * 2 * P)
        gt = sb("gt", NB * CT * N)
        rs = sb("rs", NB * CT * N)
        prm = sb("prm", B * PRM_W)
        pcur = sb("pcur", 2 * NB * PRM_W)
        idx = sb("idx", H * NT, U32)
        W_OFF = S * EEW
        A_SUM, A_SQ = 400, 400 + B

        INB, DWW, DWB, OUTB, DBCB, ANEG, DPAR, MOB = 0, 6, 12, 14, 16, 50, 66, 68

        pj = [ctx.enter_context(nc.psum_tensor(f"pj{i}", [P, HALF], F32)) for i in range(4)]
        tp = [ctx.enter_context(nc.psum_tensor(f"tp{i}", [P, HALF], F32)) for i in range(2)]
        sg = ctx.enter_context(nc.psum_tensor("sg", [P, HALF], F32))
        st = ctx.enter_context(nc.psum_tensor("st", [P, HALF], F32))

        def const(name, *dims, off=0, parts=P):
            width = CONST_WIDTHS[name]
            return v(cst, CONST_AT[name] + off, *(dims or ((1, width),)), parts=parts)

        grid_in = sem("grid_in")
        weights_in = sem("weights_in")
        x_in = [[sem(f"x_in{par}{b}") for b in range(NB)] for par in range(2)]
        out_stored = [[sem(f"out_stored{par}{b}") for b in range(NB)] for par in range(2)]
        rows_scattered = sem("rows_scattered")
        x_rows_in = sem("x_rows_in")
        dbc_rows_in = sem("dbc_rows_in")
        c_stored = sem("c_stored")
        crow_in = [sem(f"crow_in{h}") for h in range(H)]
        y_stored = [sem(f"y_stored{h}") for h in range(H)]
        y_gathered = [sem(f"y_gathered{h}") for h in range(H)]
        stats_done = sem("stats_done")
        stats_done_a = sem("stats_done_a")
        setup_v = sem("setup_v")
        setup_a = sem("setup_a")
        setup_p = sem("setup_p")
        setup_g = sem("setup_g")
        params_ready = sem("params_ready")
        ranks_ready = sem("ranks_ready")
        pcur_ready = sem("pcur_ready")
        wa_ready = sem("wa_ready")
        wg_ready = sem("wg_ready")
        wr_ready = sem("wr_ready")
        a_full, a_drained = sem("a_full"), sem("a_drained")
        g_full, g_drained = sem("g_full"), sem("g_drained")
        e_full, e_drained = sem("e_full"), sem("e_drained")
        o_full, o_drained = sem("o_full"), sem("o_drained")
        r_drained = sem("r_drained")
        x_full, x_drained = sem("x_full"), sem("x_drained")
        t_full, t_drained = sem("t_full"), sem("t_drained")
        y_full, y_drained = sem("y_full"), sem("y_drained")
        stage_ready = sem("stage_ready")
        conv_step = [sem(f"conv_step{ct}") for ct in range(CT)]
        xf_ready = sem("xf_ready")
        sp_v = sem("sp_v")
        sp_a = sem("sp_a")
        r_ready = sem("r_ready")
        sg_full = sem("sg_full")
        ee_ready = sem("ee_ready")
        w_ready = sem("w_ready")
        bc_step = sem("bc_step")
        bblk_ready = sem("bblk_ready")
        cblk_ready = sem("cblk_ready")
        m_step = sem("m_step")
        mblk_ready = sem("mblk_ready")
        st_full = sem("st_full")
        hs_ready = sem("hs_ready")
        ch_used = sem("ch_used")
        g_ready = sem("g_ready")
        z_ready = sem("z_ready")
        x1_ready = sem("x1_ready")
        out_ready = sem("out_ready")
        pool_passed = sem("pool_passed")

        A_U, R_U, G_U, E_U, O_U = NB * 4, H * NB * 2, NB * 4, NB * 4, NB * 4
        X_U, T_U, Y_U = NB * NT, H * NB * NT // 2, NB * H * 2
        CH = 4
        AHEAD = 2

        def wait(eng, semaphore, value):
            if isinstance(value, int) and value <= 0:
                return
            eng.wait_ge(semaphore, value)

        def first(i):
            return isinstance(i, int) and i == 0

        def last_phase(i):
            return isinstance(i, int) and i == PH - 1

        def residual_at(i):
            return stage if last_phase(i) else rs

        def phases(eng, cycle):
            cycle(0, 0, 0)
            with eng.Fori(0, (PH - 2) // 2) as t:
                cycle(t * 2 + 1, 1, t)
                cycle(t * 2 + 2, 0, t + 1)
            cycle(PH - 1, 1, PH // 2 - 1)

        def x_view(par, b, ct, off=0, n=N):
            return v(xb[par], (b * CT + ct) * N + off, (1, n))

        x_dram = x_d.rearrange("b (t p) n -> p b t n", p=P)
        out_dram = out_d.rearrange("b (t p) n -> p b t n", p=P)
        block = ctx.enter_context(nc.Block())

        @block.sync
        def _(sp):
            def bcast(src, n):
                return bass.AP(src.tensor, 0, [[0, P], [1, n]])

            def load_x(i, par, b):
                at = i * NB + b
                src = x_dram[:, at:at + 1] if isinstance(at, int) else x_dram[:, bass.ds(at, 1)]
                sp.dma_start(v(xb[par], b * CT * N, (CT * N, 1), (N, CT), (1, N)), src).then_inc(x_in[par][b], 16)

            sp.dma_start(cst[:, :], const_d).then_inc(grid_in, 16)
            sp.dma_start(v(small, MOB, (1, 8)), bcast(mob_d, 8)).then_inc(grid_in, 16)
            for b in range(NB):
                load_x(0, 0, b)
            sp.dma_start(v(small, ANEG, (1, 16)), bcast(alog_d, 16)).then_inc(weights_in, 16)
            sp.dma_start(v(small, DPAR, (1, 2)), bcast(dpar_d, 2)).then_inc(weights_in, 16)
            sp.dma_start(v(small, DBCB, (1, H * K1)), bcast(dbcb_d, H * K1)).then_inc(weights_in, 16)
            sp.dma_start(v(small, INB, (1, 6)), inb_d).then_inc(weights_in, 16)
            sp.dma_start(v(small, DWW, (1, 6)), dww_d).then_inc(weights_in, 16)
            sp.dma_start(v(small, DWB, (1, 2)), dwb_d).then_inc(weights_in, 16)
            sp.dma_start(v(small, OUTB, (1, 2)), outb_d).then_inc(weights_in, 16)
            for b in range(NB):
                load_x(1, 1, b)
            sp.dma_start(v(inw, 0, (3 * C, CT), (1, 3 * C)), inw_d).then_inc(weights_in, 16)
            sp.dma_start(v(outw, 0, (C, CT), (1, C)), outw_d).then_inc(weights_in, 16)
            sp.dma_start(v(dbcw, 0, (H * K1, CT), (1, H * K1)), dbcw_d).then_inc(weights_in, 16)
            sp.dma_start(v(xp, 0, (136, CT), (1, 136)), w1g_d).then_inc(weights_in, 16)
            sp.dma_start(v(xp, 272, (1, 136), parts=1), b1g_d).then_inc(weights_in, 16)
            sp.dma_start(v(xp, 408, (1, C)), w2_d).then_inc(weights_in, 16)
            sp.dma_start(v(xp, 664, (1, C), parts=E), b2_d).then_inc(weights_in, 16)
            for i in range(2, PH + 2):
                sp.wait_ge(stats_done, i - 1)
                sp.wait_ge(stats_done_a, i - 1)
                for b in range(NB):
                    load_x(i % PH, i % 2, b)

            def load_rows(i):
                sp.wait_ge(rows_scattered, 256 * (i + 1))
                if first(i):
                    sp.wait_ge(params_ready, 1)
                else:
                    sp.wait_ge(ch_used, T_U * i)
                for off, width, loaded in ((NB * P, NB * K1, dbc_rows_in), (0, NB * P, x_rows_in)):
                    sp.dma_start(v(xp, off, (ROW, H * NT), (1, width)),
                                 bass.AP(xt_d, off, [[ROW, P], [P * ROW, H * NT], [1, width]])).then_inc(loaded, 16)

            def store_c(i):
                sp.wait_ge(dbc_rows_in, 16 * (i + 1))
                sp.dma_start(bass.AP(cd_d, 0, [[S * NB, P], [P * S * NB, H * NT], [1, S * NB]]),
                             v(xp, NB * (P + 1 + S), (ROW, H * NT), (1, S * NB))).then_inc(c_stored, 16)

            def load_c(i):
                sp.wait_ge(c_stored, 16 * (i + 1))
                run = L * S * NB
                for h in range(H):
                    for c in range(CPT):
                        sp.dma_start(v(crow, h * NT * run, (run, NT), (1, run), parts=L, p0=c * L),
                                     bass.AP(cd_d, (h * NT * CPT + c) * run, [[0, L], [CPT * run, NT], [1, run]])).then_inc(crow_in[h], 16)

            def store_out(i, par, b):
                sp.wait_ge(out_ready, (i * NB + b + 1) * CT)
                at = i * NB + b
                dst = out_dram[:, at:at + 1] if isinstance(at, int) else out_dram[:, bass.ds(at, 1)]
                sp.dma_start(dst, v(xb[par], b * CT * N, (CT * N, 1), (N, CT), (1, N))).then_inc(out_stored[par][b], 16)

            def cycle(i, par, half, more):
                for h in range(H):
                    sp.wait_ge(r_drained, i * R_U + (h + 1) * 4)
                    sp.dma_start(bass.AP(yt_d, h * N * NB * P, [[NB * P, P], [P * NB * P, NT], [1, NB * P]]),
                                 v(rs, h * NT * NB * P, (NB * P, NT), (1, NB * P))).then_inc(y_stored[h], 16)
                if not last_phase(i):
                    load_rows(i + 1)
                    store_c(i + 1)
                store_out(i, par, 0)
                if not last_phase(i):
                    load_c(i + 1)
                store_out(i, par, 1)
                if more:
                    for b in range(NB):
                        sp.wait_ge(out_stored[par][b], 16 * (half + 1))
                        load_x(i + 2, par, b)

            load_rows(0)
            store_c(0)
            load_c(0)
            cycle(0, 0, 0, True)
            with sp.Fori(0, (PH - 4) // 2) as t:
                cycle(t * 2 + 1, 1, t, True)
                cycle(t * 2 + 2, 0, t + 1, True)
            for i in range(PH - 3, PH):
                cycle(i, i % 2, i // 2, i < PH - 2)
            for par in range(2):
                for b in range(NB):
                    sp.wait_ge(out_stored[par][b], 16 * (PH // 2))

        @block.gpsimd
        def _(pool):
            pool.wait_ge(params_ready, 1)

            def hold(semaphore, value):
                if isinstance(value, int) and value <= 0:
                    return
                pool.wait_ge(semaphore, value)
                pool.sem_inc(pool_passed, 1)

            def scaled(par, b, slot, col, ready):
                for ct in range(CT):
                    last = nc.gpsimd.tensor_scalar(v(wsc, (b * CT + ct) * 2 * C + slot * C, (1, C)), v(inw, ct * 3 * C + col, (1, C)),
                                                   v(pcur, (par * NB + b) * PRM_W + PRM_P + ct, (1, 1)), 0.0,
                                                   ALU.mult, ALU.add)
                last.then_inc(ready, 1)

            def weights_x(i, par, b):
                if not first(i):
                    hold(g_full, (i - 1) * G_U + (b + 1) * 4)
                scaled(par, b, 0, 0, wa_ready)

            def weights_gate(i, par, b):
                hold(a_full, i * A_U + (b + 1) * 4)
                scaled(par, b, 0, 2 * C, wg_ready)

            def weights_residual(i, par):
                hold(e_full, i * E_U)
                for b in range(NB):
                    scaled(par, b, 1, C, wr_ready)

            def scatter(i, tiles):
                for nt in tiles:
                    hold(stage_ready, i * NT + nt + 1)
                    if nt == 0:
                        hold(dbc_rows_in, 16 * i)
                        hold(x_rows_in, 16 * i)
                    for h in range(H):
                        k = h * NT + nt
                        pool.indirect_dma_start(
                            out=xt_d.ap(), out_offset=bass.IndirectOffsetOnAxis(ap=idx[:, k:k + 1], axis=0),
                            in_=v(stage, (nt * H + h) * ROW, (1, ROW)), in_offset=None).then_inc(rows_scattered, 16)

            def gather(i, h):
                hold(y_stored[h], 16 * (i + 1))
                if h == 0:
                    hold(mblk_ready, H * (i + 1))
                    hold(hs_ready, H * NB * S * (i + 1))
                for nt in range(NT):
                    k = h * NT + nt
                    pool.indirect_dma_start(
                        out=v(big, k * NB * P, (1, NB * P)), out_offset=None, in_=yt_d.ap()[0:(h + 1) * N],
                        in_offset=bass.IndirectOffsetOnAxis(ap=idx[:, k:k + 1], axis=0)).then_inc(y_gathered[h], 16)

            def weigh(i, h):
                hold(ee_ready, i * H + h + 1)
                hold(crow_in[h], 16 * CPT * (i + 1))
                hold(m_step, (i * H + h) * 3)
                for s in range(S):
                    for b in range(NB):
                        last = nc.gpsimd.tensor_tensor(
                            v(big, W_OFF + (s * Q + b * NT) * L, (L, NT), (1, L)),
                            v(big, s * EEW + SEG + b * NT * L, (L, NT), (1, L)),
                            v(crow, h * NT * L * S * NB + s * NB + b, (L * S * NB, NT), (S * NB, L)), ALU.mult)
                last.then_inc(w_ready, 1)

            def first_tap(i, b):
                for ot in range(CT):
                    hold(a_drained, i * A_U + b * 4 + ot * 2 + 2)
                    hold(x_full, (i * NB + b) * NT)
                    nc.gpsimd.tensor_scalar(v(xf, ot * N, (1, N)), v(xs, ot * (N + 2), (1, N)), v(small, DWW + ot * 3, (1, 1)), 0.0,
                                            ALU.mult, ALU.add).then_inc(conv_step[ot], 1)

            def cycle(i, par, half):
                more = not last_phase(i)
                weigh(i, 0)
                if more:
                    if not first(i):
                        hold(pcur_ready, i + 2)
                        weights_x(i + 1, 1 - par, 0)
                    weights_x(i + 1, 1 - par, 1)
                weights_residual(i, par)
                weigh(i, 1)
                if more:
                    weights_gate(i + 1, 1 - par, 0)
                    weights_gate(i + 1, 1 - par, 1)
                    first_tap(i + 1, 1)
                gather(i, 0)
                if more:
                    scatter(i + 1, range(0, 2))
                gather(i, 1)
                if more:
                    scatter(i + 1, range(2, NT))

            hold(pcur_ready, 1)
            for b in range(NB):
                weights_x(0, 0, b)
            for b in range(NB):
                weights_gate(0, 0, b)
            first_tap(0, 1)
            hold(ranks_ready, 1)
            scatter(0, range(NT))
            hold(pcur_ready, 2)
            weights_x(1, 1, 0)
            phases(pool, cycle)

        @block.scalar
        def _(act):
            def did(ins):
                ins.then_inc(setup_a, 1)

            act.wait_ge(setup_v, V_MOB)
            did(nc.scalar.activation(v(small, MOB + 10, (1, 2)), v(small, MOB + 8, (1, 2)), ACT.Sqrt))

            def statistics(i):
                if i:
                    act.wait_ge(stats_done_a, i)
                for b in range(NB):
                    act.wait_ge(x_in[i % 2][b], 16 * (i // 2 + 1))
                    src = x_view(i % 2, b, 1)
                    unused = lambda k: v(gt, (b * 2 + k) * N, (1, N))
                    nc.scalar.activation(unused(0), src, ACT.Identity, accum_out=v(rs, A_SUM + i * NB + b, (1, 1)))
                    last = nc.scalar.activation(unused(1), src, ACT.Square, accum_out=v(rs, A_SQ + i * NB + b, (1, 1)))
                last.then_inc(stats_done_a, 1)

            statistics(0)
            statistics(1)
            act.wait_ge(setup_g, 1)
            for k in range(4):
                last = nc.scalar.copy(v(crow, k * HALF, (1, HALF)), pj[k][:, :])
            did(last)
            for i in range(2, PH):
                statistics(i)
            act.wait_ge(weights_in, 14 * 16)
            did(nc.scalar.activation(v(small, ANEG, (1, 16)), v(small, ANEG, (1, 16)), ACT.Exp))
            act.wait_ge(setup_v, V_VAR1)
            did(nc.scalar.activation(v(dts, 0, (1, 32)), v(dts, 0, (1, 32)), ACT.Sqrt))
            act.wait_ge(setup_v, V_MAX)
            did(nc.scalar.activation(v(bc8, 0, (1, E), parts=B), v(bc8, 0, (1, E), parts=B), ACT.Exp,
                                     bias=v(bc8, 140, (1, 1), parts=B), accum_out=v(bc8, 141, (1, 1), parts=B)))
            act.wait_ge(setup_p, P_EXPERT)
            did(nc.scalar.activation(v(dts, 96, (1, 32)), v(tp[1], 0, (1, 32)), ACT.Exp, scale=-1.0))
            act.wait_ge(setup_v, V_VAR2)
            did(nc.scalar.activation(v(dts, 0, (1, 32)), v(dts, 0, (1, 32)), ACT.Sqrt))
            act.wait_ge(params_ready, 1)

            def bias(par, b, ot):
                return v(pcur, (par * NB + b) * PRM_W + PRM_BIAS + ot, (1, 1))

            def project(i, par, b, ot):
                act.wait_ge(pcur_ready, i + 1)
                if b or not first(i):
                    act.wait_ge(conv_step[ot], (i * NB + b) * 3)
                for nt in range(2):
                    k = b * 4 + ot * 2 + nt
                    act.wait_ge(a_full, i * A_U + k + 1)
                    nc.scalar.activation(v(xs, ot * (N + 2) + 1 + nt * HALF, (1, HALF)), pj[k % 4][:, :], ACT.Silu,
                                         bias=bias(par, b, ot)).then_inc(a_drained, 1)

            def convolved(i, b):
                for ot in range(CT):
                    act.wait_ge(conv_step[ot], (i * NB + b + 1) * 3)
                    nc.scalar.activation(v(xf, ot * N, (1, N)), v(xf, ot * N, (1, N)), ACT.Silu,
                                         bias=v(small, DWB + ot, (1, 1))).then_inc(xf_ready, 1)

            def softplus(i):
                act.wait_ge(sp_v, i * 9 + 1)
                nc.scalar.activation(v(dts, 32, (1, 32)), v(dts, 0, (1, 32)), ACT.Exp, scale=-1.0).then_inc(sp_a, 1)
                act.wait_ge(sp_v, i * 9 + 2)
                nc.scalar.activation(v(dts, 96, (1, 32)), v(dts, 64, (1, 32)), ACT.Ln).then_inc(sp_a, 1)

            def decays(i, h):
                act.wait_ge(sg_full, i * H + h + 1)
                if h == 0:
                    wait(act, y_full, i * Y_U)
                else:
                    act.wait_ge(w_ready, i * H + h)
                    act.wait_ge(hs_ready, (i * H + h) * NB * S)
                for s in range(S):
                    last = nc.scalar.activation(v(big, s * EEW, (1, EEW)), v(sg, 0, (1, EEW)), ACT.Exp,
                                                scale=v(small, ANEG + h * S + s, (1, 1)))
                last.then_inc(ee_ready, 1)

            def rows_out(i, b):
                if b == 0:
                    wait(act, rows_scattered, 256 * i)
                for nt in range(NT):
                    act.wait_ge(x_full, i * X_U + b * NT + nt + 1)
                    o = nt * H * ROW
                    nc.scalar.copy(v(stage, o + b * P, (ROW, H), (1, P)), v(tp[nt % 2], 0, (P, H), (1, P)))
                    nc.scalar.copy(v(stage, o + NB * P + b, (ROW, H), (NB, K1)),
                                   v(tp[nt % 2], 2 * P, (K1, H), (1, K1))).then_inc(x_drained, 1)

            def turned(i, h, ks):
                for k in ks:
                    u = h * 8 + k
                    act.wait_ge(t_full, i * T_U + u + 1)
                    wait(act, ch_used, i * T_U + u + 1 - CH)
                    nc.scalar.copy(v(ch, (u % CH) * 2 * P, (1, 2 * P)), v(tp[u % 2], 0, (1, 2 * P))).then_inc(t_drained, 1)

            def result(i, h, b):
                if h == 0 and b == 0:
                    wait(act, out_ready, i * NB * CT)
                act.wait_ge(ch_used, i * T_U + (h * NB + b) * 4 + 4)
                for e in range(2):
                    k = (h * NB + b) * 2 + e
                    nc.scalar.copy(v(rs, (h * NT + e) * NB * P + b * P, (2 * NB * P, 4), (1, P)),
                                   v(pj[k % 4], 0, (P, 4), (1, P))).then_inc(r_drained, 1)

            def results(i, h, turned_before=0):
                turned(i, h, range(turned_before, 4 + AHEAD))
                result(i, h, 0)
                turned(i, h, range(4 + AHEAD, 8))
                result(i, h, 1)

            def gate(i, par, units):
                for k in units:
                    b, ct, nt = k // 4, k // 2 % 2, k % 2
                    if k == 0:
                        wait(act, o_full, i * O_U)
                    act.wait_ge(g_full, i * G_U + k + 1)
                    nc.scalar.activation(v(gt, (b * CT + ct) * N + nt * HALF, (1, HALF)), pj[k % 4][:, :], ACT.Silu,
                                         bias=bias(par, b, 4 + ct)).then_inc(g_drained, 1)

            def gate_again(i, b, ct):
                act.wait_ge(g_drained, i * G_U + b * 4 + ct * 2 + 2)
                g = v(gt, (b * CT + ct) * N, (1, N))
                nc.scalar.activation(g, g, ACT.Silu).then_inc(g_ready, 1)

            def residual(i, par, units=range(E_U)):
                if not last_phase(i):
                    for h in range(H):
                        act.wait_ge(y_stored[h], 16 * (i + 1))
                elif units[0] == 0:
                    act.wait_ge(rows_scattered, 256 * PH)
                for k in units:
                    ct, b, nt = k // 4, k // 2 % 2, k % 2
                    act.wait_ge(e_full, i * E_U + k + 1)
                    nc.scalar.activation(v(residual_at(i), (b * CT + ct) * N + nt * HALF, (1, HALF)), pj[k % 4][:, :], ACT.Silu,
                                         bias=bias(par, b, 2 + ct)).then_inc(e_drained, 1)

            def x_again(i, par):
                for b in range(NB):
                    o = (par * NB + b) * PRM_W
                    for ct in range(CT):
                        last = nc.scalar.activation(x_view(par, b, ct), x_view(par, b, ct), ACT.Identity,
                                                    bias=v(pcur, o + PRM_B + ct, (1, 1)), scale=v(pcur, o + PRM_A + ct, (1, 1)))
                    last.then_inc(x1_ready, 1)

            def output(i, b):
                act.wait_ge(z_ready, i * 4 + 3 + b)
                for ot in range(CT):
                    for nt in range(2):
                        k = b * 4 + ot * 2 + nt
                        act.wait_ge(o_full, i * O_U + k + 1)
                        nc.scalar.activation(v(rs, (b * CT + ot) * N + nt * HALF, (1, HALF)), pj[k % 4][:, :], ACT.Silu,
                                             bias=v(small, OUTB + ot, (1, 1))).then_inc(o_drained, 1)

            def cycle(i, par, half):
                more = not last_phase(i)
                decays(i, 0)
                if not first(i):
                    for k in range(2):
                        gate(i, par, range(2 * k, 2 * k + 2))
                        gate_again(i, 0, k)
                    gate(i, par, range(4, 6))
                decays(i, 1)
                if not first(i):
                    gate(i, par, range(6, 8))
                turned(i, 0, range(0, AHEAD))
                if not more:
                    residual(i, par, range(0, 4))
                if more:
                    for ot in range(CT):
                        project(i + 1, 1 - par, 0, ot)
                results(i, 0, AHEAD)
                if more:
                    convolved(i + 1, 0)
                    rows_out(i + 1, 0)
                    for ot in range(CT):
                        project(i + 1, 1 - par, 1, ot)
                if not more:
                    residual(i, par, range(4, 8))
                turned(i, 1, range(0, 4 + AHEAD))
                result(i, 1, 0)
                if more:
                    convolved(i + 1, 1)
                turned(i, 1, range(4 + AHEAD, 8))
                result(i, 1, 1)
                if more:
                    rows_out(i + 1, 1)
                for ct in range(CT):
                    gate_again(i, 1, ct)
                if more:
                    residual(i, par)
                x_again(i, par)
                output(i, 0)
                if more:
                    softplus(i + 1)
                output(i, 1)

            for ot in range(CT):
                project(0, 0, 0, ot)
            convolved(0, 0)
            for ot in range(CT):
                project(0, 0, 1, ot)
            rows_out(0, 0)
            gate(0, 0, range(0, 4))
            convolved(0, 1)
            rows_out(0, 1)
            gate(0, 0, range(4, 8))
            for ct in range(CT):
                gate_again(0, 0, ct)
            softplus(0)
            phases(act, cycle)

        @block.vector
        def _(dve):
            n = [0]

            def link(ins):
                n[0] += 1
                ins.then_inc(setup_v, 1)
                dve.wait_ge(setup_v, n[0])

            def mark(number):
                assert n[0] == number, n[0]

            nc.vector.memset(v(xs, 0, (N + 2, CT), (1, 1)), 0.0)
            nc.vector.memset(v(xs, N + 1, (N + 2, CT), (1, 1)), 0.0)
            link(nc.vector.memset(v(hs, 0, ((NC + 1) * S, NB), (1, S)), 0.0))

            dve.wait_ge(grid_in, 2 * 16)
            m = MOB
            link(nc.vector.tensor_tensor(v(small, m + 8, (1, 2)), v(small, m, (4, 2)), v(small, m + 3, (4, 2)), ALU.mult))
            link(nc.vector.tensor_tensor(v(small, m + 10, (1, 2)), v(small, m + 1, (4, 2)), v(small, m + 2, (4, 2)), ALU.mult))
            link(nc.vector.tensor_tensor(v(small, m + 8, (1, 2)), v(small, m + 8, (1, 2)), v(small, m + 10, (1, 2)), ALU.subtract))
            link(nc.vector.scalar_tensor_tensor(v(small, m + 8, (1, 2)), v(small, m + 8, (1, 2)), -1.0, v(small, m + 8, (1, 2)), ALU.mult, ALU.max))
            link(nc.vector.tensor_scalar(v(small, m + 8, (1, 2)), v(small, m + 8, (1, 2)), 1e-3, None, ALU.max))
            mark(V_MOB)
            dve.wait_ge(setup_a, 1)
            link(nc.vector.reciprocal(v(small, m + 12, (1, 2)), v(small, m + 10, (1, 2))))
            for h in range(H):
                link(nc.vector.tensor_scalar(v(small, m + 4 * h, (1, 4)), v(small, m + 4 * h, (1, 4)), v(small, m + 12 + h, (1, 1)), None, ALU.mult))
            link(nc.vector.tensor_scalar(v(small, m + 3, (4, 2)), v(small, m + 3, (4, 2)), 1e-6, None, ALU.add))
            def t8(k):
                return v(bc8, k * NT, (1, NT))

            gx, gy = const("gridcol", (1, NT)), const("gridcol", (1, NT), off=NT)
            nr, ni, dr, di, t0, t1, den, num = (t8(k) for k in range(8))
            def score(h):
                a_, b_, c_, d_ = (v(small, m + 4 * h + k, (1, 1)) for k in range(4))
                nc.vector.tensor_scalar(nr, gx, a_, b_, ALU.mult, ALU.add)
                nc.vector.tensor_scalar(ni, gy, a_, None, ALU.mult)
                nc.vector.tensor_scalar(dr, gx, c_, d_, ALU.mult, ALU.add)
                link(nc.vector.tensor_scalar(di, gy, c_, None, ALU.mult))
                nc.vector.tensor_tensor(t0, dr, dr, ALU.mult)
                link(nc.vector.tensor_tensor(t1, di, di, ALU.mult))
                link(nc.vector.tensor_tensor(den, t0, t1, ALU.add))
                nc.vector.tensor_tensor(t0, nr, dr, ALU.mult)
                link(nc.vector.tensor_tensor(t1, ni, di, ALU.mult))
                link(nc.vector.tensor_tensor(num, t0, t1, ALU.add))
                nc.vector.tensor_tensor(t0, ni, dr, ALU.mult)
                link(nc.vector.tensor_tensor(t1, nr, di, ALU.mult))
                link(nc.vector.tensor_tensor(t0, t0, t1, ALU.subtract))
                link(nc.vector.scalar_tensor_tensor(num, t0, 1.3, num, ALU.mult, ALU.add))
                link(nc.vector.reciprocal(den, den))
                link(nc.vector.tensor_tensor(num, num, den, ALU.mult))
                link(nc.vector.tensor_scalar(num, num, 3.4e38, -3.4e38, ALU.min, ALU.max))
                link(nc.vector.tensor_tensor(v(big, h * N, (P, NT), (1, P)), v(bc8, 7 * NT, (1, NT), (0, P)),
                                             const("ident", (0, NT), (1, P)), ALU.mult))
            def statistics(i):
                for b in range(NB):
                    dve.wait_ge(x_in[i % 2][b], 16 * (i // 2 + 1))
                    for half in range(2):
                        last = nc.vector.bn_stats(v(rs, (i * NB + b) * 12 + half * 6, (1, 6)), x_view(i % 2, b, 0, half * HALF, HALF))
                last.then_inc(stats_done, 1)

            link(nc.vector.memset(v(rs, 0, (1, CT * B * 12)), 0.0))
            score(0)
            statistics(0)
            score(1)
            mark(V_DIAG)
            statistics(1)
            statistics(2)
            dve.wait_ge(setup_a, 2)
            MINE = 4 * H * NT
            for k in range(H * NT):
                nc.vector.scalar_tensor_tensor(v(mblk, k * P, (1, P)), v(crow, k * P, (1, P)), 1.0, const("ident"),
                                               ALU.mult, ALU.mult, accum_out=v(m16, MINE + k, (1, 1)))
            link(nc.vector.memset(v(m16, 0, (1, 4 * H * NT)), 0.0))

            def rank(h, nt):
                mine = v(m16, MINE + h * NT + nt, (1, 1))

                def span(lo, hi):
                    return v(crow, h * N + lo, (1, hi - lo))

                def count(k):
                    return v(m16, (h * NT + nt) * 4 + k, (1, 1))

                lo, hi = nt * P, nt * P + P
                if nt:
                    nc.vector.tensor_scalar(v(mblk, 0, (1, lo)), span(0, lo), mine, None, ALU.is_le, ALU.add, accum_out=count(0))
                if nt < NT - 1:
                    nc.vector.tensor_scalar(v(mblk, N - P, (1, N - hi)), span(hi, N), mine, None, ALU.is_lt, ALU.add, accum_out=count(1))
                nc.vector.scalar_tensor_tensor(v(mblk, 2 * (N - P), (1, P)), span(lo, hi), mine, const("before"), ALU.is_le, ALU.mult, accum_out=count(2))
                link(nc.vector.scalar_tensor_tensor(v(mblk, 2 * N - P, (1, P)), span(lo, hi), mine, const("notbefore"), ALU.is_lt, ALU.mult, accum_out=count(3)))

            tiles = iter([(h, nt) for h in range(H) for nt in range(NT)])
            for i in range(3, PH):
                for _ in range(1 if i == 3 else 2):
                    rank(*next(tiles))
                statistics(i)
            dve.wait_ge(stats_done, PH)
            U = CT * B
            MEAN, SQ, T = 1024, 1024 + U, 1024 + 2 * U
            col = lambda off: v(rs, off, (1, U))
            link(nc.vector.tensor_reduce(col(MEAN), v(rs, 1, (12, U), (3, 4)), AX.X, ALU.add))
            link(nc.vector.tensor_scalar(col(MEAN), col(MEAN), 0.25, None, ALU.mult))
            link(nc.vector.tensor_tensor(v(rs, 1200, (4, U), (1, 4)), v(rs, 1, (12, U), (3, 4)), v(rs, 1, (12, U), (3, 4)), ALU.mult))
            link(nc.vector.tensor_reduce(col(SQ), v(rs, 1200, (4, U), (1, 4)), AX.X, ALU.add))
            link(nc.vector.tensor_reduce(col(T), v(rs, 2, (12, U), (3, 4)), AX.X, ALU.add))
            link(nc.vector.tensor_scalar(col(T), col(T), 1.0 / N, None, ALU.mult))
            link(nc.vector.scalar_tensor_tensor(col(SQ), col(SQ), 0.25, col(T), ALU.mult, ALU.add))
            dve.wait_ge(setup_a, 3)
            link(nc.vector.tensor_scalar(v(small, ANEG, (1, 16)), v(small, ANEG, (1, 16)), -1.0, None, ALU.mult))
            dve.wait_ge(stats_done_a, PH)
            nc.vector.tensor_scalar(v(rs, MEAN + B, (1, B)), v(rs, A_SUM, (1, B)), 1.0 / N, None, ALU.mult)
            link(nc.vector.tensor_scalar(v(rs, SQ + B, (1, B)), v(rs, A_SQ, (1, B)), 1.0 / N, None, ALU.mult))
            mark(V_STATS)

            def group_variance():
                link(nc.vector.tensor_copy(v(dts, 32, (1, U)), v(tp[0], 0, (1, U))))
                link(nc.vector.tensor_tensor(v(dts, 64, (1, U)), v(dts, 32, (1, U)), v(dts, 32, (1, U)), ALU.mult))
                link(nc.vector.tensor_tensor(v(dts, 0, (1, U)), v(tp[0], U, (1, U)), v(dts, 64, (1, U)), ALU.subtract))
                link(nc.vector.tensor_scalar(v(dts, 0, (1, U)), v(dts, 0, (1, U)), 0.0, EPS, ALU.max, ALU.add))

            MG, RSTD = v(dts, 32, (1, U)), v(dts, 128, (1, U))
            dve.wait_ge(setup_p, 1)
            group_variance()
            mark(V_VAR1)
            rank(*next(tiles))
            dve.wait_ge(setup_a, 4)
            link(nc.vector.reciprocal(RSTD, v(dts, 0, (1, U))))
            link(nc.vector.tensor_tensor(col(T), col(MEAN), MG, ALU.subtract))
            link(nc.vector.tensor_tensor(col(T), col(T), RSTD, ALU.mult))
            mark(V_Y)
            dve.wait_ge(setup_p, 2)
            link(nc.vector.tensor_copy(v(bc8, 0, (1, 136), parts=B), v(tp[1], 0, (1, 136), parts=B)))
            link(nc.vector.reduce_max(v(bc8, 140, (1, 1), parts=B), v(bc8, 0, (1, E), parts=B), AX.X))
            link(nc.vector.tensor_scalar(v(bc8, 140, (1, 1), parts=B), v(bc8, 140, (1, 1), parts=B), -1.0, None, ALU.mult))
            mark(V_MAX)
            rank(*next(tiles))
            dve.wait_ge(setup_a, 5)
            link(nc.vector.reciprocal(v(bc8, 142, (1, 1), parts=B), v(bc8, 141, (1, 1), parts=B)))
            link(nc.vector.tensor_scalar(v(bc8, 0, (1, E), parts=B), v(bc8, 0, (1, E), parts=B), v(bc8, 142, (1, 1), parts=B), None, ALU.mult))
            link(nc.vector.scalar_tensor_tensor(v(bc8, 8, (R, E), (1, R), parts=B), v(bc8, 8, (R, E), (1, R), parts=B), 0.0,
                                                v(bc8, 0, (1, E), (0, R), parts=B), ALU.max, ALU.mult))
            mark(V_HID)
            dve.wait_ge(setup_p, 3)
            nc.vector.tensor_copy(v(bc8, 160, (1, B)), v(tp[0], 0, (1, B)))
            link(nc.vector.tensor_copy(v(bc8, 180, (1, B), parts=E), v(tp[0], P, (1, B), parts=E)))
            mark(V_HIDT)
            rank(*next(tiles))
            dve.wait_ge(setup_a, 6)
            SC, A_, B_ = v(dts, 96, (1, U)), v(dts, 160, (1, U)), v(dts, 192, (1, U))
            link(nc.vector.tensor_scalar(SC, SC, 1.0, None, ALU.add))
            link(nc.vector.reciprocal(SC, SC))
            link(nc.vector.tensor_tensor(SC, SC, RSTD, ALU.mult))
            link(nc.vector.tensor_scalar(A_, SC, 1.0, None, ALU.add))
            link(nc.vector.tensor_tensor(B_, SC, MG, ALU.mult))
            link(nc.vector.tensor_scalar(B_, B_, -1.0, None, ALU.mult))
            link(nc.vector.tensor_tensor(col(T), col(MEAN), col(MEAN), ALU.mult))
            link(nc.vector.tensor_tensor(col(SQ), col(SQ), col(T), ALU.subtract))
            link(nc.vector.tensor_tensor(col(SQ), col(SQ), A_, ALU.mult))
            link(nc.vector.tensor_tensor(col(SQ), col(SQ), A_, ALU.mult))
            link(nc.vector.tensor_tensor(col(MEAN), col(MEAN), A_, ALU.mult))
            link(nc.vector.tensor_tensor(col(MEAN), col(MEAN), B_, ALU.add))
            link(nc.vector.tensor_tensor(col(T), col(MEAN), col(MEAN), ALU.mult))
            link(nc.vector.tensor_tensor(col(SQ), col(SQ), col(T), ALU.add))
            mark(V_STATS2)
            dve.wait_ge(setup_p, 5)
            group_variance()
            mark(V_VAR2)
            dve.wait_ge(setup_a, 7)
            link(nc.vector.reciprocal(RSTD, v(dts, 0, (1, U))))
            link(nc.vector.tensor_tensor(SC, B_, MG, ALU.subtract))
            link(nc.vector.tensor_tensor(col(T), SC, RSTD, ALU.mult))
            mark(V_Q)
            per_image = lambda off: v(prm, off, (1, CT), (PRM_W, B))
            nc.vector.tensor_tensor(per_image(PRM_P), v(dts, 128, (B, CT), (1, B)), v(dts, 160, (B, CT), (1, B)), ALU.mult)
            nc.vector.tensor_copy(per_image(PRM_A), v(dts, 160, (B, CT), (1, B)))
            nc.vector.tensor_copy(per_image(PRM_B), v(dts, 192, (B, CT), (1, B)))
            dve.wait_ge(setup_p, 6)
            link(nc.vector.tensor_tensor(v(prm, PRM_BIAS, (1, 6), (PRM_W, B)), v(tp[1], 0, (B, 6), (1, B)),
                                         v(small, INB, (1, 6), (0, B)), ALU.add))
            nc.vector.memset(v(gt, 0, (1, 1)), 0.0).then_inc(params_ready, 1)

            def take_params(i, par):
                if not (isinstance(i, int) and i < 2):
                    dve.wait_ge(x1_ready, (i - 1) * NB)
                    dve.wait_ge(e_drained, (i - 1) * E_U)
                src = (v(prm, i * NB * PRM_W, (1, NB * PRM_W)) if isinstance(i, int)
                       else prm[:, bass.ds(i * (NB * PRM_W), NB * PRM_W)])
                nc.vector.tensor_copy(v(pcur, par * NB * PRM_W, (1, NB * PRM_W)), src).then_inc(pcur_ready, 1)

            def convolve(i, b):
                for ot in range(CT):
                    step = (i * NB + b) * 3
                    dst = v(xf, ot * N, (1, N))
                    tap = lambda k: v(xs, ot * (N + 2) + k, (1, N))
                    wt = lambda k: v(small, DWW + ot * 3 + k, (1, 1))
                    if b == 0:
                        dve.wait_ge(a_drained, i * A_U + ot * 2 + 2)
                        wait(dve, x_full, i * X_U)
                        nc.vector.tensor_scalar(dst, tap(0), wt(0), None, ALU.mult).then_inc(conv_step[ot], 1)
                    for k in (1, 2):
                        dve.wait_ge(conv_step[ot], step + k)
                        nc.vector.scalar_tensor_tensor(dst, tap(k), wt(k), dst, ALU.mult, ALU.add).then_inc(conv_step[ot], 1)

            def add_bias(i):
                for nt in range(NT):
                    dve.wait_ge(x_drained, i * X_U + NT + nt + 1)
                    d = v(stage, nt * H * ROW + NB * P, (ROW, H), (NB, K1), (1, NB))
                    nc.vector.tensor_tensor(d, d, v(small, DBCB, (K1, H), (1, K1), (0, NB)), ALU.add).then_inc(stage_ready, 1)

            HQ = H * Q
            AXO, UO, WO, LO, MO, DO = 0, 32, 64, 96, 128, 192
            DB, DBE, CS = 0, Q * S, 2 * Q * S

            def part(h, off):
                return h * NT * ROW + NB * P + off

            def softplus(i):
                d = lambda off: v(dts, off, (1, HQ))
                s0 = i * 9
                dve.wait_ge(dbc_rows_in, 16 * (i + 1))
                wait(dve, sg_full, i * H)
                for h in range(H):
                    raw = v(xp, part(h, 0), (1, NB), (ROW, NT))
                    last = nc.vector.scalar_tensor_tensor(v(dts, AXO + h * Q, (NT, NB), (1, NT)), raw, -1.0, raw, ALU.mult, ALU.max)
                last.then_inc(sp_v, 1)
                dve.wait_ge(sp_a, i * 2 + 1)
                nc.vector.tensor_scalar(d(WO), d(UO), 1.0, None, ALU.add).then_inc(sp_v, 1)
                dve.wait_ge(sp_v, s0 + 2)
                nc.vector.tensor_scalar(d(MO), d(WO), 1.0, None, ALU.is_equal).then_inc(sp_v, 1)
                dve.wait_ge(sp_v, s0 + 3)
                dve.wait_ge(sp_a, i * 2 + 2)
                nc.vector.tensor_tensor(d(LO), d(LO), d(MO), ALU.add).then_inc(sp_v, 1)
                nc.vector.scalar_tensor_tensor(d(WO), d(WO), -1.0, d(MO), ALU.add, ALU.add).then_inc(sp_v, 1)
                dve.wait_ge(sp_v, s0 + 5)
                nc.vector.reciprocal(d(WO), d(WO)).then_inc(sp_v, 1)
                dve.wait_ge(sp_v, s0 + 6)
                nc.vector.tensor_tensor(d(LO), d(LO), d(WO), ALU.mult).then_inc(sp_v, 1)
                dve.wait_ge(sp_v, s0 + 7)
                nc.vector.tensor_tensor(d(LO), d(LO), d(UO), ALU.mult).then_inc(sp_v, 1)
                dve.wait_ge(sp_v, s0 + 8)
                for h in range(H):
                    last = nc.vector.scalar_tensor_tensor(
                        v(dts, DO + h * Q, (NT, NB), (1, NT)), v(xp, part(h, 0), (1, NB), (ROW, NT)), 0.0,
                        v(dts, LO + h * Q, (NT, NB), (1, NT)), ALU.max, ALU.add)
                last.then_inc(sp_v, 1)
                dve.wait_ge(sp_v, s0 + 9)
                nc.vector.tensor_tensor(v(rseg, 0, (L, HQ), (1, L)), v(dts, DO, (1, HQ), (0, L)),
                                        const("fromstart", (0, HQ), (1, L)), ALU.mult).then_inc(r_ready, 1)
                nc.vector.tensor_tensor(v(rtot, 0, (CPT, HQ), (1, CPT)), v(dts, DO, (1, HQ), (0, CPT)),
                                        const("chunk", (0, HQ), (1, CPT)), ALU.mult).then_inc(r_ready, 1)

            def scans(i, h, b):
                ih = i * H + h
                dve.wait_ge(st_full, ih * NB + b + 1)
                wait(dve, t_full, (ih - 1) * 8 + (b + 1) * 4)
                for s in range(S):
                    nc.vector.tensor_tensor_scan(
                        v(hs, (b * (NC + 1) + 1) * S + s, (S, NC)), v(big, s * EEW + TOT + b * NC, (1, NC)),
                        v(st, s, (S, NC)), 0.0, ALU.mult, ALU.add).then_inc(hs_ready, 1)

            def factors(i, h):
                ih = i * H + h
                for b in range(NB):
                    last = nc.vector.tensor_tensor(
                        v(bc8, DB + b * NT * S, (S, NT), (1, S)), v(xp, part(h, NB + b), (ROW, NT), (NB, S)),
                        v(dts, DO + h * Q + b * NT, (1, NT), (0, S)), ALU.mult)
                last.then_inc(bc_step, 1)
                dve.wait_ge(ee_ready, ih + 1)
                dve.wait_ge(bc_step, ih * 3 + 1)
                nc.vector.tensor_tensor(v(bc8, DBE, (S, Q), (1, S)), v(bc8, DB, (S, Q), (1, S)),
                                        v(big, SEG + L - 1, (L, Q), (EEW, S)), ALU.mult).then_inc(bc_step, 1)
                for b in range(NB):
                    last = nc.vector.tensor_tensor(
                        v(bc8, CS + b * NT * S, (S, NT), (1, S)), v(xp, part(h, NB * (1 + S) + b), (ROW, NT), (NB, S)),
                        v(big, CUM + b * NT, (1, NT), (EEW, S)), ALU.mult)
                last.then_inc(bc_step, 1)
                wait(dve, st_full, ih * NB)
                dve.wait_ge(bc_step, ih * 3 + 2)
                nc.vector.tensor_tensor(v(bblk, 0, (CPT * S, Q), (S, CPT), (1, S)), v(bc8, DBE, (S, Q), (0, CPT), (1, S)),
                                        const("chunk", (0, Q), (1, CPT), (0, S)), ALU.mult).then_inc(bblk_ready, 1)

            def turned_factors(i, h):
                ih = i * H + h
                dve.wait_ge(bc_step, ih * 3 + 3)
                wait(dve, t_full, ih * 8)
                nc.vector.tensor_tensor(v(cblk, 0, (CPT * S, Q), (S, CPT), (1, S)), v(bc8, CS, (S, Q), (0, CPT), (1, S)),
                                        const("chunk", (0, Q), (1, CPT), (0, S)), ALU.mult).then_inc(cblk_ready, 1)

            def token_weights(i, h):
                ih = i * H + h
                dve.wait_ge(w_ready, ih + 1)
                W = v(big, W_OFF, (Q * L, S), (L, Q), (1, L))
                nc.vector.tensor_tensor(W, W, v(bc8, DB, (1, S), (S, Q), (0, L)), ALU.mult).then_inc(m_step, 1)
                dve.wait_ge(m_step, ih * 3 + 1)
                nc.vector.tensor_reduce(m16[:, :], v(big, W_OFF, (1, Q * L), (Q * L, S)), AX.X, ALU.add).then_inc(m_step, 1)
                dve.wait_ge(m_step, ih * 3 + 2)
                nc.vector.scalar_tensor_tensor(v(m16, 0, (L, Q), (1, L)), const("diag", (0, Q), (1, L)),
                                               v(small, DPAR + h, (1, 1)), v(m16, 0, (L, Q), (1, L)),
                                               ALU.mult, ALU.add).then_inc(m_step, 1)
                dve.wait_ge(m_step, ih * 3 + 3)
                wait(dve, ch_used, ih * 8)
                nc.vector.tensor_tensor(v(mblk, 0, (P, Q), (L, CPT), (1, L)), v(m16, 0, (L, Q), (0, CPT), (1, L)),
                                        const("causal", (0, Q), (L, CPT), (1, L)), ALU.mult).then_inc(mblk_ready, 1)

            def gated(i, h, b):
                dve.wait_ge(g_ready, (i * NB + b) * CT + h + 1)
                for nq in range(2):
                    k = (h * NB + b) * 2 + nq
                    dve.wait_ge(y_full, i * Y_U + k + 1)
                    half_gate = v(gt, (b * CT + h) * N + nq * HALF, (1, HALF))
                    nc.vector.tensor_tensor(half_gate, v(tp[k % 2], 0, (1, HALF)), half_gate, ALU.mult).then_inc(y_drained, 1)

            def add_residual(i, h, b):
                o = (b * CT + h) * N
                dve.wait_ge(y_drained, i * Y_U + h * 4 + b * 2 + 2)
                dve.wait_ge(e_drained, i * E_U + h * 4 + b * 2 + 2)
                nc.vector.tensor_tensor(v(gt, o, (1, N)), v(gt, o, (1, N)), v(residual_at(i), o, (1, N)), ALU.add).then_inc(z_ready, 1)

            def output(i, par, b):
                dve.wait_ge(x1_ready, i * NB + b + 1)
                for ot in range(CT):
                    dve.wait_ge(o_drained, i * O_U + b * 4 + ot * 2 + 2)
                    nc.vector.tensor_tensor(x_view(par, b, ot), x_view(par, b, ot), v(rs, (b * CT + ot) * N, (1, N)),
                                            ALU.add).then_inc(out_ready, 1)

            def cycle(i, par, half):
                more = not last_phase(i)
                if more and not first(i):
                    take_params(i + 1, 1 - par)
                factors(i, 0)
                turned_factors(i, 0)
                scans(i, 0, 0)
                scans(i, 0, 1)
                token_weights(i, 0)
                factors(i, 1)
                if more:
                    convolve(i + 1, 0)
                turned_factors(i, 1)
                scans(i, 1, 0)
                token_weights(i, 1)
                scans(i, 1, 1)
                if more:
                    convolve(i + 1, 1)
                    add_bias(i + 1)
                for b in range(NB):
                    gated(i, 0, b)
                for b in range(NB):
                    add_residual(i, 0, b)
                for b in range(NB):
                    gated(i, 1, b)
                    add_residual(i, 1, b)
                output(i, par, 0)
                if more:
                    softplus(i + 1)
                output(i, par, 1)

            take_params(0, 0)
            convolve(0, 0)
            for tile in tiles:
                rank(*tile)
            link(nc.vector.tensor_reduce(v(bblk, 0, (1, H * NT)), v(m16, 0, (4, H * NT), (1, 4)), AX.X, ALU.add))
            nc.vector.tensor_scalar(v(idx, 0, (1, NT)), v(bblk, 0, (1, NT)), 0.0, None, ALU.add)
            nc.vector.tensor_scalar(v(idx, NT, (1, NT)), v(bblk, NT, (1, NT)), float(N), None, ALU.add).then_inc(ranks_ready, 1)
            convolve(0, 1)
            add_bias(0)
            take_params(1, 1)
            softplus(0)
            phases(dve, cycle)

        @block.tensor
        def _(pe):
            U = CT * B
            MEAN, T = 1024, 1024 + 2 * U
            pe.wait_ge(setup_v, V_DIAG)
            for k in range(4):
                last = nc.tensor.matmul(pj[k][:, :], const("ones"), v(big, k * HALF, (1, HALF)), start=True, stop=True)
            last.then_inc(setup_g, 1)
            pe.wait_ge(weights_in, 14 * 16)
            pe.wait_ge(setup_v, V_STATS)
            nc.tensor.matmul(v(tp[0], 0, (1, 2 * U)), const("group"), v(rs, MEAN, (1, 2 * U)), start=True, stop=True).then_inc(setup_p, 1)
            pe.wait_ge(setup_v, V_Y)
            for ct in range(CT):
                nc.tensor.matmul(v(tp[1], 0, (1, 136), parts=B), v(rs, T + ct * B, (1, B)), v(xp, ct * 136, (1, 136)), start=(ct == 0), stop=False)
            nc.tensor.matmul(v(tp[1], 0, (1, 136), parts=B), const("ones", (1, B), parts=1), v(xp, 272, (1, 136), parts=1),
                             start=False, stop=True).then_inc(setup_p, 1)
            pe.wait_ge(setup_v, V_HID)
            ident16 = const("ident", (1, B), parts=B)
            nc.tensor.transpose(v(tp[0], 0, (1, B)), v(bc8, 8, (1, P), parts=B), ident16)
            nc.tensor.transpose(v(tp[0], P, (1, B), parts=E), v(bc8, 0, (1, E), parts=B), ident16).then_inc(setup_p, 1)
            pe.wait_ge(setup_v, V_HIDT)
            for ct in range(CT):
                o = v(tp[1], ct * B, (1, B))
                nc.tensor.matmul(o, v(xp, 408 + ct * P, (1, P)), v(bc8, 160, (1, B)), start=True, stop=False)
                last = nc.tensor.matmul(o, v(xp, 664 + ct * P, (1, P), parts=E), v(bc8, 180, (1, B), parts=E), start=False, stop=True)
            last.then_inc(setup_p, 1)
            pe.wait_ge(setup_v, V_STATS2)
            nc.tensor.matmul(v(tp[0], 0, (1, 2 * U)), const("group"), v(rs, MEAN, (1, 2 * U)), start=True, stop=True).then_inc(setup_p, 1)
            pe.wait_ge(setup_v, V_Q)
            for ot in range(6):
                for ct in range(CT):
                    last = nc.tensor.matmul(v(tp[1], ot * B, (1, B)), v(inw, ct * 3 * C + ot * P, (1, P)),
                                            v(rs, T + ct * B, (1, B)), start=(ct == 0), stop=(ct == CT - 1))
            last.then_inc(setup_p, 1)
            pe.wait_ge(params_ready, 1)

            def pj_slot(k, own, own_base, before):
                if k < 4:
                    if before:
                        wait(pe, before[0], before[1] - 3 + k)
                else:
                    pe.wait_ge(own, own_base + k - 3)
                return pj[k % 4]

            def tp_slot(k, own, own_base, before):
                if k < 2:
                    if before:
                        wait(pe, before[0], before[1] - 1 + k)
                else:
                    pe.wait_ge(own, own_base + k - 1)
                return tp[k % 2]

            def part(o, par, b, slot, ot, nt):
                for ct in range(CT):
                    last = nc.tensor.matmul(o[:, :], v(wsc, (b * CT + ct) * 2 * C + slot * C + ot * P, (1, P)),
                                            x_view(par, b, ct, nt * HALF, HALF), start=(ct == 0), stop=(ct == CT - 1))
                return last

            def project(i, par, half, b, before, units=range(4)):
                for k in units:
                    if k == 0:
                        pe.wait_ge(x_in[par][b], 16 * (PH // 2 + half + 1))
                        pe.wait_ge(wa_ready, i * NB + b + 1)
                    o = pj_slot(k, a_drained, i * A_U + b * 4, before)
                    part(o, par, b, 0, k // 2, k % 2).then_inc(a_full, 1)

            def rows(i, b, before, tiles=range(NT)):
                pe.wait_ge(xf_ready, (i * NB + b + 1) * CT)
                for nt in tiles:
                    o = tp_slot(nt, x_drained, i * X_U + b * NT, before)
                    tile = lambda ct: v(xf, ct * N + nt * P, (1, P))
                    for ct in range(CT):
                        nc.tensor.transpose(v(o, ct * P, (1, P)), tile(ct), const("ident"))
                    for ct in range(CT):
                        last = nc.tensor.matmul(v(o, 2 * P, (1, H * K1)), tile(ct), v(dbcw, ct * H * K1, (1, H * K1)),
                                                start=(ct == 0), stop=(ct == CT - 1))
                    last.then_inc(x_full, 1)

            def segments(i, h):
                wait(pe, ee_ready, i * H + h)
                nc.tensor.matmul(v(sg, SEG, (1, Q * L)), const("after"), v(rseg, h * Q * L, (1, Q * L)), start=True, stop=True)
                nc.tensor.matmul(v(sg, CUM, (1, Q)), const("upto"), v(dts, 192 + h * Q, (1, Q)), start=True, stop=True)
                nc.tensor.matmul(v(sg, TOT, (1, Q * CPT)), const("ones"), v(rtot, h * Q * CPT, (1, Q * CPT)),
                                 start=True, stop=True).then_inc(sg_full, 1)

            def x_rows(h, b, g):
                return v(xp, (h * NT + g) * ROW + b * P, (1, P))

            def chunk_sums(i, h, b):
                wait(pe, hs_ready, ((i * H + h) * NB + b) * S)
                if h == 0 and b == 0:
                    pe.wait_ge(x_rows_in, 16 * (i + 1))
                pe.wait_ge(bblk_ready, i * H + h + 1)
                for g in range(NT):
                    last = nc.tensor.matmul(v(st, g * CPT * S, (1, CPT * S)), x_rows(h, b, g),
                                            v(bblk, (b * NT + g) * CPT * S, (1, CPT * S)), start=True, stop=True)
                last.then_inc(st_full, 1)

            def turn(i, h, k, before):
                b, gp = divmod(k, 4)
                o = tp_slot(k, t_drained, i * T_U + h * 8, before)
                if gp == 0:
                    pe.wait_ge(cblk_ready, i * H + h + 1)
                    pe.wait_ge(hs_ready, ((i * H + h) * NB + b + 1) * S)
                nc.tensor.transpose(v(o, 0, (1, P)), v(cblk, (b * NT + 2 * gp) * CPT * S, (1, P)), const("ident"))
                nc.tensor.transpose(v(o, P, (1, P)), v(hs, (b * (NC + 1) + 2 * gp * CPT) * S, (1, P)), const("ident")).then_inc(t_full, 1)

            def result(i, h, k, before):
                b, gp = divmod(k, 4)
                u = h * 8 + k
                if gp == 0:
                    pj_slot(2 * b + 1, None, None, before)
                    pe.wait_ge(mblk_ready, i * H + h + 1)
                pe.wait_ge(t_drained, i * T_U + u + 1)
                for e in range(2):
                    g = 2 * gp + e
                    d = v(pj[2 * b + e], gp * P, (1, P))
                    nc.tensor.matmul(d, v(mblk, (b * NT + g) * P, (1, P)), x_rows(h, b, g), start=True, stop=False)
                    half_rows = dict(parts=64, p0=64 * e)
                    last = nc.tensor.matmul(d, v(ch, (u % CH) * 2 * P, (1, P), **half_rows),
                                            v(ch, (u % CH) * 2 * P + P, (1, P), **half_rows), start=False, stop=True)
                last.then_inc(ch_used, 1)

            def results(i, h, before_t, before_r, turned_before=0, between=None):
                for k in range(turned_before, AHEAD):
                    turn(i, h, k, before_t)
                for k in range(8):
                    if k + AHEAD < 8:
                        turn(i, h, k + AHEAD, before_t)
                    result(i, h, k, before_r)
                    if k == 3 and between:
                        between()

            def gate(i, par, units, before):
                for k in units:
                    b = k // 4
                    if k % 4 == 0:
                        pe.wait_ge(wg_ready, i * NB + b + 1)
                    o = pj_slot(k, g_drained, i * G_U, before)
                    part(o, par, b, 0, k // 2 % 2, k % 2).then_inc(g_full, 1)

            def residual(i, par, units, before, restart=0):
                pe.wait_ge(wr_ready, (i + 1) * NB)
                for k in units:
                    o = pj_slot(k - restart, e_drained, i * E_U + restart, before)
                    part(o, par, k // 2 % 2, 1, k // 4, k % 2).then_inc(e_full, 1)

            def turn_back(i, h, before, images=range(NB)):
                pe.wait_ge(y_gathered[h], 128 * (i + 1))
                for k in (h * 4 + b * 2 + half for b in images for half in range(2)):
                    b, nq = k // 2 % 2, k % 2
                    o = tp_slot(k, y_drained, i * Y_U, before)
                    for e in range(4):
                        last = nc.tensor.transpose(v(o, e * P, (1, P)), v(big, (h * NT + nq * 4 + e) * NB * P + b * P, (1, P)), const("ident"))
                    last.then_inc(y_full, 1)

            def output(i, before):
                for k in range(O_U):
                    b, ot, nt = k // 4, k // 2 % 2, k % 2
                    if k % 4 == 0:
                        pe.wait_ge(z_ready, i * 4 + 3 + b)
                    o = pj_slot(k, o_drained, i * O_U, before)
                    for h in range(CT):
                        last = nc.tensor.matmul(o[:, :], v(outw, h * C + ot * P, (1, P)),
                                                v(gt, (b * CT + h) * N + nt * HALF, (1, HALF)), start=(h == 0), stop=(h == CT - 1))
                    last.then_inc(o_full, 1)

            def cycle(i, par, half):
                more = not last_phase(i)
                nxt = (i + 1, 1 - par, half + par)
                before_g = (o_drained, i * O_U)
                before_t = (x_drained, X_U) if first(i) else (y_drained, i * Y_U)
                g_all = (g_drained, (i + 1) * G_U)
                pe.wait_ge(r_ready, i * 2 + 2)
                segments(i, 0)
                if first(i):
                    chunk_sums(i, 0, 0)
                    segments(i, 1)
                    chunk_sums(i, 0, 1)
                else:
                    gate(i, par, range(0, 4), before_g)
                    chunk_sums(i, 0, 0)
                    segments(i, 1)
                    gate(i, par, range(4, 5), before_g)
                    chunk_sums(i, 0, 1)
                    gate(i, par, range(5, 8), before_g)
                for k in range(AHEAD):
                    turn(i, 0, k, before_t)
                if not more:
                    residual(i, par, range(0, 4), g_all)
                elif not first(i):
                    project(*nxt, 0, g_all)
                results(i, 0, before_t, (a_drained, (i + 1) * A_U + 4) if more else (e_drained, i * E_U + 4), AHEAD,
                        between=lambda: chunk_sums(i, 1, 0))
                r_half = (r_drained, i * R_U + 4)
                t_half = (t_drained, i * T_U + 8)
                r_all = (r_drained, (i + 1) * R_U)
                t_all = (t_drained, (i + 1) * T_U)
                if more:
                    project(*nxt, 1, r_half, range(0, 2))
                if more:
                    for k in range(2):
                        rows(i + 1, 0, t_half, range(4 * k, 4 * k + 4))
                        project(*nxt, 1, r_half, range(2 + k, 3 + k))
                    chunk_sums(i, 1, 1)
                else:
                    chunk_sums(i, 1, 1)
                    residual(i, par, range(4, 8), r_half, restart=4)
                results(i, 1, (x_drained, (i + 1) * X_U + NT) if more else t_half,
                        (a_drained, (i + 2) * A_U) if more else (e_drained, (i + 1) * E_U))
                if more:
                    for k in range(4):
                        rows(i + 1, 1, t_all, range(2 * k, 2 * k + 2))
                        residual(i, par, range(k, k + 1), r_all)
                    turn_back(i, 0, (x_drained, (i + 2) * X_U))
                    residual(i, par, range(4, 6), None)
                    turn_back(i, 1, None, (0,))
                    residual(i, par, range(6, 8), None)
                    turn_back(i, 1, None, (1,))
                    output(i, (e_drained, (i + 1) * E_U))
                else:
                    turn_back(i, 0, t_all)
                    turn_back(i, 1, None)
                    output(i, r_all)

            project(0, 0, 0, 0, None)
            project(0, 0, 0, 1, (a_drained, 4))
            rows(0, 0, None)
            gate(0, 0, range(0, 4), (a_drained, A_U))
            rows(0, 1, (x_drained, NT))
            gate(0, 0, range(4, 8), None)
            project(1, 1, 0, 0, (g_drained, G_U))
            phases(pe, cycle)


V_MOB = 6
V_STATS = 54
V_VAR1 = 58
V_Y = 62
V_MAX = 65
V_HID = 69
V_HIDT = 70
V_STATS2 = 85
V_VAR2 = 89
V_DIAG = 35
V_Q = 92
P_EXPERT = 4


def kernel(**inputs):
    import concourse.bacc as _bacc
    from concourse.bass_utils import run_bass_kernel_spmd as _run

    w = {k: np.ascontiguousarray(np.asarray(a)) for k, a in inputs.items()}
    L1, L0 = "L1_conv_", "L0_conv_"

    def by_tile(a):
        return np.ascontiguousarray(a.reshape(-1, P, a.shape[-1]).transpose(1, 0, 2))

    def column(a):
        return np.ascontiguousarray(a.reshape(-1, P).T)

    table = constants()
    w1 = w[L0 + "W1"].reshape(E * R, C).T
    arrays = dict(
        x=w["x"].reshape(B, C, N),
        w1g=by_tile(np.concatenate([w[L0 + "Wg"].T, w1], 1)),
        b1g=np.concatenate([w[L0 + "bg"], w[L0 + "b1"].reshape(-1)])[None],
        w2=np.ascontiguousarray(w[L0 + "W2"].transpose(0, 2, 1).reshape(E * R, C)),
        b2=w[L0 + "b2"],
        inw=by_tile(w[L1 + "in_proj_w"].T),
        inb=column(w[L1 + "in_proj_b"]),
        dww=np.ascontiguousarray(w[L1 + "dw_w"].reshape(CT, P, 3).transpose(1, 0, 2).reshape(P, 6)),
        dwb=column(w[L1 + "dw_b"]),
        dbcw=by_tile(w[L1 + "dbc_w"].T),
        dbcb=w[L1 + "dbc_b"][None],
        alog=w[L1 + "A_log"].reshape(1, H * S),
        dpar=w[L1 + "Dparam"][None],
        mob=w[L1 + "mobius"].reshape(1, 4 * H),
        outw=by_tile(w[L1 + "out_proj_w"].T),
        outb=column(w[L1 + "out_proj_b"]),
        const=table)
    nc = _bacc.Bacc("TRN2", target_bir_lowering=False, num_devices=1)
    feeds, args = {}, []
    for name, a in arrays.items():
        a = np.ascontiguousarray(a)
        feeds[f"in_{name}"] = a
        args.append(nc.dram_tensor(f"in_{name}", a.shape, mybir.dt.from_np(a.dtype), kind="ExternalInput").ap())
    out = nc.dram_tensor("out_0", (B, C, N), F32, kind="ExternalOutput").ap()
    build(nc, *args, out)
    r = _run(nc, [feeds], core_ids=[0])
    return r.results[0]["out_0"].reshape(B, C, IMG, IMG)
```
